# Optimizing a Trainium2 kernel written in Bass

```python
import numpy as np
import jax
import jax.numpy as jnp

def _softmax(x, axis=-1):
    return jax.nn.softmax(x, axis=axis)

def _gelu(x):
    return jax.nn.gelu(x, approximate=True)

def _silu(x):
    return jax.nn.silu(x)

def _sigmoid(x):
    return jax.nn.sigmoid(x)

def _layernorm(x, axis=-1, eps=1e-05):
    m = jnp.mean(x, axis=axis, keepdims=True)
    v = jnp.var(x, axis=axis, keepdims=True)
    return (x - m) / jnp.sqrt(v + eps)

def _scatter_add(tgt, idx, src, axis=0):
    return tgt.at[idx].add(src)

def _segment_sum(src, seg, n):
    return jax.ops.segment_sum(src, seg, n)
kernel_name = 'mk_xattn_ffn_d2_seqx_r4_fcfcc0'

def setup_inputs(seed: int=0):
    np.random.seed(seed)
    _w = jnp.asarray

    def _rec_inputs():
        import jax
        import jax.numpy as jnp
        _rk = jax.random.key(seed)
        x = 4.136e-05 + 0.9999 * jax.random.normal(jax.random.fold_in(_rk, 1), (16, 128, 256), jnp.float32)
        _lenS = 128 - jax.random.randint(jax.random.fold_in(_rk, 7), (16,), 0, max(1, 128 // 4) + 1, jnp.int32)
        _lenS2 = 128 - jax.random.randint(jax.random.fold_in(_rk, 8), (16,), 0, max(1, 128 // 4) + 1, jnp.int32)
        _ctx_1024P = jax.random.normal(jax.random.fold_in(_rk, 11), (16, 16, 256), jnp.float32)
        _ctx_1024c = jax.random.dirichlet(jax.random.fold_in(_rk, 511), 0.3 * jnp.ones((16,), jnp.float32), (16, 128))
        _ctx_1024t = jnp.einsum('bsk,bkd->bsd', _ctx_1024c, _ctx_1024P)
        _ctx_1024t = _ctx_1024t * jax.lax.rsqrt(jnp.mean(jnp.square(_ctx_1024t)) + 1e-12) * 0.953939
        ctx_1024 = 7.22013e-05 + 1.00017 * (_ctx_1024t + 0.3 * jax.random.normal(jax.random.fold_in(_rk, 611), (16, 128, 256), jnp.float32))
        return (x, ctx_1024)
    x, ctx_1024 = _rec_inputs()

    def _L0_xattn_setup():
        import jax, jax.numpy as jnp
        import numpy as np
        B, L_Q, L_KV, D, H = (4, 512, 512, 256, 16)
        key = jax.random.key(seed)
        ks = jax.random.split(key, 11)
        s = 0.02
        return {'kv': jax.random.normal(ks[0], (B, L_KV, D), dtype=jnp.float32), 'q': jax.random.normal(ks[1], (B, L_Q, D), dtype=jnp.float32), 'Wq': jax.random.normal(ks[2], (D, D), dtype=jnp.float32) * s, 'bq': jnp.zeros((D,), dtype=jnp.float32), 'Wk': jax.random.normal(ks[3], (D, D), dtype=jnp.float32) * s, 'bk': jnp.zeros((D,), dtype=jnp.float32), 'Wv': jax.random.normal(ks[4], (D, D), dtype=jnp.float32) * s, 'bv': jnp.zeros((D,), dtype=jnp.float32), 'Wo': jax.random.normal(ks[5], (D, D), dtype=jnp.float32) * s, 'bo': jnp.zeros((D,), dtype=jnp.float32)}
    _L0_xattn_all = _L0_xattn_setup()
    _L0_xattn_in = {k: v for k, v in _L0_xattn_all.items() if k in ('Wq', 'bq', 'Wk', 'bk', 'Wv', 'bv', 'Wo', 'bo')}
    del _L0_xattn_all

    def _L0_ffn_setup():
        import jax, jax.numpy as jnp
        import numpy as np
        B, S, D, H, F, E = (2, 256, 256, 16, 512, 8)
        HD = D // H

        def _ln(x, g, b, eps=1e-05):
            m = x.mean(-1, keepdims=True)
            v = ((x - m) ** 2).mean(-1, keepdims=True)
            return (x - m) / jnp.sqrt(v + eps) * g + b
        key = jax.random.key(seed)
        ks = jax.random.split(key, 12)
        rn = lambda k, shp, s=0.02: jax.random.normal(k, shp, jnp.float32) * s
        return {'src': jax.random.normal(ks[0], (B, S, D), jnp.float32), 'q_w': rn(ks[1], (D, D)), 'k_w': rn(ks[2], (D, D)), 'v_w': rn(ks[3], (D, D)), 'out_w': rn(ks[4], (D, D)), 'gate_w': rn(ks[5], (D, D)), 'gate_b': rn(ks[6], (D,)), 'scale_w': rn(ks[7], (H, HD)), 'n1_g': jnp.ones((D,), jnp.float32), 'n1_b': jnp.zeros((D,), jnp.float32), 'n2_g': jnp.ones((D,), jnp.float32), 'n2_b': jnp.zeros((D,), jnp.float32), 'moe_gate_w': rn(ks[8], (D, E)), 'moe_gate_b': jnp.zeros((E,), jnp.float32), 'w1': rn(ks[9], (E, D, F)), 'b1': jnp.zeros((E, F), jnp.float32), 'ln_g': jnp.ones((E, F), jnp.float32), 'ln_b': jnp.zeros((E, F), jnp.float32), 'w2': rn(ks[10], (E, F, D)), 'b2': jnp.zeros((E, D), jnp.float32), 'res_scale': jnp.ones((E,), jnp.float32)}
    _L0_ffn_all = _L0_ffn_setup()
    _L0_ffn_in = {k: v for k, v in _L0_ffn_all.items() if k in ('q_w', 'k_w', 'v_w', 'out_w', 'gate_w', 'gate_b', 'scale_w', 'n1_g', 'n1_b', 'n2_g', 'n2_b', 'moe_gate_w', 'moe_gate_b', 'w1', 'b1', 'ln_g', 'ln_b', 'w2', 'b2', 'res_scale')}
    del _L0_ffn_all

    def _L1_xattn_setup():
        import jax, jax.numpy as jnp
        import numpy as np
        EMBED_DIM = 256
        NUM_HEADS = 16
        HEAD_DIM = EMBED_DIM // NUM_HEADS
        WINDOW = 128
        B, S_Q, S_K = (2, 512, 512)

        def apply_rope(x):
            Dh = x.shape[-1]
            half = Dh // 2
            pos = jnp.arange(x.shape[2], dtype=jnp.float32)
            inv_freq = 1.0 / 10000.0 ** (jnp.arange(0, half, dtype=jnp.float32) / half)
            ang = pos[:, None] * inv_freq[None, :]
            cos = jnp.cos(ang)[None, None, :, :].astype(x.dtype)
            sin = jnp.sin(ang)[None, None, :, :].astype(x.dtype)
            x1, x2 = (x[..., :half], x[..., half:])
            return jnp.concatenate([x1 * cos - x2 * sin, x1 * sin + x2 * cos], axis=-1)
        key = jax.random.key(seed)
        ks = jax.random.split(key, 11)
        scale = 1.0 / np.sqrt(EMBED_DIM)
        inp = {'query': jax.random.normal(ks[0], (B, S_Q, EMBED_DIM), jnp.float32), 'key': jax.random.normal(ks[1], (B, S_K, EMBED_DIM), jnp.float32), 'value': jax.random.normal(ks[2], (B, S_K, EMBED_DIM), jnp.float32), 'Wq': jax.random.normal(ks[3], (EMBED_DIM, EMBED_DIM), jnp.float32) * scale, 'bq': jnp.zeros((EMBED_DIM,), jnp.float32), 'Wk': jax.random.normal(ks[4], (EMBED_DIM, EMBED_DIM), jnp.float32) * scale, 'bk': jnp.zeros((EMBED_DIM,), jnp.float32), 'Wv': jax.random.normal(ks[5], (EMBED_DIM, EMBED_DIM), jnp.float32) * scale, 'bv': jnp.zeros((EMBED_DIM,), jnp.float32), 'Wo': jax.random.normal(ks[6], (EMBED_DIM, EMBED_DIM), jnp.float32) * scale, 'bo': jnp.zeros((EMBED_DIM,), jnp.float32)}
        return inp
    _L1_xattn_all = _L1_xattn_setup()
    _L1_xattn_in = {k: v for k, v in _L1_xattn_all.items() if k in ('Wq', 'bq', 'Wk', 'bk', 'Wv', 'bv', 'Wo', 'bo')}
    del _L1_xattn_all

    def _L1_ffn_setup():
        import jax, jax.numpy as jnp
        import numpy as np
        key = jax.random.key(seed)
        k_x, k_W, k_b, k_ids, k_w = jax.random.split(key, 5)
        N_ADAPTERS, D_OUT, D_IN = (32, 256, 256)
        B, S = (2, 512)
        K = 8
        x = jax.random.normal(k_x, (B, S, D_IN), dtype=jnp.float32)
        W = jax.random.normal(k_W, (N_ADAPTERS, D_OUT, D_IN), dtype=jnp.float32)
        b = jax.random.normal(k_b, (N_ADAPTERS, D_OUT), dtype=jnp.float32)
        ids = jax.random.randint(k_ids, (K,), 0, N_ADAPTERS, dtype=jnp.int64)
        weights = jax.random.uniform(k_w, (K,), dtype=jnp.float32)
        return {'x': x, 'W': W, 'b': b, 'ids': ids, 'weights': weights}
    _L1_ffn_all = _L1_ffn_setup()
    _L1_ffn_in = {k: v for k, v in _L1_ffn_all.items() if k in ('W', 'b', 'ids', 'weights')}
    del _L1_ffn_all
    return {'x': x, 'ctx_1024': ctx_1024, 'L0_xattn_Wq': _L0_xattn_in['Wq'], 'L0_xattn_bq': _L0_xattn_in['bq'], 'L0_xattn_Wk': _L0_xattn_in['Wk'], 'L0_xattn_bk': _L0_xattn_in['bk'], 'L0_xattn_Wv': _L0_xattn_in['Wv'], 'L0_xattn_bv': _L0_xattn_in['bv'], 'L0_xattn_Wo': _L0_xattn_in['Wo'], 'L0_xattn_bo': _L0_xattn_in['bo'], 'L0_ffn_q_w': _L0_ffn_in['q_w'], 'L0_ffn_k_w': _L0_ffn_in['k_w'], 'L0_ffn_v_w': _L0_ffn_in['v_w'], 'L0_ffn_out_w': _L0_ffn_in['out_w'], 'L0_ffn_gate_w': _L0_ffn_in['gate_w'], 'L0_ffn_gate_b': _L0_ffn_in['gate_b'], 'L0_ffn_scale_w': _L0_ffn_in['scale_w'], 'L0_ffn_n1_g': _L0_ffn_in['n1_g'], 'L0_ffn_n1_b': _L0_ffn_in['n1_b'], 'L0_ffn_n2_g': _L0_ffn_in['n2_g'], 'L0_ffn_n2_b': _L0_ffn_in['n2_b'], 'L0_ffn_moe_gate_w': _L0_ffn_in['moe_gate_w'], 'L0_ffn_moe_gate_b': _L0_ffn_in['moe_gate_b'], 'L0_ffn_w1': _L0_ffn_in['w1'], 'L0_ffn_b1': _L0_ffn_in['b1'], 'L0_ffn_ln_g': _L0_ffn_in['ln_g'], 'L0_ffn_ln_b': _L0_ffn_in['ln_b'], 'L0_ffn_w2': _L0_ffn_in['w2'], 'L0_ffn_b2': _L0_ffn_in['b2'], 'L0_ffn_res_scale': _L0_ffn_in['res_scale'], 'L1_xattn_Wq': _L1_xattn_in['Wq'], 'L1_xattn_bq': _L1_xattn_in['bq'], 'L1_xattn_Wk': _L1_xattn_in['Wk'], 'L1_xattn_bk': _L1_xattn_in['bk'], 'L1_xattn_Wv': _L1_xattn_in['Wv'], 'L1_xattn_bv': _L1_xattn_in['bv'], 'L1_xattn_Wo': _L1_xattn_in['Wo'], 'L1_xattn_bo': _L1_xattn_in['bo'], 'L1_ffn_W': _L1_ffn_in['W'], 'L1_ffn_b': _L1_ffn_in['b'], 'L1_ffn_ids': _L1_ffn_in['ids'], 'L1_ffn_weights': _L1_ffn_in['weights']}

def reference(x, ctx_1024, L0_xattn_Wq, L0_xattn_bq, L0_xattn_Wk, L0_xattn_bk, L0_xattn_Wv, L0_xattn_bv, L0_xattn_Wo, L0_xattn_bo, L0_ffn_q_w, L0_ffn_k_w, L0_ffn_v_w, L0_ffn_out_w, L0_ffn_gate_w, L0_ffn_gate_b, L0_ffn_scale_w, L0_ffn_n1_g, L0_ffn_n1_b, L0_ffn_n2_g, L0_ffn_n2_b, L0_ffn_moe_gate_w, L0_ffn_moe_gate_b, L0_ffn_w1, L0_ffn_b1, L0_ffn_ln_g, L0_ffn_ln_b, L0_ffn_w2, L0_ffn_b2, L0_ffn_res_scale, L1_xattn_Wq, L1_xattn_bq, L1_xattn_Wk, L1_xattn_bk, L1_xattn_Wv, L1_xattn_bv, L1_xattn_Wo, L1_xattn_bo, L1_ffn_W, L1_ffn_b, L1_ffn_ids, L1_ffn_weights):
    import jax
    import jax.numpy as jnp

    def _L0_xattn_ref(kv, q, Wq, bq, Wk, bk, Wv, bv, Wo, bo):
        import jax, jax.numpy as jnp
        import numpy as np
        B, L_Q, L_KV, D, H = (4, 512, 512, 256, 16)
        Bb, Lkv, Dm = kv.shape
        Lq = q.shape[1]
        hd = Dm // H
        scale = hd ** (-0.5)
        qh = (q @ Wq.T + bq).reshape(Bb, Lq, H, hd).transpose(0, 2, 1, 3)
        kh = (kv @ Wk.T + bk).reshape(Bb, Lkv, H, hd).transpose(0, 2, 1, 3)
        vh = (kv @ Wv.T + bv).reshape(Bb, Lkv, H, hd).transpose(0, 2, 1, 3)
        scores = jnp.einsum('bhqd,bhkd->bhqk', qh, kh) * scale
        mask = jnp.arange(Lkv)[None, :] <= jnp.arange(Lq)[:, None]
        scores = jnp.where(mask[None, None], scores, -jnp.inf)
        attn = jax.nn.softmax(scores, axis=-1)
        out = jnp.einsum('bhqk,bhkd->bhqd', attn, vh)
        out = out.transpose(0, 2, 1, 3).reshape(Bb, Lq, Dm)
        return out @ Wo.T + bo

    def _L0_ffn_ref(src, q_w, k_w, v_w, out_w, gate_w, gate_b, scale_w, n1_g, n1_b, n2_g, n2_b, moe_gate_w, moe_gate_b, w1, b1, ln_g, ln_b, w2, b2, res_scale):
        import jax, jax.numpy as jnp
        import numpy as np
        B, S, D, H, F, E = (2, 256, 256, 16, 512, 8)
        HD = D // H

        def _ln(x, g, b, eps=1e-05):
            m = x.mean(-1, keepdims=True)
            v = ((x - m) ** 2).mean(-1, keepdims=True)
            return (x - m) / jnp.sqrt(v + eps) * g + b
        b, s, d = src.shape
        h = scale_w.shape[0]
        hd = d // h
        q = (src @ q_w).reshape(b, s, h, hd).transpose(0, 2, 1, 3)
        k = (src @ k_w).reshape(b, s, h, hd).transpose(0, 2, 1, 3)
        v = (src @ v_w).reshape(b, s, h, hd).transpose(0, 2, 1, 3)
        scores = jnp.einsum('bhqd,bhkd->bhqk', q, k) / np.float32(np.sqrt(hd))
        scale = jax.nn.sigmoid(jnp.einsum('bhsd,hd->bhs', q, scale_w)) * 2.0
        scores = scores * scale[..., None]
        aw = jax.nn.softmax(scores, axis=-1)
        out = jnp.einsum('bhqk,bhkd->bhqd', aw, v).transpose(0, 2, 1, 3).reshape(b, s, d)
        gate = jax.nn.sigmoid(out @ gate_w + gate_b)
        attn = out * gate @ out_w
        x = _ln(src + attn, n1_g, n1_b)
        xr = x.reshape(-1, d)
        n = xr.shape[0]
        logits = xr @ moe_gate_w + moe_gate_b
        top_v, top_i = jax.lax.top_k(logits, 2)
        wts = jax.nn.softmax(top_v, axis=-1)
        chosen = jnp.max(top_i, axis=-1)

        def expert(W1, B1, G, Bt, W2, B2, rsc):
            hh = xr @ W1 + B1
            hh = jax.nn.gelu(_ln(hh, G, Bt), approximate=False)
            return (hh @ W2 + B2) * rsc + xr
        outs = jax.vmap(expert)(w1, b1, ln_g, ln_b, w2, b2, res_scale)
        sel = jnp.take_along_axis(outs.transpose(1, 0, 2), chosen[:, None, None], axis=1)[:, 0]
        moe = sel * jnp.sum(wts, axis=-1, keepdims=True)
        return _ln(x + moe.reshape(b, s, d), n2_g, n2_b)

    def _L1_xattn_ref(query, key, value, Wq, bq, Wk, bk, Wv, bv, Wo, bo):
        import jax, jax.numpy as jnp
        import numpy as np
        EMBED_DIM = 256
        NUM_HEADS = 16
        HEAD_DIM = EMBED_DIM // NUM_HEADS
        WINDOW = 128
        B, S_Q, S_K = (2, 512, 512)

        def apply_rope(x):
            Dh = x.shape[-1]
            half = Dh // 2
            pos = jnp.arange(x.shape[2], dtype=jnp.float32)
            inv_freq = 1.0 / 10000.0 ** (jnp.arange(0, half, dtype=jnp.float32) / half)
            ang = pos[:, None] * inv_freq[None, :]
            cos = jnp.cos(ang)[None, None, :, :].astype(x.dtype)
            sin = jnp.sin(ang)[None, None, :, :].astype(x.dtype)
            x1, x2 = (x[..., :half], x[..., half:])
            return jnp.concatenate([x1 * cos - x2 * sin, x1 * sin + x2 * cos], axis=-1)
        Bq, Sq, D = query.shape
        Sk = key.shape[1]
        H, Dh = (NUM_HEADS, HEAD_DIM)

        def proj(x, W, b):
            return (x @ W.T + b).reshape(x.shape[0], x.shape[1], H, Dh).transpose(0, 2, 1, 3)
        q = apply_rope(proj(query, Wq, bq))
        k = apply_rope(proj(key, Wk, bk))
        v = proj(value, Wv, bv)
        q = q * Dh ** (-0.5)
        scores = jnp.einsum('bhqd,bhkd->bhqk', q, k)
        q_idx = jnp.arange(Sq)[:, None]
        kv_idx = jnp.arange(Sk)[None, :]
        rel = kv_idx - q_idx
        mask = (rel > 0) | (rel < -WINDOW)
        mask4 = mask[None, None, :, :]
        neg = jnp.finfo(scores.dtype).min
        scores = jnp.where(mask4, neg, scores)
        probs = jax.nn.softmax(scores, axis=-1)
        all_masked = jnp.all(mask4, axis=-1, keepdims=True)
        probs = jnp.where(all_masked, jnp.zeros((), probs.dtype), probs)
        out = jnp.einsum('bhqk,bhkd->bhqd', probs, v)
        out = out.transpose(0, 2, 1, 3).reshape(Bq, Sq, D)
        return out @ Wo.T + bo

    def _L1_ffn_ref(x, W, b, ids, weights):
        import jax, jax.numpy as jnp
        import numpy as np
        Wsel = W[ids]
        bsel = b[ids]
        out = jnp.einsum('k,kod,bsd->bso', weights, Wsel, x)
        out = out + jnp.einsum('k,ko->o', weights, bsel)
        return out
    x = x + _L0_xattn_ref(ctx_1024, _layernorm(x, axis=-1), L0_xattn_Wq, L0_xattn_bq, L0_xattn_Wk, L0_xattn_bk, L0_xattn_Wv, L0_xattn_bv, L0_xattn_Wo, L0_xattn_bo)
    x = x + _L0_ffn_ref(_layernorm(x, axis=-1), L0_ffn_q_w, L0_ffn_k_w, L0_ffn_v_w, L0_ffn_out_w, L0_ffn_gate_w, L0_ffn_gate_b, L0_ffn_scale_w, L0_ffn_n1_g, L0_ffn_n1_b, L0_ffn_n2_g, L0_ffn_n2_b, L0_ffn_moe_gate_w, L0_ffn_moe_gate_b, L0_ffn_w1, L0_ffn_b1, L0_ffn_ln_g, L0_ffn_ln_b, L0_ffn_w2, L0_ffn_b2, L0_ffn_res_scale)
    x = x + _L1_xattn_ref(_layernorm(x, axis=-1), ctx_1024, ctx_1024, L1_xattn_Wq, L1_xattn_bq, L1_xattn_Wk, L1_xattn_bk, L1_xattn_Wv, L1_xattn_bv, L1_xattn_Wo, L1_xattn_bo)
    x = x + _L1_ffn_ref(_layernorm(x, axis=-1), L1_ffn_W, L1_ffn_b, L1_ffn_ids, L1_ffn_weights)
    return x

_drawn_inputs = setup_inputs


def setup_inputs(seed=0):
    import zlib

    import numpy as np

    out = dict(_drawn_inputs(seed))
    spreads = {'L0_xattn_bq': (0.0, 0.8),
     'L0_xattn_bk': (0.0, 0.8),
     'L0_xattn_bv': (0.0, 0.1),
     'L0_xattn_bo': (0.0, 0.1),
     'L0_ffn_n1_g': (1.0, 0.2),
     'L0_ffn_n1_b': (0.0, 0.1),
     'L0_ffn_n2_g': (1.0, 0.2),
     'L0_ffn_n2_b': (0.0, 0.1),
     'L0_ffn_moe_gate_b': (0.0, 0.1),
     'L0_ffn_b1': (0.0, 0.334),
     'L0_ffn_ln_g': (1.0, 0.6),
     'L0_ffn_ln_b': (0.0, 0.8),
     'L0_ffn_b2': (0.0, 0.305),
     'L0_ffn_res_scale': (1.0, 0.6),
     'L1_xattn_bq': (0.0, 0.72),
     'L1_xattn_bk': (0.0, 0.8),
     'L1_xattn_bv': (0.0, 0.1),
     'L1_xattn_bo': (0.0, 0.1)}
    factors = {'L0_xattn_Wq': 8.0,
     'L0_xattn_Wk': 8.0,
     'L0_ffn_q_w': 8.0,
     'L0_ffn_k_w': 8.0,
     'L0_ffn_v_w': 7.423,
     'L0_ffn_out_w': 5.897,
     'L0_ffn_gate_w': 8.0,
     'L0_ffn_gate_b': 8.0,
     'L0_ffn_scale_w': 8.0}
    for name, (base, spread) in spreads.items():
        noise = np.random.default_rng([zlib.crc32(name.encode()), seed]).standard_normal(out[name].shape)
        drawn = base * np.exp(spread * noise) if base else spread * noise
        out[name] = jnp.asarray(drawn.astype(out[name].dtype))
    for name, factor in factors.items():
        out[name] = (out[name] * factor).astype(out[name].dtype)
    return out
```

```python
from contextlib import ExitStack

import numpy as np

import concourse.bass as bass
from concourse import mybir

F32 = mybir.dt.float32
BF16 = mybir.dt.bfloat16
I32 = mybir.dt.int32
U32 = mybir.dt.uint32
ALU = mybir.AluOpType
ACT = mybir.ActivationFunctionType
AX = mybir.AxisListType

P = 128
B, D, H, HD = 16, 256, 16, 16
C = D // P
SLOTS = 2
NI = B // SLOTS
G, HG = 4, 4
E, F = 8, 512
FC = F // P
TILES = B * P // P + E - 1
XSLOTS = 4
ADAPTERS, K_ADAPT = 32, 8
VW = 32
EPS = 1e-5
MASKED = -1e30
STEP1, STEP3 = 20, 10
PER_TURN1, PER_TURN3 = 62, 58
LN1, LN3 = 3, 3


def at(i, per, k, base=0):
    return i * per + (base + k + 1)


def wait(eng, sem, value):
    if isinstance(value, int) and value <= 0:
        return
    eng.wait_ge(sem, value)


class Chain:

    def __init__(self, eng, sem):
        self.eng, self.sem, self.base, self.k, self.turn, self.per = eng, sem, 0, 0, 0, 0

    def start(self, turn, per):
        self.base, self.k, self.turn, self.per = self.base + self.k, 0, turn, per

    def end(self, turns):
        assert self.k == self.per, (self.k, self.per)
        self.base, self.k, self.turn, self.per = self.base + turns * self.per, 0, 0, 0

    def mark(self, ins):
        ins.then_inc(self.sem, 1)
        self.k += 1

    def join_by(self, spare):
        self.join()
        self.mark(self.eng.memset(spare, 0.0))

    def join(self):
        self.eng.wait_ge(self.sem, self.turn * self.per + (self.base + self.k))


def schedule(core, side):
    steps = [("scores", 0), ("scores", 1), ("turn", 0), ("scores", 2), ("mix", 0), ("turn", 1),
             ("scores", 3), ("mix", 1), ("turn", 2), ("mix", 2), ("turn", 3), ("mix", 3)]
    out, given = [], 0
    for n, (name, g) in enumerate(steps):
        out.append((name, core, g))
        upto = (n + 1) * len(side) // len(steps)
        out += [(s, None, slot_turn) for s, slot_turn in side[given:upto]]
        given = upto
    return out


SIDE_A = ["a_norm", "a_norm2", "a_kv", "a_q", "a_qkT"]
SIDE_B = ["b_o", "b_oT", "b_res", "b_norm", "b_qk", "b_v", "b_scale", "b_qkT"]
SIDE_C = ["c_o", "c_oT", "c_gate", "c_gate2", "c_gT", "c_out", "c_norm", "c_x1T", "c_logits"]
SIDE_D = ["d_moe", "d_norm", "d_norm2", "d_kv", "d_q", "d_rope", "d_qkT"]
SIDE_E = ["e_o", "e_oT", "e_res", "e_norm", "e_ffn"]


def turn1(i, first, last):
    def s(names, slot, t):
        return [(n, (slot, t)) for n in names]
    out = []
    if first:
        out += [(n, None, st) for n, st in s(SIDE_A, 0, i)]
    out += schedule((0, 0, i), ([] if first else s(SIDE_C, 1, i - 1)) + s(SIDE_A, 1, i))
    out += schedule((1, 0, i), s(SIDE_B, 0, i))
    out += schedule((0, 1, i), s(SIDE_B, 1, i))
    out += schedule((1, 1, i), s(SIDE_C, 0, i) + ([] if last else s(SIDE_A, 0, i + 1)))
    if last:
        out += [(n, None, st) for n, st in s(SIDE_C, 1, i)]
    return out


def turn3(i, first, last):
    def s(names, slot, t):
        return [(n, (slot, t)) for n in names]
    out = []
    if first:
        out += [(n, None, st) for n, st in s(SIDE_D, 0, i)]
    out += schedule((0, 2, i), ([] if first else s(SIDE_E, 1, i - 1)) + s(SIDE_D, 1, i))
    out += schedule((1, 2, i), s(SIDE_E, 0, i) + ([] if last else s(SIDE_D, 0, i + 1)))
    if last:
        out += [(n, None, st) for n, st in s(SIDE_E, 1, i)]
    return out


def run_turns(eng, order, step, chain=None, per=0):
    for body, turns in ((0, 1), (1, NI - 2), (2, 1)):
        if body == 1:
            with eng.Fori(1, NI - 1) as i:
                if chain:
                    chain.start(i - 1, per)
                for s in order(i, False, False):
                    step(*s)
                if chain:
                    chain.end(turns)
        else:
            i = 0 if body == 0 else NI - 1
            for s in order(i, body == 0, body == 2):
                step(*s)


def build(nc, t):
    ctx = ExitStack()
    with ctx:
        def sb(name, shape, dt=F32):
            return ctx.enter_context(nc.sbuf_tensor(name, shape, dt))

        def sem(name):
            return ctx.enter_context(nc.semaphore(name))

        ps = ctx.enter_context(nc.psum_tensor("ps", [P, 8, 512], F32))
        bank = [ps[:, n, :] for n in range(8)]
        PT = [bank[4], bank[5]]
        M = [bank[6], bank[7]]

        w_kv = sb("w_kv", [P, C, 2 * D])
        w_q = sb("w_q", [P, C, D])
        w_o = sb("w_o", [P, C, D])
        w_qk2 = sb("w_qk2", [P, C, 2 * D])
        w_v2 = sb("w_v2", [P, C, D])
        w_gate = sb("w_gate", [P, C, D])
        w_out = sb("w_out", [P, C, D])
        w_route = sb("w_route", [P, C, E])
        w1 = sb("w1", [P, C, E * F])
        w2 = sb("w2", [P, FC, E * D])
        w_mix = w_gate
        r_kv = sb("r_kv", [P, 2 * D])
        r_q = sb("r_q", [P, D])
        r_o = sb("r_o", [P, D])
        r_gate = sb("r_gate", [P, D])
        r_scale = sb("r_scale", [P, D])
        r_n1 = sb("r_n1", [P, 2, D])
        r_n2 = sb("r_n2", [P, 2, D])
        r_route = sb("r_route", [P, E])
        rope = sb("rope", [P, 2, D])
        r_mix = r_gate
        ident = sb("ident", [P, P])
        ident_bf = sb("ident_bf", [P, P], BF16)
        ones = sb("ones", [P, P])
        before_me = sb("before_me", [P, P])
        mask_bf = sb("mask_bf", [P, HG, P], BF16)
        headmask = sb("headmask", [P, P // HD])
        minus_half = sb("minus_half", [P, 1])
        x_all = sb("x_all", [P, B, D])
        x1_all = sb("x1_all", [P, B, D])
        logits = sb("logits", [P, B, E])
        wsum = sb("wsum", [P, B])
        kexp = sb("kexp", [P, SLOTS, H, P])
        prob = sb("prob", [P, G, HG * P])
        pts = sb("pts", [P, 2, HG * P])
        b1_all = kexp[:, :, :, :].rearrange("p s h k -> p (s h k)")
        b2_all = prob[:, :, :].rearrange("p g k -> p (g k)")
        g_all = w1[:, 0, :].rearrange("p (b d) -> p b d", b=B)
        w_adapt = w1[:, 1, :].rearrange("p (k n) -> p k n", k=K_ADAPT)
        ARENA = 4608
        arena = [sb(f"arena{u}", [P, ARENA]) for u in range(SLOTS)]

        def carve(a, sizes):
            out, off = [], 0
            for n in sizes:
                out.append(a[:, off:off + n])
                off += n
            assert off <= ARENA
            return out
        (x_in, c_in, xbo, xn, srcT, qk, vaug, qkT, ots, oT, xcur) = map(list, zip(*[
            carve(arena[u], [D, D, D, D, 2 * D, 2 * D, H * VW, 2 * D, 512, D, D]) for u in range(SLOTS)]))
        o_tok, gate, tmp = xn, [sb(f"gate{u}", [P, D]) for u in range(SLOTS)], [sb(f"tmp{u}", [P, 2 * D]) for u in range(SLOTS)]
        vaug = [v.rearrange("p (h w) -> p h w", w=VW) for v in vaug]
        stats = [sb(f"stats{u}", [P, 6]) for u in range(XSLOTS)]
        mv = [sb(f"mv{u}", [P, 2]) for u in range(XSLOTS)]
        veps = [sb(f"veps{u}", [P, 1]) for u in range(XSLOTS)]
        rstd = [sb(f"rstd{u}", [P, 1]) for u in range(XSLOTS)]
        spare = [sb(f"spare{u}", [P, 1]) for u in range(XSLOTS)]
        rsum = [sb(f"rsum{u}", [P, H]) for u in range(SLOTS)]
        rowscale = [sb(f"rowscale{u}", [P, H]) for u in range(SLOTS)]
        rz = [sb(f"rz{u}", [P, H]) for u in range(SLOTS)]
        nbias = sb("nbias", [P, H])
        (xe, xeT, hid, hT, ye) = map(list, zip(*[
            carve(arena[u // 2][:, (u % 2) * (ARENA // 2):(u % 2 + 1) * (ARENA // 2)], [D, D, F, F, D])
            for u in range(XSLOTS)]))
        xe_rows = xe
        top8 = sb("top8", [P, B, 8])
        idx8 = sb("idx8", [P, B, 8], U32)
        chosen = sb("chosen", [P, B])
        onehot = sb("onehot", [P, B, E])
        tot = sb("tot", [P, B, E])
        base = sb("base", [P, B, E])
        iota_e = sb("iota_e", [P, E])
        iota_j = sb("iota_j", [P, B])
        iota_t = sb("iota_t", [P, TILES])
        iota_i = sb("iota_i", [P, 32], I32)
        ecount = sb("ecount", [P, E])
        etiles = sb("etiles", [P, E])
        estart = sb("estart", [P, E])
        eend = sb("eend", [P, E])
        ecmp = sb("ecmp", [P, E, B])
        tcmp = sb("tcmp", [P, TILES, E])
        texp = sb("texp", [P, TILES])
        texp_i = sb("texp_i", [P, TILES], I32)
        pos = sb("pos", [P, B])
        pos_u = sb("pos_u", [P, B], U32)
        small = sb("small", [P, 4, B])
        gcol = sb("gcol", [P, 2, E, FC])
        ecol = [sb(f"ecol{u}", [P, 2, FC]) for u in range(XSLOTS)]
        rs_row = sb("rs_row", [P, E])
        ers = [sb(f"ers{u}", [P, 1]) for u in range(XSLOTS)]
        ids_i = sb("ids_i", [P, K_ADAPT], I32)
        ids_f = sb("ids_f", [P, K_ADAPT])
        ids_n = sb("ids_n", [P, K_ADAPT])
        wts = sb("wts", [P, K_ADAPT])
        b_adapt = w2[:, 0, :].rearrange("p (k d) -> p k d", k=K_ADAPT)

        sorted_x = nc.dram_tensor("sorted_x", [TILES * P, D], F32)
        sorted_y = nc.dram_tensor("sorted_y", [TILES * P, D], F32)

        x_loaded = [sem(f"x_loaded{u}") for u in range(SLOTS)]
        c_loaded = [sem(f"c_loaded{u}") for u in range(SLOTS)]
        weights0 = sem("weights0")
        weights2 = sem("weights2")
        rows2 = sem("rows2")
        weights3 = sem("weights3")
        adapters = sem("adapters")
        consts = sem("consts")
        pool_own = sem("pool_own")
        dve_own = sem("dve_own")
        act_own = sem("act_own")
        ready = [sem(f"ready{u}") for u in range(SLOTS)]
        full = [sem(f"full{u}") for u in range(SLOTS)]
        var_ready = [sem(f"var_ready{u}") for u in range(SLOTS)]
        rstd_ready = [sem(f"rstd_ready{u}") for u in range(SLOTS)]
        kexp_ready = [sem(f"kexp_ready{u}") for u in range(SLOTS)]
        z_ready = [sem(f"z_ready{u}") for u in range(SLOTS)]
        ez_ready = [sem(f"ez_ready{u}") for u in range(SLOTS)]
        kept = [sem(f"kept{u}") for u in range(SLOTS)]
        scored = sem("scored")
        maxed = sem("maxed")
        exped = sem("exped")
        turned = sem("turned")
        copied = sem("copied")
        mixed = sem("mixed")
        y_done = [sem(f"y_done{u}") for u in range(SLOTS)]
        y_stored = [sem(f"y_stored{u}") for u in range(SLOTS)]
        zeroed = sem("zeroed")
        zero_ready = sem("zero_ready")
        route_a = sem("route_a")
        route_b = sem("route_b")
        route_c = sem("route_c")
        scattered = sem("scattered")
        gathered = sem("gathered")
        tile_in, tile_full, tile_ready, tile_var, tile_rstd, tile_cols, tile_out, tile_stored = (
            [sem(f"{name}{s}") for s in range(XSLOTS)]
            for name in ("tile_in", "tile_full", "tile_ready", "tile_var", "tile_rstd", "tile_cols", "tile_out", "tile_stored"))
        dve_own2 = sem("dve_own2")
        dve_own3 = sem("dve_own3")
        pool_own3 = sem("pool_own3")
        mix_ready = sem("mix_ready")

        def slot_bn(i, u):
            return i * SLOTS + u

        def bc_row(name, n):
            return t[name].rearrange("(a n) -> a n", a=1).broadcast_to([P, n])

        def pool_steps(pool):
            def rstd_step(u, n):
                pool.wait_ge(var_ready[u], n)
                pool.tensor_tensor(rstd[u][:, :], veps[u][:, :], minus_half[:, :], ALU.pow).then_inc(rstd_ready[u], 1)

            def expand(u, n, seen):
                pool.wait_ge(ready[u], seen)
                for g in range(G):
                    c = g // 2
                    keys = qkT[u][:, D + c * P:D + (c + 1) * P]
                    h0 = (g % 2) * HG
                    pool.tensor_tensor(kexp[:, u, g * HG:(g + 1) * HG, :], keys.unsqueeze(1).broadcast_to([P, HG, P]),
                                       headmask[:, h0:h0 + HG].unsqueeze(2).broadcast_to([P, HG, P]),
                                       ALU.mult).then_inc(kexp_ready[u], 1)

            def keep(u, dst, src, b, value, saved):
                pool.wait_ge(ready[u], value)
                pool.tensor_copy(dst[:, bass.ds(b, 1), :].rearrange("p a d -> p (a d)"), src).then_inc(kept[u], 1)

            def step(name, core, st):
                if core is not None:
                    return
                u, i = st
                if name == "a_norm":
                    rstd_step(u, at(i, LN1, 0))
                elif name == "a_qkT":
                    expand(u, 2, at(i, STEP1, 4))
                elif name == "b_res":
                    rstd_step(u, at(i, LN1, 1))
                elif name == "b_norm":
                    keep(u, x_all, xcur[u], slot_bn(i, u), at(i, STEP1, 8), None)
                elif name == "b_qkT":
                    expand(u, 2, at(i, STEP1, 12))
                elif name == "c_out":
                    rstd_step(u, at(i, LN1, 2))
                elif name == "c_norm":
                    keep(u, x1_all, tmp[u][:, 0:D], slot_bn(i, u), at(i, STEP1, 18), None)
                elif name == "d_moe":
                    rstd_step(u, at(i, LN3, 0, NI * LN1))
                elif name == "d_norm":
                    rstd_step(u, at(i, LN3, 1, NI * LN1))
                elif name == "d_qkT":
                    expand(u, 1, at(i, STEP3, 4, NI * STEP1))
                elif name == "e_res":
                    rstd_step(u, at(i, LN3, 2, NI * LN1))
            return step

        def core_number(core):
            u, a, i = core
            if a == 2:
                return i * SLOTS + (u + 2 * SLOTS * NI), i + 2 * NI
            return i * (2 * SLOTS) + (a * SLOTS + u), i * 2 + a

        def groups(n, g):
            return n * G + (g + 1)

        def product(core):
            u, a, i = core
            return at(i, STEP3, 4, NI * STEP1) if a == 2 else at(i, STEP1, 12 if a else 4)

        def pe_steps(pe):
            def transposes(dst, srcs):
                for n, s in enumerate(srcs):
                    last = pe.transpose(dst[:, n * P:(n + 1) * P], s, ident[:, :])
                return last

            def halves(x):
                return [x[:, c * P:(c + 1) * P] for c in range(x.shape[1] // P)]

            def project(dst, xT, w):
                for c in range(C):
                    last = pe.matmul(dst, xT[:, c * P:(c + 1) * P], w[:, c, :], start=(c == 0), stop=(c == C - 1))
                return last

            def core_step(name, core, g):
                u, a, i = core
                n, nu = core_number(core)
                if name == "scores":
                    if g == 0:
                        pe.wait_ge(ready[u], product(core))
                    pe.wait_ge(kexp_ready[u], groups(nu, g))
                    wait(pe, exped, groups(n, g) - G)
                    if a != 1:
                        pe.matmul(bank[g], ident_bf[:, :], mask_bf[:, :, :].rearrange("p h k -> p (h k)"),
                                  start=True, stop=False)
                    c = g // 2
                    pe.matmul(bank[g], qkT[u][:, c * P:(c + 1) * P],
                              kexp[:, u, g * HG:(g + 1) * HG, :].rearrange("p h k -> p (h k)"),
                              start=(a == 1), stop=True).then_inc(scored, 1)
                elif name == "turn":
                    pe.wait_ge(exped, groups(n, g))
                    wait(pe, copied, groups(n, g) - 2)
                    transposes(PT[g % 2], [prob[:, g, j * P:(j + 1) * P] for j in range(HG)]).then_inc(turned, 1)
                else:
                    if g == 0:
                        pe.wait_ge(ready[u], product(core))
                    pe.wait_ge(copied, groups(n, g))
                    for j in range(HG):
                        last = pe.matmul(M[u][VW * j:VW * (j + 1), g * P:(g + 1) * P], vaug[u][:, g * HG + j, :],
                                         pts[:, g % 2, j * P:(j + 1) * P], start=True, stop=True)
                    last.then_inc(mixed, 1)

            def step(name, core, st):
                if core is not None:
                    return core_step(name, core, st)
                u, i = st
                m = M[u]

                def start(k):
                    pe.wait_ge(ready[u], at(i, STEP1, k))

                def start3(k):
                    pe.wait_ge(ready[u], at(i, STEP3, k, NI * STEP1))
                if name == "a_norm2":
                    if isinstance(i, int) and i == 0 and u == 0:
                        pe.wait_ge(weights0, W0_ALL)
                    start(0)
                    pe.wait_ge(c_loaded[u], at(i, 16, 15))
                    transposes(m, halves(c_in[u]) + halves(xn[u])).then_inc(full[u], 1)
                elif name == "a_kv":
                    start(1)
                    project(m, srcT[u][:, 0:D], w_kv).then_inc(full[u], 1)
                elif name == "a_q":
                    start(2)
                    project(m[:, 0:D], srcT[u][:, D:2 * D], w_q).then_inc(full[u], 1)
                elif name == "a_qkT":
                    start(3)
                    transposes(m, halves(qk[u])).then_inc(full[u], 1)
                elif name == "b_o":
                    start(5)
                    transposes(m, halves(ots[u])).then_inc(full[u], 1)
                elif name == "b_oT":
                    start(6)
                    transposes(m, halves(o_tok[u])).then_inc(full[u], 1)
                elif name == "b_res":
                    start(7)
                    project(m[:, 0:D], oT[u], w_o).then_inc(full[u], 1)
                elif name == "b_norm":
                    start(8)
                    transposes(m, halves(xn[u])).then_inc(full[u], 1)
                elif name == "b_qk":
                    start(9)
                    project(m, srcT[u][:, 0:D], w_qk2).then_inc(full[u], 1)
                elif name == "b_v":
                    start(10)
                    project(m[:, 0:D], srcT[u][:, 0:D], w_v2).then_inc(full[u], 1)
                elif name == "b_qkT":
                    start(11)
                    transposes(m, halves(qk[u])).then_inc(full[u], 1)
                elif name == "c_o":
                    start(13)
                    transposes(m, halves(ots[u])).then_inc(full[u], 1)
                elif name == "c_oT":
                    start(14)
                    transposes(m, halves(gate[u])).then_inc(full[u], 1)
                elif name == "c_gate":
                    start(15)
                    project(m[:, 0:D], oT[u], w_gate).then_inc(full[u], 1)
                elif name == "c_gT":
                    start(16)
                    transposes(m, halves(gate[u])).then_inc(full[u], 1)
                elif name == "c_out":
                    start(17)
                    project(m[:, 0:D], oT[u], w_out).then_inc(full[u], 1)
                elif name == "c_x1T":
                    start(18)
                    transposes(m, halves(tmp[u][:, 0:D])).then_inc(full[u], 1)
                elif name == "c_logits":
                    start(19)
                    project(m[:, 0:E], oT[u], w_route).then_inc(full[u], 1)
                elif name == "d_norm2":
                    start3(0)
                    pe.wait_ge(c_loaded[u], at(i, 16, 15, 16 * NI))
                    transposes(m, halves(c_in[u]) + halves(xn[u])).then_inc(full[u], 1)
                elif name == "d_kv":
                    start3(1)
                    project(m, srcT[u][:, 0:D], w_kv).then_inc(full[u], 1)
                elif name == "d_q":
                    start3(2)
                    project(m[:, 0:D], srcT[u][:, D:2 * D], w_q).then_inc(full[u], 1)
                elif name == "d_qkT":
                    start3(3)
                    transposes(m, halves(qk[u])).then_inc(full[u], 1)
                elif name == "e_o":
                    start3(5)
                    transposes(m, halves(ots[u])).then_inc(full[u], 1)
                elif name == "e_oT":
                    start3(6)
                    transposes(m, halves(o_tok[u])).then_inc(full[u], 1)
                elif name == "e_res":
                    start3(7)
                    project(m[:, 0:D], oT[u], w_o).then_inc(full[u], 1)
                elif name == "e_norm":
                    start3(8)
                    transposes(m, halves(xn[u])).then_inc(full[u], 1)
                elif name == "e_ffn":
                    start3(9)
                    project(m[:, 0:D], srcT[u][:, 0:D], w_mix).then_inc(full[u], 1)
            return step

        def act_steps(act):
            def core_step(name, core, g):
                u, a, i = core
                n, _ = core_number(core)
                if name == "scores":
                    act.wait_ge(maxed, groups(n, g))
                    wait(act, turned, groups(n, g) - G)
                    for j in range(HG):
                        h = g * HG + j
                        last = act.activation(prob[:, g, j * P:(j + 1) * P], bank[g][:, j * P:(j + 1) * P], ACT.Exp,
                                              bias=nbias[:, h:h + 1],
                                              scale=rowscale[u][:, h:h + 1] if a == 1 else float(HD) ** -0.5)
                    last.then_inc(exped, 1)
                elif name == "mix" and g == G - 1:
                    act.wait_ge(mixed, groups(n, g))
                    act.copy(ots[u], M[u]).then_inc(ready[u], 1)

            def step(name, core, st):
                if core is not None:
                    return core_step(name, core, st)
                u, i = st
                m = M[u]

                def copy_out(dst, n, k, per=STEP1, base=0):
                    act.wait_ge(full[u], at(i, per - 2 if per == STEP1 else per - 1, k, base))
                    act.copy(dst, m[:, 0:n]).then_inc(ready[u], 1)
                if name == "a_norm2":
                    copy_out(srcT[u], 512, 0)
                elif name == "a_qkT":
                    copy_out(qkT[u], 512, 3)
                elif name == "b_oT":
                    copy_out(oT[u], D, 5)
                elif name == "b_norm":
                    copy_out(srcT[u][:, 0:D], D, 7)
                elif name == "b_qk":
                    copy_out(qk[u], 512, 8)
                elif name == "b_v":
                    act.wait_ge(full[u], at(i, STEP1 - 2, 9))
                    act.copy(vaug[u][:, :, 0:HD], m[:, 0:D].rearrange("p (h w) -> p h w", w=HD)).then_inc(ready[u], 1)
                elif name == "b_scale":
                    act.wait_ge(z_ready[u], at(i, 2, 0))
                    act.activation(rz[u][:, :], rsum[u][:, :], ACT.Exp, scale=-1.0).then_inc(ez_ready[u], 1)
                elif name == "b_qkT":
                    copy_out(qkT[u], 512, 10)
                elif name == "c_oT":
                    copy_out(oT[u], D, 12)
                elif name == "c_gate":
                    act.wait_ge(z_ready[u], at(i, 2, 1))
                    act.activation(tmp[u][:, D:2 * D], tmp[u][:, 0:D], ACT.Exp, scale=-1.0).then_inc(ez_ready[u], 1)
                elif name == "c_gT":
                    copy_out(oT[u], D, 14)
                elif name == "c_x1T":
                    copy_out(oT[u], D, 16)
                elif name == "d_norm2":
                    copy_out(srcT[u], 512, 0, STEP3, NI * (STEP1 - 2))
                elif name == "d_qkT":
                    copy_out(qkT[u], 512, 3, STEP3, NI * (STEP1 - 2))
                elif name == "e_oT":
                    copy_out(oT[u], D, 5, STEP3, NI * (STEP1 - 2))
                elif name == "e_norm":
                    copy_out(srcT[u][:, 0:D], D, 7, STEP3, NI * (STEP1 - 2))
            return step

        def dve_steps(dve, own):
            def norm_stats(u, src):
                own.mark(dve.bn_stats(stats[u][:, :], src))
                own.join_by(spare[u][:, :])
                own.mark(dve.bn_aggr(mv[u][:, :], stats[u][:, :]))
                own.join()
                dve.tensor_scalar(veps[u][:, :], mv[u][:, 1:2], EPS, None, ALU.add).then_inc(var_ready[u], 1)

            def normalize(u, dst, src, n):
                dve.wait_ge(rstd_ready[u], n)
                return dve.tensor_scalar(dst, src, mv[u][:, 0:1], rstd[u][:, :], ALU.subtract, ALU.mult)

            def heads(x, w):
                return x.rearrange("p (h w) -> p h w", w=w)

            def sigmoid_of(dst, e, scale):
                own.mark(dve.tensor_scalar(e, e, 1.0, 1.0 / scale, ALU.add, ALU.mult))
                own.join()
                return dve.reciprocal(dst, e)

            def attention_out(u, dst):
                o = heads(M[u], VW)
                own.mark(dve.reciprocal(rsum[u][:, :], o[:, :, HD]))
                own.join()
                dve.tensor_tensor(heads(dst, HD), o[:, :, 0:HD],
                                  rsum[u][:, :].unsqueeze(2).broadcast_to([P, H, HD]), ALU.mult).then_inc(ready[u], 1)

            def core_step(name, core, g):
                u, a, i = core
                n, _ = core_number(core)
                if name == "scores":
                    dve.wait_ge(scored, groups(n, g))
                    hs = slice(g * HG, (g + 1) * HG)
                    own.mark(dve.tensor_reduce(nbias[:, hs], bank[g].rearrange("p (h k) -> p h k", h=HG), AX.X, ALU.max, negate=True))
                    own.join()
                    if a == 1:
                        dve.tensor_tensor(nbias[:, hs], nbias[:, hs], rowscale[u][:, hs], ALU.mult).then_inc(maxed, 1)
                    else:
                        dve.tensor_scalar(nbias[:, hs], nbias[:, hs], float(HD) ** -0.5, None, ALU.mult).then_inc(maxed, 1)
                elif name == "turn":
                    dve.wait_ge(turned, groups(n, g))
                    wait(dve, mixed, groups(n, g) - 2)
                    dve.tensor_copy(pts[:, g % 2, :], PT[g % 2]).then_inc(copied, 1)

            def step(name, core, st):
                if core is not None:
                    return core_step(name, core, st)
                u, i = st
                m = M[u]

                def taken(k):
                    dve.wait_ge(full[u], at(i, STEP1 - 2, k))

                def taken3(k):
                    dve.wait_ge(full[u], at(i, STEP3 - 1, k, NI * (STEP1 - 2)))
                if name == "a_norm":
                    dve.wait_ge(x_loaded[u], at(i, 16, 15))
                    own.mark(dve.tensor_tensor(xbo[u], x_in[u], r_o[:, :], ALU.add))
                    norm_stats(u, x_in[u])
                elif name == "a_norm2":
                    normalize(u, xn[u], x_in[u], at(i, LN1, 0)).then_inc(ready[u], 1)
                elif name == "a_kv":
                    taken(1)
                    own.mark(dve.tensor_tensor(qk[u][:, D:2 * D], m[:, 0:D], r_kv[:, 0:D], ALU.add))
                    dve.tensor_tensor(vaug[u][:, :, 0:HD], heads(m[:, D:2 * D], HD), heads(r_kv[:, D:2 * D], HD), ALU.add).then_inc(ready[u], 1)
                elif name == "a_q":
                    taken(2)
                    dve.tensor_tensor(qk[u][:, 0:D], m[:, 0:D], r_q[:, :], ALU.add).then_inc(ready[u], 1)
                elif name == "b_o":
                    taken(4)
                    attention_out(u, o_tok[u])
                elif name == "b_res":
                    taken(6)
                    if not (isinstance(i, int) and i == 0):
                        dve.wait_ge(kept[u], at(i, 2, 0, -2))
                    own.mark(dve.tensor_tensor(xcur[u], m[:, 0:D], xbo[u], ALU.add))
                    own.join()
                    norm_stats(u, xcur[u])
                elif name == "b_norm":
                    normalize(u, xn[u], xcur[u], at(i, LN1, 1)).then_inc(ready[u], 1)
                elif name == "b_scale":
                    dve.wait_ge(ready[u], at(i, STEP1, 10))
                    if not (isinstance(i, int) and i == 0):
                        dve.wait_ge(kept[u], at(i, 2, 1, -2))
                    own.mark(dve.tensor_tensor(tmp[u][:, 0:D], qk[u][:, 0:D], r_scale[:, :], ALU.mult))
                    own.join()
                    dve.tensor_reduce(rsum[u][:, :], heads(tmp[u][:, 0:D], HD), AX.X, ALU.add).then_inc(z_ready[u], 1)
                    dve.wait_ge(ez_ready[u], at(i, 2, 0))
                    own.mark(sigmoid_of(rowscale[u][:, :], rz[u][:, :], 2.0 * float(HD) ** -0.5))
                    own.join()
                elif name == "c_o":
                    taken(11)
                    attention_out(u, gate[u])
                elif name == "c_gate":
                    taken(13)
                    dve.tensor_tensor(tmp[u][:, 0:D], m[:, 0:D], r_gate[:, :], ALU.add).then_inc(z_ready[u], 1)
                elif name == "c_gate2":
                    dve.wait_ge(ez_ready[u], at(i, 2, 1))
                    own.mark(sigmoid_of(tmp[u][:, 0:D], tmp[u][:, D:2 * D], 1.0))
                    own.join()
                    dve.tensor_tensor(gate[u][:, :], gate[u][:, :], tmp[u][:, 0:D], ALU.mult).then_inc(ready[u], 1)
                elif name == "c_out":
                    taken(15)
                    own.mark(dve.tensor_tensor(tmp[u][:, D:2 * D], m[:, 0:D], xn[u], ALU.add))
                    own.join()
                    norm_stats(u, tmp[u][:, D:2 * D])
                elif name == "c_norm":
                    own.mark(normalize(u, tmp[u][:, 0:D], tmp[u][:, D:2 * D], at(i, LN1, 2)))
                    own.join()
                    own.mark(dve.tensor_tensor(tmp[u][:, 0:D], tmp[u][:, 0:D], r_n1[:, 0, :], ALU.mult))
                    own.join()
                    dve.tensor_tensor(tmp[u][:, 0:D], tmp[u][:, 0:D], r_n1[:, 1, :], ALU.add).then_inc(ready[u], 1)
                elif name == "c_logits":
                    taken(17)
                    own.mark(dve.tensor_tensor(logits[:, bass.ds(slot_bn(i, u), 1), :].rearrange("p a e -> p (a e)"),
                                               m[:, 0:E], r_route[:, :], ALU.add))
                elif name == "d_moe":
                    b = slot_bn(i, u)
                    row = lambda a: a[:, bass.ds(b, 1), :].rearrange("p a d -> p (a d)")
                    own.mark(dve.scalar_tensor_tensor(out=tmp[u][:, 0:D], in0=row(g_all), scalar=wsum[:, bass.ds(b, 1)],
                                                      in1=row(x1_all), op0=ALU.mult, op1=ALU.add))
                    own.join()
                    norm_stats(u, tmp[u][:, 0:D])
                elif name == "d_norm":
                    b = slot_bn(i, u)
                    own.mark(normalize(u, tmp[u][:, 0:D], tmp[u][:, 0:D], at(i, LN3, 0, NI * LN1)))
                    own.join()
                    own.mark(dve.tensor_tensor(tmp[u][:, 0:D], tmp[u][:, 0:D], r_n2[:, 0, :], ALU.mult))
                    own.join()
                    own.mark(dve.tensor_tensor(tmp[u][:, 0:D], tmp[u][:, 0:D], r_n2[:, 1, :], ALU.add))
                    own.join()
                    own.mark(dve.tensor_tensor(xcur[u], tmp[u][:, 0:D], x_all[:, bass.ds(b, 1), :].rearrange("p a d -> p (a d)"), ALU.add))
                    own.join()
                    own.mark(dve.tensor_tensor(xbo[u], xcur[u], r_o[:, :], ALU.add))
                    norm_stats(u, xcur[u])
                elif name == "d_norm2":
                    normalize(u, xn[u], xcur[u], at(i, LN3, 1, NI * LN1)).then_inc(ready[u], 1)
                elif name == "d_kv":
                    taken3(1)
                    own.mark(dve.tensor_tensor(qk[u][:, D:2 * D], m[:, 0:D], r_kv[:, 0:D], ALU.add))
                    dve.tensor_tensor(vaug[u][:, :, 0:HD], heads(m[:, D:2 * D], HD), heads(r_kv[:, D:2 * D], HD), ALU.add).then_inc(ready[u], 1)
                elif name == "d_q":
                    taken3(2)
                    own.mark(dve.tensor_tensor(qk[u][:, 0:D], m[:, 0:D], r_q[:, :], ALU.add))
                    own.join()
                elif name == "d_rope":
                    both = qk[u].rearrange("p (a d) -> p a d", a=2)
                    hh = HD // 2
                    for a in range(2):
                        rot = heads(tmp[u][:, a * D:(a + 1) * D], HD)
                        x = heads(qk[u][:, a * D:(a + 1) * D], HD)
                        sn = heads(rope[:, 1, :], HD)
                        own.mark(dve.tensor_tensor(rot[:, :, 0:hh], x[:, :, hh:HD], sn[:, :, 0:hh], ALU.mult))
                        own.mark(dve.tensor_tensor(rot[:, :, hh:HD], x[:, :, 0:hh], sn[:, :, hh:HD], ALU.mult))
                    own.join()
                    own.mark(dve.tensor_tensor(both, both, rope[:, 0, :].unsqueeze(1).broadcast_to([P, 2, D]), ALU.mult))
                    own.join()
                    dve.tensor_tensor(qk[u], qk[u], tmp[u][:, :], ALU.add).then_inc(ready[u], 1)
                elif name == "e_o":
                    taken3(4)
                    attention_out(u, o_tok[u])
                elif name == "e_res":
                    taken3(6)
                    own.mark(dve.tensor_tensor(xcur[u], m[:, 0:D], xbo[u], ALU.add))
                    own.join()
                    own.mark(dve.tensor_tensor(xbo[u], xcur[u], r_mix[:, :], ALU.add))
                    norm_stats(u, xcur[u])
                elif name == "e_norm":
                    normalize(u, xn[u], xcur[u], at(i, LN3, 2, NI * LN1)).then_inc(ready[u], 1)
                elif name == "e_ffn":
                    taken3(8)
                    wait(dve, y_stored[u], at(i, 16, -1))
                    dve.tensor_tensor(gate[u][:, :], m[:, 0:D], xbo[u], ALU.add).then_inc(y_done[u], 1)
            return step

        W0_ALL = 16 * 16
        with nc.Block() as block:

            @block.sync
            def _(sp):
                def load_rows(u, i):
                    if isinstance(i, int) and i == 0:
                        pass
                    else:
                        sp.wait_ge(ready[u], at(i, STEP1, 8, -STEP1))
                    b = slot_bn(i, u)
                    sp.dma_start(x_in[u], t["x"][bass.ds(b, 1), :, :].rearrange("a p d -> p (a d)")).then_inc(x_loaded[u], 16)
                    sp.dma_start(c_in[u], t["ctx"][bass.ds(b, 1), :, :].rearrange("a p d -> p (a d)")).then_inc(c_loaded[u], 16)

                load_rows(0, 0)
                sp.dma_start(w_kv[:, :, :], t["w_kv"].rearrange("(c p) n -> p c n", p=P)).then_inc(weights0, 16)
                sp.dma_start(r_kv[:, :], bc_row("r_kv", 2 * D)).then_inc(weights0, 16)
                sp.dma_start(w_q[:, :, :], t["w_q"].rearrange("(c p) n -> p c n", p=P)).then_inc(weights0, 16)
                sp.dma_start(r_q[:, :], bc_row("r_q", D)).then_inc(weights0, 16)
                load_rows(1, 0)
                for dst, name in ((w_o, "w_o"), (w_qk2, "w_qk2"), (w_v2, "w_v2"), (w_gate, "w_gate"),
                                  (w_out, "w_out"), (w_route, "w_route")):
                    sp.dma_start(dst[:, :, :], t[name].rearrange("(c p) n -> p c n", p=P)).then_inc(weights0, 16)
                for dst, name, n in ((r_o, "r_o", D), (r_gate, "r_gate", D), (r_scale, "r_scale", D),
                                     (r_route, "r_route", E)):
                    sp.dma_start(dst[:, :], bc_row(name, n)).then_inc(weights0, 16)
                sp.dma_start(r_n1[:, :, :].rearrange("p a d -> p (a d)"), bc_row("r_n1", 2 * D)).then_inc(weights0, 16)
                sp.dma_start(r_n2[:, :, :].rearrange("p a d -> p (a d)"), bc_row("r_n2", 2 * D)).then_inc(weights0, 16)
                sp.dma_start(ids_i[:, :], t["ids"].rearrange("(a n) -> a n", a=1).broadcast_to([P, K_ADAPT])).then_inc(weights2, 16)
                sp.dma_start(wts[:, :], bc_row("wts", K_ADAPT)).then_inc(weights2, 16)
                sp.dma_start(rs_row[:, :], bc_row("res_scale", E)).then_inc(weights2, 16)
                sp.dma_start(rope[:, :, :], t["rope"]).then_inc(weights2, 16)
                sp.dma_start(gcol[:, :, :, :], t["ln_gb"]).then_inc(weights2, 16)
                for e in range(E):
                    sp.dma_start(w1[:, :, e * F:(e + 1) * F], t["w1"][e].rearrange("(c p) n -> p c n", p=P)).then_inc(weights2, 16)
                    sp.dma_start(w2[:, :, e * D:(e + 1) * D], t["w2"][e].rearrange("(c p) n -> p c n", p=P)).then_inc(weights2, 16)
                sp.wait_ge(zero_ready, 1)
                for n in range(TILES):
                    sp.dma_start(sorted_x[n * P:(n + 1) * P, :].rearrange("p (a n) -> p a n", a=2), top8[:, :, :].rearrange("p b e -> p (b e)")[:, 0:P].unsqueeze(1).broadcast_to([P, 2, P])).then_inc(zeroed, 16)
                with sp.Fori(1, NI) as i:
                    for u in range(SLOTS):
                        load_rows(u, i)
                sp.wait_ge(ready[0], at(NI - 1, STEP1, 17))
                sp.wait_ge(ready[1], at(NI - 1, STEP1, 17))
                sp.wait_ge(turned, 2 * SLOTS * NI * G)
                sp.dma_start(b1_all, bc_row("b1", E * F)).then_inc(rows2, 16)
                sp.dma_start(b2_all, bc_row("b2", E * D)).then_inc(rows2, 16)
                for dst, name in ((w_kv, "w_kv3"), (w_q, "w_q3"), (w_o, "w_o3")):
                    sp.dma_start(dst[:, :, :], t[name].rearrange("(c p) n -> p c n", p=P)).then_inc(weights3, 16)
                for dst, name, n in ((r_kv, "r_kv3", 2 * D), (r_q, "r_q3", D), (r_o, "r_o3", D)):
                    sp.dma_start(dst[:, :], bc_row(name, n)).then_inc(weights3, 16)

            @block.gpsimd
            def _(pool):
                own = Chain(pool, pool_own)
                own.mark(pool.memset(ones[:, :], 1.0))
                own.mark(pool.memset(minus_half[:, :], -0.5))
                own.mark(pool.memset(mask_bf[:, :, :], 0.0))
                own.mark(pool.iota(iota_i[:, 0:32], pattern=[[1, 32]], base=0, channel_multiplier=0))
                own.join()
                own.mark(pool.affine_select(out=ident[:, :], in_=ones[:, :], compare_op=ALU.is_equal, fill=0.0,
                                            base=0, pattern=[[-1, P]], channel_multiplier=1))
                own.mark(pool.affine_select(out=ident_bf[:, :], in_=ones[:, :], compare_op=ALU.is_equal, fill=0.0,
                                            base=0, pattern=[[-1, P]], channel_multiplier=1))
                own.mark(pool.affine_select(out=before_me[:, :], in_=ones[:, :], compare_op=ALU.is_gt, fill=0.0,
                                            base=0, pattern=[[1, P]], channel_multiplier=-1))
                own.mark(pool.affine_select(out=mask_bf[:, :, :], in_=mask_bf[:, :, :], compare_op=ALU.is_ge, fill=MASKED,
                                            base=0, pattern=[[0, HG], [-1, P]], channel_multiplier=1))
                own.mark(pool.affine_select(out=headmask[:, :], in_=ones[:, 0:P // HD], compare_op=ALU.is_ge, fill=0.0,
                                            base=0, pattern=[[-HD, P // HD]], channel_multiplier=1))
                own.join()
                own.mark(pool.affine_select(out=headmask[:, :], in_=headmask[:, :], compare_op=ALU.is_ge, fill=0.0,
                                            base=HD - 1, pattern=[[HD, P // HD]], channel_multiplier=-1))
                own.mark(pool.tensor_copy(iota_e[:, :], iota_i[:, 0:E]))
                own.mark(pool.tensor_copy(iota_t[:, :], iota_i[:, 0:TILES]))
                own.mark(pool.tensor_scalar(iota_j[:, :], iota_i[:, 0:B], float(P), None, ALU.mult))
                own.join()
                for u in range(SLOTS):
                    own.mark(pool.memset(vaug[u], 0.0))
                own.join()
                for u in range(SLOTS):
                    pool.memset(vaug[u][:, :, HD:HD + 1], 1.0).then_inc(consts, 1)

                steps = pool_steps(pool)
                run_turns(pool, turn1, steps)

                pool.wait_ge(route_c, 1)
                pool.wait_ge(zeroed, 16 * TILES)
                for u in range(SLOTS):
                    pool.wait_ge(kept[u], 2 * NI)
                for b in range(B):
                    pool.indirect_dma_start(out=sorted_x[:, :], out_offset=bass.IndirectOffsetOnAxis(ap=pos_u[:, b:b + 1], axis=0),
                                            in_=x1_all[:, b, :], in_offset=None).then_inc(scattered, 16)
                pool.wait_ge(scattered, 16 * B)

            @block.tensor
            def _(pe):
                pe.wait_ge(consts, 2)
                run_turns(pe, turn1, pe_steps(pe))
                pe.wait_ge(route_a, 1)
                pe.matmul(bank[0][:, 0:P], before_me[:, :], onehot[:, :, :].rearrange("p b e -> p (b e)"), start=True, stop=True).then_inc(route_b, 1)
                pe.matmul(bank[1][:, 0:P], ones[:, :], onehot[:, :, :].rearrange("p b e -> p (b e)"), start=True, stop=True).then_inc(route_b, 1)

            @block.scalar
            def _(act):
                run_turns(act, turn1, act_steps(act))
                act.wait_ge(z_ready[0], 2 * NI + 1)
                act.activation(small[:, 1, :], small[:, 0, :], ACT.Exp).then_inc(ez_ready[0], 1)

            @block.vector
            def _(dve):
                dve.memset(top8[:, :, :], 0.0).then_inc(zero_ready, 1)
                dve.wait_ge(weights0, W0_ALL)
                dve.wait_ge(consts, 2)
                own = Chain(dve, dve_own)
                run_turns(dve, turn1, dve_steps(dve, own), own, PER_TURN1)

                dve.wait_ge(zeroed, 16 * TILES)
                own.join()
                own.mark(dve.tensor_scalar(ids_f[:, :], ids_i[:, :], 0.0, None, ALU.add))
                for b in range(B):
                    own.mark(dve.max(top8[:, b, :], logits[:, b, :]))
                own.join()
                for b in range(B):
                    own.mark(dve.max_index(idx8[:, b, :], top8[:, b, :], logits[:, b, :]))
                dve.tensor_tensor(small[:, 0, :], top8[:, :, 1], top8[:, :, 0], ALU.subtract).then_inc(z_ready[0], 1)
                own.join()
                own.mark(dve.tensor_tensor(chosen[:, :], idx8[:, :, 0], idx8[:, :, 1], ALU.max))
                own.join()
                dve.tensor_tensor(onehot[:, :, :], chosen[:, :].unsqueeze(2).broadcast_to([P, B, E]),
                                  iota_e[:, :].unsqueeze(1).broadcast_to([P, B, E]), ALU.is_equal).then_inc(route_a, 1)
                dve.wait_ge(ez_ready[0], 2 * NI + 1)
                own.mark(dve.tensor_scalar(small[:, 2, :], small[:, 1, :], 1.0, None, ALU.add))
                own.join()
                own.mark(dve.reciprocal(small[:, 3, :], small[:, 2, :]))
                own.join()
                own.mark(dve.tensor_tensor(small[:, 1, :], small[:, 1, :], small[:, 3, :], ALU.mult))
                own.join()
                own.mark(dve.tensor_tensor(wsum[:, :], small[:, 1, :], small[:, 3, :], ALU.add))
                dve.wait_ge(route_b, 2)
                own.mark(dve.tensor_copy(tot[:, :, :].rearrange("p b e -> p (b e)"), bank[1][:, 0:P]))
                own.mark(dve.memset(base[:, 0, :], 0.0))
                own.join()
                for b in range(1, B):
                    own.mark(dve.tensor_tensor(base[:, b, :], base[:, b - 1, :], tot[:, b - 1, :], ALU.add))
                    own.join()
                own.mark(dve.tensor_tensor(ecount[:, :], base[:, B - 1, :], tot[:, B - 1, :], ALU.add))
                own.join()
                own.mark(dve.tensor_tensor(ecmp[:, :, :], ecount[:, :].unsqueeze(2).broadcast_to([P, E, B]),
                                           iota_j[:, :].unsqueeze(1).broadcast_to([P, E, B]), ALU.is_gt))
                own.join()
                own.mark(dve.tensor_reduce(etiles[:, :], ecmp[:, :, :], AX.X, ALU.add))
                own.mark(dve.memset(estart[:, 0:1], 0.0))
                own.join()
                for e in range(1, E):
                    own.mark(dve.tensor_tensor(estart[:, e:e + 1], estart[:, e - 1:e], etiles[:, e - 1:e], ALU.add))
                    own.join()
                own.mark(dve.tensor_tensor(eend[:, :], estart[:, :], etiles[:, :], ALU.add))
                own.mark(dve.scalar_tensor_tensor(out=base[:, :, :], in0=estart[:, :].unsqueeze(1).broadcast_to([P, B, E]), scalar=float(P),
                                                  in1=base[:, :, :], op0=ALU.mult, op1=ALU.add))
                own.join()
                own.mark(dve.tensor_tensor(base[:, :, :], base[:, :, :],
                                           bank[0][:, 0:P].rearrange("p (b e) -> p b e", e=E), ALU.add))
                own.mark(dve.tensor_tensor(tcmp[:, :, :], iota_t[:, :].unsqueeze(2).broadcast_to([P, TILES, E]),
                                           eend[:, :].unsqueeze(1).broadcast_to([P, TILES, E]), ALU.is_ge))
                own.join()
                own.mark(dve.tensor_tensor(base[:, :, :], base[:, :, :], onehot[:, :, :], ALU.mult))
                own.mark(dve.tensor_reduce(texp[:, :], tcmp[:, :, :], AX.X, ALU.add))
                own.join()
                own.mark(dve.tensor_reduce(pos[:, :], base[:, :, :], AX.X, ALU.add))
                own.mark(dve.tensor_scalar(texp_i[:, :], texp[:, :], float(E - 1), None, ALU.min))
                own.join()
                dve.tensor_copy(pos_u[:, :], pos[:, :]).then_inc(route_c, 1)
                dve.wait_ge(weights2, 16)
                own.mark(dve.tensor_scalar(ids_n[:, :], ids_f[:, :], 0.0, float(ADAPTERS), ALU.is_lt, ALU.mult))
                own.join()
                own.mark(dve.tensor_tensor(ids_f[:, :], ids_f[:, :], ids_n[:, :], ALU.add))
                own.join()
                dve.tensor_scalar(ids_i[:, :], ids_f[:, :], 0.0, float(ADAPTERS - 1), ALU.max, ALU.min).then_inc(route_c, 1)


        TURNS2, REST2 = TILES // XSLOTS, TILES % XSLOTS

        def run_tiles(eng, turn):
            turn(0, XSLOTS)
            with eng.Fori(1, TURNS2) as i:
                turn(i, XSLOTS)
            turn(TURNS2, REST2)

        with nc.Block() as block:
            @block.sync
            def _(sp):
                def turn(i, n):
                    for s in range(n):
                        wait(sp, tile_out[s], i)
                        sp.dma_start(xe[s], sorted_x[bass.ds((i * XSLOTS + s) * P, P), :]).then_inc(tile_in[s], 16)
                run_tiles(sp, turn)

            @block.gpsimd
            def _(pool):
                def turn(i, n):
                    for s in range(n):
                        pool.wait_ge(tile_var[s], i + 1)
                        pool.tensor_tensor(rstd[s][:, :], veps[s][:, :], minus_half[:, :], ALU.pow).then_inc(tile_rstd[s], 1)
                    for s in range(n):
                        pool.wait_ge(tile_out[s], i + 1)
                        pool.dma_start(sorted_y[bass.ds((i * XSLOTS + s) * P, P), :], ye[s]).then_inc(tile_stored[s], 16)
                run_tiles(pool, turn)
                for s in range(XSLOTS):
                    pool.wait_ge(tile_stored[s], 16 * (TURNS2 + (s < REST2)))
                for b in range(B):
                    pool.indirect_dma_start(out=g_all[:, b, :], out_offset=None, in_=sorted_y[:, :],
                                            in_offset=bass.IndirectOffsetOnAxis(ap=pos_u[:, b:b + 1], axis=0)).then_inc(gathered, 16)
                pool.wait_ge(gathered, 16 * B)

            @block.tensor
            def _(pe):
                pe.wait_ge(weights2, 16 * (5 + 2 * E))

                def turn(i, n):
                    for s in range(n):
                        pe.wait_ge(tile_in[s], at(i, 16, 15))
                        wait(pe, tile_out[s], i)
                        for c in range(C):
                            last = pe.transpose(bank[s][:, c * P:(c + 1) * P], xe[s][:, c * P:(c + 1) * P], ident[:, :])
                        last.then_inc(tile_full[s], 1)
                    for s in range(n):
                        e = pe.value_load(texp_i[0:1, bass.ds(i * XSLOTS + s, 1)], min_val=0, max_val=E - 1)
                        pe.wait_ge(tile_ready[s], at(i, 3, 0))
                        for c in range(C):
                            last = pe.matmul(bank[s], xeT[s][:, c * P:(c + 1) * P], w1[:, c, bass.ds(e * F, F)],
                                             start=(c == 0), stop=(c == C - 1))
                        last.then_inc(tile_full[s], 1)
                    for s in range(n):
                        pe.wait_ge(tile_ready[s], at(i, 3, 1))
                        for c in range(FC):
                            last = pe.transpose(bank[s][:, c * P:(c + 1) * P], hid[s][:, c * P:(c + 1) * P], ident[:, :])
                        last.then_inc(tile_full[s], 1)
                    for s in range(n):
                        e = pe.value_load(texp_i[0:1, bass.ds(i * XSLOTS + s, 1)], min_val=0, max_val=E - 1)
                        pe.wait_ge(tile_ready[s], at(i, 3, 2))
                        for c in range(FC):
                            last = pe.matmul(bank[s][:, 0:D], hT[s][:, c * P:(c + 1) * P], w2[:, c, bass.ds(e * D, D)],
                                             start=(c == 0), stop=(c == FC - 1))
                        last.then_inc(tile_full[s], 1)
                run_tiles(pe, turn)

            @block.scalar
            def _(act):
                def turn(i, n):
                    for s in range(n):
                        act.wait_ge(tile_full[s], at(i, 4, 0))
                        act.copy(xeT[s], bank[s][:, 0:D]).then_inc(tile_ready[s], 1)
                    for s in range(n):
                        act.wait_ge(tile_full[s], at(i, 4, 2))
                        act.wait_ge(tile_cols[s], i + 1)
                        for c in range(FC):
                            last = act.activation(hT[s][:, c * P:(c + 1) * P], bank[s][:, c * P:(c + 1) * P], ACT.Gelu,
                                                  bias=ecol[s][:, 1, c:c + 1], scale=ecol[s][:, 0, c:c + 1])
                        last.then_inc(tile_ready[s], 1)
                run_tiles(act, turn)

            @block.vector
            def _(dve):
                dve.wait_ge(weights2, 16 * (5 + 2 * E))
                dve.wait_ge(rows2, 32)
                own = Chain(dve, dve_own2)

                def turn(i, n):
                    for s in range(n):
                        e = dve.value_load(texp_i[0:1, bass.ds(i * XSLOTS + s, 1)], min_val=0, max_val=E - 1)
                        dve.wait_ge(tile_full[s], at(i, 4, 1))
                        own.mark(dve.tensor_tensor(hid[s], bank[s], b1_all[:, bass.ds(e * F, F)], ALU.add))
                        own.join()
                        own.mark(dve.bn_stats(stats[s][:, :], hid[s]))
                        own.join_by(spare[s][:, :])
                        own.mark(dve.bn_aggr(mv[s][:, :], stats[s][:, :]))
                        own.join()
                        dve.tensor_scalar(veps[s][:, :], mv[s][:, 1:2], EPS, None, ALU.add).then_inc(tile_var[s], 1)
                        own.mark(dve.tensor_copy(ers[s][:, :], rs_row[:, bass.ds(e, 1)]))
                        dve.tensor_copy(ecol[s][:, :, :], gcol[:, :, bass.ds(e, 1), :].rearrange("p a o c -> p a (o c)")).then_inc(tile_cols[s], 1)
                    for s in range(n):
                        dve.wait_ge(tile_rstd[s], i + 1)
                        dve.tensor_scalar(hid[s], hid[s], mv[s][:, 0:1], rstd[s][:, :], ALU.subtract, ALU.mult).then_inc(tile_ready[s], 1)
                    for s in range(n):
                        e = dve.value_load(texp_i[0:1, bass.ds(i * XSLOTS + s, 1)], min_val=0, max_val=E - 1)
                        dve.wait_ge(tile_full[s], at(i, 4, 3))
                        wait(dve, tile_stored[s], at(i, 16, -1))
                        own.mark(dve.tensor_tensor(ye[s], bank[s][:, 0:D], b2_all[:, bass.ds(e * D, D)], ALU.add))
                        own.join()
                        dve.scalar_tensor_tensor(out=ye[s], in0=ye[s], scalar=ers[s][:, 0:1], in1=xe[s],
                                                 op0=ALU.mult, op1=ALU.add).then_inc(tile_out[s], 1)
                turn(0, XSLOTS)
                with dve.Fori(1, TURNS2) as i:
                    own.start(i - 1, XSLOTS * 6)
                    turn(i, XSLOTS)
                    own.end(TURNS2 - 1)
                turn(TURNS2, REST2)

        with nc.Block() as block:
            @block.sync
            def _(sp):
                def load_context(u, i):
                    if not (isinstance(i, int) and i == 0):
                        sp.wait_ge(ready[u], at(i, STEP3, 1, NI * STEP1 - STEP3))
                    sp.dma_start(c_in[u], t["ctx"][bass.ds(slot_bn(i, u), 1), :, :].rearrange("a p d -> p (a d)")).then_inc(c_loaded[u], 16)

                def store_rows(u, i):
                    sp.wait_ge(y_done[u], i + 1)
                    sp.dma_start(t["out"][bass.ds(slot_bn(i, u), 1), :, :].rearrange("a p d -> p (a d)"), gate[u][:, :]).then_inc(y_stored[u], 16)
                for u in range(SLOTS):
                    load_context(u, 0)
                for k in range(K_ADAPT):
                    a = sp.value_load(ids_i[0:1, k:k + 1], min_val=0, max_val=ADAPTERS - 1)
                    sp.dma_start(w_adapt[:, k, :].rearrange("p (c n) -> p c n", c=C),
                                 t["w_adapt"][bass.ds(a, 1), :, :].rearrange("o (c p) n -> p (o c) n", p=P)).then_inc(adapters, 16)
                    sp.dma_start(b_adapt[:, k, :], t["b_adapt"][bass.ds(a, 1), :].broadcast_to([P, D])).then_inc(adapters, 16)
                with sp.Fori(1, NI) as i:
                    for u in range(SLOTS):
                        load_context(u, i)
                    for u in range(SLOTS):
                        store_rows(u, i - 1)
                for u in range(SLOTS):
                    store_rows(u, NI - 1)
                    sp.wait_ge(y_stored[u], 16 * NI)

            @block.gpsimd
            def _(pool):
                own = Chain(pool, pool_own3)
                for u in range(SLOTS):
                    own.mark(pool.memset(vaug[u], 0.0))
                own.join()
                for u in range(SLOTS):
                    pool.memset(vaug[u][:, :, HD:HD + 1], 1.0).then_inc(consts, 1)
                run_turns(pool, turn3, pool_steps(pool))

            @block.tensor
            def _(pe):
                pe.wait_ge(weights3, 16 * 6)
                pe.wait_ge(mix_ready, 1)
                run_turns(pe, turn3, pe_steps(pe))

            @block.scalar
            def _(act):
                run_turns(act, turn3, act_steps(act))

            @block.vector
            def _(dve):
                dve.wait_ge(weights3, 16 * 6)
                own = Chain(dve, dve_own3)
                dve.wait_ge(adapters, 2 * 16 * K_ADAPT)
                mix = w_mix[:, :, :].rearrange("p c n -> p (c n)")
                for k in range(K_ADAPT):
                    if k:
                        own.join()
                    if k == 0:
                        own.mark(dve.tensor_scalar(mix, w_adapt[:, 0, :], wts[:, 0:1], None, ALU.mult))
                        own.mark(dve.tensor_scalar(r_mix[:, :], b_adapt[:, 0, :], wts[:, 0:1], None, ALU.mult))
                        continue
                    ins = dve.scalar_tensor_tensor(out=mix, in0=w_adapt[:, k, :], scalar=wts[:, k:k + 1], in1=mix,
                                                   op0=ALU.mult, op1=ALU.add)
                    if k == K_ADAPT - 1:
                        ins.then_inc(mix_ready, 1)
                    else:
                        own.mark(ins)
                    own.mark(dve.scalar_tensor_tensor(out=r_mix[:, :], in0=b_adapt[:, k, :], scalar=wts[:, k:k + 1], in1=r_mix[:, :],
                                                      op0=ALU.mult, op1=ALU.add))
                own.join()
                run_turns(dve, turn3, dve_steps(dve, own), own, PER_TURN3)


def kernel(**inputs):
    import concourse.bacc as bacc
    from concourse.bass_utils import run_bass_kernel_spmd

    x = {k: np.asarray(v) for k, v in inputs.items()}
    half = HD // 2
    freq = (np.float32(1.0) / np.float32(10000.0) ** (np.arange(half, dtype=np.float32) / np.float32(half))).astype(np.float32)
    angle = np.arange(P, dtype=np.float32)[:, None] * freq[None, :]
    cos, sin = np.cos(angle), np.sin(angle)
    rope = np.stack([np.tile(np.concatenate([cos, cos], 1), (1, H)), np.tile(np.concatenate([-sin, sin], 1), (1, H))], 1)
    cat = np.concatenate
    arrays = {
        "x": x["x"], "ctx": x["ctx_1024"],
        "w_kv": cat([x["L0_xattn_Wk"].T, x["L0_xattn_Wv"].T], 1), "r_kv": cat([x["L0_xattn_bk"], x["L0_xattn_bv"]]),
        "w_q": x["L0_xattn_Wq"].T, "r_q": x["L0_xattn_bq"], "w_o": x["L0_xattn_Wo"].T, "r_o": x["L0_xattn_bo"],
        "w_qk2": cat([x["L0_ffn_q_w"], x["L0_ffn_k_w"]], 1), "w_v2": x["L0_ffn_v_w"], "w_gate": x["L0_ffn_gate_w"],
        "w_out": x["L0_ffn_out_w"], "w_route": x["L0_ffn_moe_gate_w"], "r_gate": x["L0_ffn_gate_b"],
        "r_scale": x["L0_ffn_scale_w"].reshape(-1), "r_route": x["L0_ffn_moe_gate_b"],
        "r_n1": cat([x["L0_ffn_n1_g"], x["L0_ffn_n1_b"]]), "r_n2": cat([x["L0_ffn_n2_g"], x["L0_ffn_n2_b"]]),
        "w1": x["L0_ffn_w1"], "w2": x["L0_ffn_w2"], "b1": x["L0_ffn_b1"].reshape(-1), "b2": x["L0_ffn_b2"].reshape(-1),
        "ln_gb": np.stack([x["L0_ffn_ln_g"], x["L0_ffn_ln_b"]]).reshape(2, E, FC, P).transpose(3, 0, 1, 2), "res_scale": x["L0_ffn_res_scale"],
        "w_kv3": cat([x["L1_xattn_Wk"].T, x["L1_xattn_Wv"].T], 1), "r_kv3": cat([x["L1_xattn_bk"], x["L1_xattn_bv"]]),
        "w_q3": x["L1_xattn_Wq"].T, "r_q3": x["L1_xattn_bq"], "w_o3": x["L1_xattn_Wo"].T, "r_o3": x["L1_xattn_bo"],
        "w_adapt": x["L1_ffn_W"].transpose(0, 2, 1), "b_adapt": x["L1_ffn_b"], "ids": x["L1_ffn_ids"],
        "wts": x["L1_ffn_weights"], "rope": rope.astype(np.float32),
    }
    arrays = {f"in_{k}": np.ascontiguousarray(v) for k, v in arrays.items()}
    nc = bacc.Bacc("TRN2", target_bir_lowering=False, num_devices=1)
    t = {k[3:]: nc.dram_tensor(k, v.shape, mybir.dt.from_np(v.dtype), kind="ExternalInput").ap() for k, v in arrays.items()}
    t["out"] = nc.dram_tensor("out", (B, P, D), F32, kind="ExternalOutput").ap()
    build(nc, t)
    r = run_bass_kernel_spmd(nc, [arrays], core_ids=[0])
    return r.results[0]["out"]
```

```python
from contextlib import ExitStack

import numpy as np

import concourse.bass as bass
from concourse import mybir

F32 = mybir.dt.float32
BF16 = mybir.dt.bfloat16
I32 = mybir.dt.int32
U32 = mybir.dt.uint32
ALU = mybir.AluOpType
ACT = mybir.ActivationFunctionType
AX = mybir.AxisListType

P = 128
B, D, H, HD = 16, 256, 16, 16
C = D // P
SLOTS = 4
NI = B // SLOTS
G, HG = 4, 4
E, F = 8, 512
FC = F // P
TILES = B * P // P + E - 1
XSLOTS = 4
ADAPTERS, K_ADAPT = 32, 8
VW = 32
EPS = 1e-5
MASKED = -1e30
STEP1, STEP3 = 20, 10
PER_TURN1, PER_TURN3 = 124, 100
LN1, LN3 = 3, 2


def at(i, per, k, base=0):
    return i * per + (base + k + 1)


def wait(eng, sem, value):
    if isinstance(value, int) and value <= 0:
        return
    eng.wait_ge(sem, value)


class Chain:

    def __init__(self, eng, sem):
        self.eng, self.sem, self.base, self.k, self.turn, self.per = eng, sem, 0, 0, 0, 0

    def start(self, turn, per):
        self.base, self.k, self.turn, self.per = self.base + self.k, 0, turn, per

    def end(self, turns):
        assert self.k == self.per, (self.k, self.per)
        self.base, self.k, self.turn, self.per = self.base + turns * self.per, 0, 0, 0

    def mark(self, ins):
        ins.then_inc(self.sem, 1)
        self.k += 1

    def join_by(self, spare):
        self.join()
        self.mark(self.eng.memset(spare, 0.0))

    def join(self):
        self.eng.wait_ge(self.sem, self.turn * self.per + (self.base + self.k))


SIDE_CA = ((["c_o", "c_oT", "c_gate", "c_gate2", "c_gT"], []),
           (["c_out", "c_norm", "c_x1T", "c_logits"], ["a_stat", "a_norm", "a_T"]),
           ([], ["a_kv", "a_q", "a_qkT"]))
SIDE_B = (([], ["b_o", "b_oT", "b_res"]), ([], ["b_norm", "b_T", "b_qk", "b_v"]), ([], ["b_scale", "b_qkT", "b_scale2"]))
SIDE_ED = ((["e_o", "e_oT", "e_res", "e_norm"], []), (["e_T", "e_ffn"], ["d_stat", "d_norm", "d_T", "d_kv"]),
           ([], ["d_q", "d_rope", "d_qkT"]))
SIDE_D0 = ["d_moe", "d_n2"]
WINDOWS = ((0.3, 1.0), (0.0, 1.0), (0.0, 0.5), (0.3, 1.0))
COST = {"scores": 1.07, "turn": 0.43, "mix": 0.32, "a_T": 0.43, "a_kv": 1.71, "a_q": 0.86, "a_qkT": 0.43, "b_o": 0.43,
        "b_oT": 0.21, "b_res": 0.86, "b_T": 0.21, "b_qk": 1.71, "b_v": 0.86, "b_qkT": 0.43, "c_o": 0.43, "c_oT": 0.21,
        "c_gate": 0.86, "c_gT": 0.21, "c_out": 0.86, "c_x1T": 0.21, "c_logits": 0.86, "d_T": 0.43, "d_kv": 1.71,
        "d_q": 0.86, "d_qkT": 0.43, "e_o": 0.43, "e_oT": 0.21, "e_res": 0.86, "e_T": 0.21, "e_ffn": 0.86}
AFTER = {("pool", "a_stat"): 0.7, ("pool", "b_res"): 0.8, ("pool", "c_out"): 0.8,
         ("pool", "d_moe"): 1.1, ("pool", "d_n2"): 1.6, ("pool", "d_stat"): 0.7, ("pool", "e_res"): 0.8,
         ("act", "scores"): 0.9, ("act", "c_gate"): 0.45, ("act", "b_scale"): 0.7, ("pool", "e_ffn"): 0.6}


def interval(core, before, following, sides):
    steps = [("turn", core, 0), ("scores", core, 2), ("mix", before, 3), ("turn", core, 1), ("scores", core, 3),
             ("mix", core, 0), ("turn", core, 2), ("scores", following, 0), ("mix", core, 1), ("turn", core, 3),
             ("scores", following, 1), ("mix", core, 2)]
    placed = [((n + 0.5) / len(steps), s) for n, s in enumerate(steps) if s[1] is not None]
    for names, (start, end) in zip(sides, WINDOWS):
        placed += [(start + (end - start) * (k + 0.4) / len(names), s) for k, s in enumerate(names)]
    if following is not None:
        placed += [(0.5 + 0.1 * g, ("expand", following, g)) for g in range(G)]
    return [s for _, s in sorted(placed, key=lambda p: p[0])]


def order_of(engine, steps):
    if engine == "pe":
        return steps
    now, keyed, free = 0.0, [], {}
    for s in steps:
        start, cost = now, COST.get(s[0], 0.0)
        if s[1] is None:
            chain = (s[2][0], s[0] in SIDE_D0)
            start = max(now, free.get(chain, 0.0), free.get((s[2][0], True), 0.0) if s[0] == "d_stat" else 0.0)
            free[chain] = start + cost + 0.1 + max([t for (_, n), t in AFTER.items() if n == s[0]] + [0.0])
        if cost:
            now = start + cost
        keyed.append((start + cost + 0.05 + AFTER.get((engine, s[0]), 0.0), s))
    return [s for _, s in sorted(keyed, key=lambda k: k[0])]


def turn_steps(i, first, last, attns, between, extra=None):
    per = len(attns) * SLOTS

    def core_of(q):
        if (q < 0 and first) or (q >= per and last):
            return None
        turn = i + q // per
        return q % SLOTS, attns[q % per // SLOTS], turn

    def part(q, k):
        if q < 0 or (first and q < 0) or (last and q >= per + SLOTS):
            return []
        slot, turn, names = q % SLOTS, i + q // per, between[q % per // SLOTS][k]
        old = [] if (first and q < SLOTS) else names[0]
        new = [] if (last and q >= per) else names[1]
        return [(n, None, (slot, turn - 1)) for n in old] + [(n, None, (slot, turn)) for n in new]
    out = []
    for q in range(-3 if first else 0, per + 3 if last else per):
        sides = [part(q + 3 - k, k) for k in range(3)]
        if extra and not (last and q + 3 >= per):
            slot, turn = (q + 3) % SLOTS, i + (q + 3) // per
            sides.append([(n, None, (slot, turn)) for n in extra])
        out += interval(core_of(q), core_of(q - 1) if (q > 0 or not first) else None,
                        core_of(q + 1) if q >= -1 else None, sides)
    return out


def turn1(i, first, last):
    return turn_steps(i, first, last, (0, 1), (SIDE_CA, SIDE_B))


def turn3(i, first, last):
    return turn_steps(i, first, last, (2,), (SIDE_ED,), SIDE_D0)


def run_turns(eng, name, turn, step, chain=None, per=0):
    for body, turns in ((0, 1), (1, NI - 2), (2, 1)):
        if body == 1:
            with eng.Fori(1, NI - 1) as i:
                if chain:
                    chain.start(i - 1, per)
                for s in order_of(name, turn(i, False, False)):
                    step(*s)
                if chain:
                    chain.end(turns)
        else:
            i = 0 if body == 0 else NI - 1
            for s in order_of(name, turn(i, body == 0, body == 2)):
                step(*s)


def build(nc, t):
    ctx = ExitStack()
    with ctx:
        def sb(name, shape, dt=F32):
            return ctx.enter_context(nc.sbuf_tensor(name, shape, dt))

        def sem(name):
            return ctx.enter_context(nc.semaphore(name))

        ps = ctx.enter_context(nc.psum_tensor("ps", [P, 8, 512], F32))
        bank = [ps[:, n, :] for n in range(8)]
        SC = [bank[0], bank[1]]
        PT = [bank[2], bank[3]]
        M = bank[4:8]

        w_kv = sb("w_kv", [P, C, 2 * D])
        w_q = sb("w_q", [P, C, D])
        w_o = sb("w_o", [P, C, D])
        w_qk2 = sb("w_qk2", [P, C, 2 * D])
        w_v2 = sb("w_v2", [P, C, D])
        w_gate = sb("w_gate", [P, C, D])
        w_out = sb("w_out", [P, C, D])
        w_route = sb("w_route", [P, C, E])
        w1 = sb("w1", [P, C, E * F])
        w2 = sb("w2", [P, FC, E * D])
        w_mix = w_gate
        r_kv = sb("r_kv", [P, 2 * D])
        r_q = sb("r_q", [P, D])
        r_o = sb("r_o", [P, D])
        r_gate = sb("r_gate", [P, D])
        r_scale = sb("r_scale", [P, D])
        r_n1 = sb("r_n1", [P, 2, D])
        r_n2 = sb("r_n2", [P, 2, D])
        r_route = sb("r_route", [P, E])
        rope = sb("rope", [P, 2, D])
        r_mix = r_gate
        ident = sb("ident", [P, P])
        ident_bf = sb("ident_bf", [P, P], BF16)
        ones = sb("ones", [P, P])
        before_me = sb("before_me", [P, P])
        mask_bf = sb("mask_bf", [P, HG, P], BF16)
        headmask = sb("headmask", [P, P // HD])
        minus_half = sb("minus_half", [P, 1])
        x_all = sb("x_all", [P, B, D])
        x1_all = sb("x1_all", [P, B, D])
        logits = sb("logits", [P, B, E])
        wsum = sb("wsum", [P, B])
        kexp = sb("kexp", [P, 2, H, P])
        prob = sb("prob", [P, G, HG * P])
        pts = sb("pts", [P, 2, HG * P])
        b1_all = kexp[:, :, :, :].rearrange("p s h k -> p (s h k)")
        b2_all = prob[:, :, :].rearrange("p g k -> p (g k)")
        g_all = w1[:, 0, :].rearrange("p (b d) -> p b d", b=B)
        w_adapt = w1[:, 1, :].rearrange("p (k n) -> p k n", k=K_ADAPT)
        ARENA = 3584
        w2_all = w2[:, :, :].rearrange("p c n -> p (c n)")
        arena = [sb("arena0", [P, ARENA])[:, :], sb("arena1", [P, ARENA])[:, :],
                 w2_all[:, 0:ARENA], w2_all[:, ARENA:2 * ARENA]]

        def carve(a, sizes):
            out, off = [], 0
            for n in sizes:
                out.append(a[:, off:off + n])
                off += n
            assert off <= ARENA
            return out
        (xcur, c_in, xn, srcT, qk, vaug, qkT, gate, tmp) = map(list, zip(*[
            carve(arena[u], [D, D, D, 2 * D, 2 * D, H * VW, 2 * D, D, 2 * D]) for u in range(SLOTS)]))
        o_tok, ots = xn, qk
        oT = [s[:, D:2 * D] for s in srcT]
        vaug = [v.rearrange("p (h w) -> p h w", w=VW) for v in vaug]
        stats = [sb(f"stats{u}", [P, 6]) for u in range(XSLOTS)]
        mv = [sb(f"mv{u}", [P, 2]) for u in range(XSLOTS)]
        veps = [sb(f"veps{u}", [P, 1]) for u in range(XSLOTS)]
        rstd = [sb(f"rstd{u}", [P, 1]) for u in range(XSLOTS)]
        spare = [sb(f"spare{u}", [P, 1]) for u in range(XSLOTS)]
        rsum = [sb(f"rsum{u}", [P, H]) for u in range(SLOTS)]
        rowscale = [sb(f"rowscale{u}", [P, H]) for u in range(SLOTS)]
        rz = [sb(f"rz{u}", [P, H]) for u in range(SLOTS)]
        nbias = sb("nbias", [P, H])
        (xe, xeT, hid, hT, ye) = map(list, zip(*[
            carve(arena[u // 2][:, (u % 2) * (ARENA // 2):(u % 2 + 1) * (ARENA // 2)], [D, D, F, F, D])
            for u in range(XSLOTS)]))
        xe_rows = xe
        top8 = sb("top8", [P, B, 8])
        idx8 = sb("idx8", [P, B, 8], U32)
        chosen = sb("chosen", [P, B])
        onehot = sb("onehot", [P, B, E])
        tot = sb("tot", [P, B, E])
        base = sb("base", [P, B, E])
        iota_e = sb("iota_e", [P, E])
        iota_j = sb("iota_j", [P, B])
        iota_t = sb("iota_t", [P, TILES])
        iota_i = sb("iota_i", [P, 32], I32)
        ecount = sb("ecount", [P, E])
        etiles = sb("etiles", [P, E])
        estart = sb("estart", [P, E])
        eend = sb("eend", [P, E])
        ecmp = sb("ecmp", [P, E, B])
        tcmp = sb("tcmp", [P, TILES, E])
        texp = sb("texp", [P, TILES])
        texp_i = sb("texp_i", [P, TILES], I32)
        pos = sb("pos", [P, B])
        pos_u = sb("pos_u", [P, B], U32)
        small = sb("small", [P, 4, B])
        gcol = sb("gcol", [P, 2, E, FC])
        ecol = [sb(f"ecol{u}", [P, 2, FC]) for u in range(XSLOTS)]
        rs_row = sb("rs_row", [P, E])
        ers = [sb(f"ers{u}", [P, 1]) for u in range(XSLOTS)]
        ids_i = sb("ids_i", [P, K_ADAPT], I32)
        ids_f = sb("ids_f", [P, K_ADAPT])
        ids_n = sb("ids_n", [P, K_ADAPT])
        wts = sb("wts", [P, K_ADAPT])
        b_adapt = b2_all.rearrange("p (k d) -> p k d", k=K_ADAPT)

        sorted_x = nc.dram_tensor("sorted_x", [TILES * P, D], F32)
        sorted_y = nc.dram_tensor("sorted_y", [TILES * P, D], F32)

        x_loaded = [sem(f"x_loaded{u}") for u in range(SLOTS)]
        c_loaded = [sem(f"c_loaded{u}") for u in range(SLOTS)]
        weights0 = sem("weights0")
        weights2 = sem("weights2")
        down_loaded = sem("down_loaded")
        rows2 = sem("rows2")
        weights3 = sem("weights3")
        adapters = sem("adapters")
        consts = sem("consts")
        pool_own = sem("pool_own")
        dve_own = sem("dve_own")
        act_own = sem("act_own")
        ready = [sem(f"ready{u}") for u in range(SLOTS)]
        full = [sem(f"full{u}") for u in range(SLOTS)]
        var_ready = [sem(f"var_ready{u}") for u in range(SLOTS)]
        rstd_ready = [sem(f"rstd_ready{u}") for u in range(SLOTS)]
        kexp_ready = sem("kexp_ready")
        z_ready = [sem(f"z_ready{u}") for u in range(SLOTS)]
        ez_ready = [sem(f"ez_ready{u}") for u in range(SLOTS)]
        kept = [sem(f"kept{u}") for u in range(SLOTS)]
        scored = sem("scored")
        maxed = sem("maxed")
        exped = sem("exped")
        turned = sem("turned")
        copied = sem("copied")
        mixed = sem("mixed")
        y_done = [sem(f"y_done{u}") for u in range(SLOTS)]
        y_stored = [sem(f"y_stored{u}") for u in range(SLOTS)]
        zeroed = sem("zeroed")
        zero_ready = sem("zero_ready")
        route_a = sem("route_a")
        route_b = sem("route_b")
        route_c = sem("route_c")
        scattered = sem("scattered")
        gathered = sem("gathered")
        tile_in, tile_full, tile_ready, tile_var, tile_rstd, tile_cols, tile_out, tile_stored = (
            [sem(f"{name}{s}") for s in range(XSLOTS)]
            for name in ("tile_in", "tile_full", "tile_ready", "tile_var", "tile_rstd", "tile_cols", "tile_out", "tile_stored"))
        dve_own2 = sem("dve_own2")
        dve_own3 = sem("dve_own3")
        pool_own3 = sem("pool_own3")
        mix_ready = sem("mix_ready")

        normed = [sem(f"normed{u}") for u in range(SLOTS)]
        shifted = [sem(f"shifted{u}") for u in range(SLOTS)]
        row_norm = [(mv[u], veps[u], rstd[u], var_ready[u], rstd_ready[u]) for u in range(SLOTS)]
        block_norm = [(sb(f"mv_b{u}", [P, 2]), sb(f"veps_b{u}", [P, 1]), sb(f"rstd_b{u}", [P, 1]),
                       sem(f"var_ready_b{u}"), sem(f"rstd_ready_b{u}")) for u in range(SLOTS)]

        def slot_bn(i, u):
            return i * SLOTS + u

        def bc_row(name, n):
            return t[name].rearrange("(a n) -> a n", a=1).broadcast_to([P, n])

        def pool_steps(pool, own):
            def rstd_step(u, n, norm=row_norm):
                mv, veps, rstd, var_ready, rstd_ready = norm[u]
                pool.wait_ge(var_ready, n)
                pool.tensor_tensor(rstd[:, :], veps[:, :], minus_half[:, :], ALU.pow).then_inc(rstd_ready, 1)

            def expand(core, g):
                u, _, _ = core
                n = core_number(core)
                if g == 0:
                    pool.wait_ge(ready[u], product(core))
                    if not (isinstance(n, int) and n < 2):
                        pool.wait_ge(scored, groups(n, G - 1) - 2 * G)
                c, h0 = g // 2, (g % 2) * HG
                keys = qkT[u][:, D + c * P:D + (c + 1) * P]
                pool.tensor_tensor(kexp[:, u % 2, g * HG:(g + 1) * HG, :], keys.unsqueeze(1).broadcast_to([P, HG, P]),
                                   headmask[:, h0:h0 + HG].unsqueeze(2).broadcast_to([P, HG, P]),
                                   ALU.mult).then_inc(kexp_ready, 1)

            def keep(u, dst, src, b, value, saved):
                pool.wait_ge(ready[u], value)
                pool.tensor_copy(dst[:, bass.ds(b, 1), :].rearrange("p a d -> p (a d)"), src).then_inc(kept[u], 1)

            def step(name, core, st):
                if name == "expand":
                    return expand(core, st)
                if core is not None:
                    return
                u, i = st
                if name == "a_stat":
                    rstd_step(u, at(i, LN1, 0))
                elif name == "b_res":
                    rstd_step(u, at(i, LN1, 1))
                elif name == "b_T":
                    keep(u, x_all, xcur[u], slot_bn(i, u), at(i, STEP1, 8), None)
                elif name == "c_out":
                    rstd_step(u, at(i, LN1, 2))
                elif name == "c_x1T":
                    keep(u, x1_all, tmp[u][:, 0:D], slot_bn(i, u), at(i, STEP1, 18), None)
                elif name == "d_moe":
                    rstd_step(u, i + 1, block_norm)
                elif name == "d_n2":
                    x = tmp[u][:, 0:D]
                    pool.wait_ge(normed[u], i + 1)
                    own.mark(pool.tensor_tensor(x, x, r_n2[:, 0, :], ALU.mult))
                    own.join()
                    own.mark(pool.tensor_tensor(x, x, r_n2[:, 1, :], ALU.add))
                    own.join()
                    pool.tensor_tensor(x, x, x_all[:, bass.ds(slot_bn(i, u), 1), :].rearrange("p a d -> p (a d)"),
                                       ALU.add).then_inc(shifted[u], 1)
                elif name == "d_stat":
                    rstd_step(u, at(i, LN3, 0, NI * LN1))
                elif name == "e_res":
                    rstd_step(u, at(i, LN3, 1, NI * LN1))
                elif name == "e_ffn":
                    pool.wait_ge(y_done[u], i + 1)
                    pool.dma_start(t["out"][bass.ds(slot_bn(i, u), 1), :, :].rearrange("a p d -> p (a d)"),
                                   gate[u]).then_inc(y_stored[u], 16)
            return step

        def core_number(core):
            u, a, i = core
            if a == 2:
                return i * SLOTS + (u + 2 * SLOTS * NI)
            return i * (2 * SLOTS) + (a * SLOTS + u)

        def groups(n, g):
            return n * G + (g + 1)

        def product(core):
            u, a, i = core
            return at(i, STEP3, 4, NI * STEP1) if a == 2 else at(i, STEP1, 12 if a else 4)

        def pe_steps(pe):
            def transposes(dst, srcs):
                for n, s in enumerate(srcs):
                    last = pe.transpose(dst[:, n * P:(n + 1) * P], s, ident[:, :])
                return last

            def halves(x):
                return [x[:, c * P:(c + 1) * P] for c in range(x.shape[1] // P)]

            def project(dst, xT, w):
                for c in range(C):
                    last = pe.matmul(dst, xT[:, c * P:(c + 1) * P], w[:, c, :], start=(c == 0), stop=(c == C - 1))
                return last

            def core_step(name, core, g):
                u, a, i = core
                n = core_number(core)
                if name == "scores":
                    if g == 0:
                        pe.wait_ge(ready[u], product(core))
                    pe.wait_ge(kexp_ready, groups(n, g))
                    wait(pe, exped, groups(n, g) - 2)
                    if a != 1:
                        pe.matmul(SC[g % 2], ident_bf[:, :], mask_bf[:, :, :].rearrange("p h k -> p (h k)"),
                                  start=True, stop=False)
                    c = g // 2
                    pe.matmul(SC[g % 2], qkT[u][:, c * P:(c + 1) * P],
                              kexp[:, u % 2, g * HG:(g + 1) * HG, :].rearrange("p h k -> p (h k)"),
                              start=(a == 1), stop=True).then_inc(scored, 1)
                elif name == "turn":
                    pe.wait_ge(exped, groups(n, g))
                    wait(pe, copied, groups(n, g) - 2)
                    transposes(PT[g % 2], [prob[:, g, j * P:(j + 1) * P] for j in range(HG)]).then_inc(turned, 1)
                elif name == "mix":
                    pe.wait_ge(copied, groups(n, g))
                    for j in range(HG):
                        last = pe.matmul(M[u][VW * j:VW * (j + 1), g * P:(g + 1) * P], vaug[u][:, g * HG + j, :],
                                         pts[:, g % 2, j * P:(j + 1) * P], start=True, stop=True)
                    last.then_inc(mixed, 1)

            def step(name, core, st):
                if core is not None:
                    return core_step(name, core, st)
                u, i = st
                m = M[u]

                def start(k):
                    pe.wait_ge(ready[u], at(i, STEP1, k))

                def start3(k):
                    pe.wait_ge(ready[u], at(i, STEP3, k, NI * STEP1))
                if name == "a_T":
                    if isinstance(i, int) and i == 0 and u == 0:
                        pe.wait_ge(weights0, W0_ALL)
                    start(0)
                    pe.wait_ge(c_loaded[u], at(i, 16, 15))
                    transposes(m, halves(c_in[u]) + halves(xn[u])).then_inc(full[u], 1)
                elif name == "a_kv":
                    start(1)
                    project(m, srcT[u][:, 0:D], w_kv).then_inc(full[u], 1)
                elif name == "a_q":
                    start(2)
                    project(m[:, 0:D], srcT[u][:, D:2 * D], w_q).then_inc(full[u], 1)
                elif name == "a_qkT":
                    start(3)
                    transposes(m, halves(qk[u])).then_inc(full[u], 1)
                elif name == "b_o":
                    start(5)
                    transposes(m, halves(ots[u])).then_inc(full[u], 1)
                elif name == "b_oT":
                    start(6)
                    transposes(m, halves(o_tok[u])).then_inc(full[u], 1)
                elif name == "b_res":
                    start(7)
                    project(m[:, 0:D], oT[u], w_o).then_inc(full[u], 1)
                elif name == "b_T":
                    start(8)
                    transposes(m, halves(xn[u])).then_inc(full[u], 1)
                elif name == "b_qk":
                    start(9)
                    project(m, srcT[u][:, 0:D], w_qk2).then_inc(full[u], 1)
                elif name == "b_v":
                    start(10)
                    project(m[:, 0:D], srcT[u][:, 0:D], w_v2).then_inc(full[u], 1)
                elif name == "b_qkT":
                    start(11)
                    transposes(m, halves(qk[u])).then_inc(full[u], 1)
                elif name == "c_o":
                    start(13)
                    transposes(m, halves(ots[u])).then_inc(full[u], 1)
                elif name == "c_oT":
                    start(14)
                    transposes(m, halves(gate[u])).then_inc(full[u], 1)
                elif name == "c_gate":
                    start(15)
                    project(m[:, 0:D], oT[u], w_gate).then_inc(full[u], 1)
                elif name == "c_gT":
                    start(16)
                    transposes(m, halves(gate[u])).then_inc(full[u], 1)
                elif name == "c_out":
                    start(17)
                    project(m[:, 0:D], oT[u], w_out).then_inc(full[u], 1)
                elif name == "c_x1T":
                    start(18)
                    transposes(m, halves(tmp[u][:, 0:D])).then_inc(full[u], 1)
                elif name == "c_logits":
                    start(19)
                    project(m[:, 0:E], oT[u], w_route).then_inc(full[u], 1)
                elif name == "d_T":
                    start3(0)
                    pe.wait_ge(c_loaded[u], at(i, 16, 15, 16 * NI))
                    transposes(m, halves(c_in[u]) + halves(xn[u])).then_inc(full[u], 1)
                elif name == "d_kv":
                    start3(1)
                    project(m, srcT[u][:, 0:D], w_kv).then_inc(full[u], 1)
                elif name == "d_q":
                    start3(2)
                    project(m[:, 0:D], srcT[u][:, D:2 * D], w_q).then_inc(full[u], 1)
                elif name == "d_qkT":
                    start3(3)
                    transposes(m, halves(qk[u])).then_inc(full[u], 1)
                elif name == "e_o":
                    start3(5)
                    transposes(m, halves(ots[u])).then_inc(full[u], 1)
                elif name == "e_oT":
                    start3(6)
                    transposes(m, halves(o_tok[u])).then_inc(full[u], 1)
                elif name == "e_res":
                    start3(7)
                    project(m[:, 0:D], oT[u], w_o).then_inc(full[u], 1)
                elif name == "e_T":
                    start3(8)
                    transposes(m, halves(xn[u])).then_inc(full[u], 1)
                elif name == "e_ffn":
                    start3(9)
                    project(m[:, 0:D], srcT[u][:, 0:D], w_mix).then_inc(full[u], 1)
            return step

        def act_steps(act):
            def core_step(name, core, g):
                u, a, i = core
                n = core_number(core)
                if name == "scores":
                    act.wait_ge(maxed, groups(n, g))
                    wait(act, turned, groups(n, g) - G)
                    for j in range(HG):
                        h = g * HG + j
                        last = act.activation(prob[:, g, j * P:(j + 1) * P], SC[g % 2][:, j * P:(j + 1) * P], ACT.Exp,
                                              bias=nbias[:, h:h + 1],
                                              scale=rowscale[u][:, h:h + 1] if a == 1 else float(HD) ** -0.5)
                    last.then_inc(exped, 1)
                elif name == "turn":
                    act.wait_ge(turned, groups(n, g))
                    wait(act, mixed, groups(n, g) - 2)
                    act.copy(pts[:, g % 2, :], PT[g % 2]).then_inc(copied, 1)
                elif name == "mix" and g == G - 1:
                    act.wait_ge(mixed, groups(n, g))
                    act.copy(ots[u], M[u]).then_inc(ready[u], 1)

            def step(name, core, st):
                if core is not None:
                    return core_step(name, core, st)
                u, i = st
                m = M[u]

                def copy_out(dst, n, k, per=STEP1, base=0):
                    act.wait_ge(full[u], at(i, per - 2 if per == STEP1 else per - 1, k, base))
                    act.copy(dst, m[:, 0:n]).then_inc(ready[u], 1)
                if name == "a_T":
                    copy_out(srcT[u], 512, 0)
                elif name == "a_qkT":
                    copy_out(qkT[u], 512, 3)
                elif name == "b_oT":
                    copy_out(oT[u], D, 5)
                elif name == "b_T":
                    copy_out(srcT[u][:, 0:D], D, 7)
                elif name == "b_qk":
                    copy_out(qk[u], 512, 8)
                elif name == "b_v":
                    act.wait_ge(full[u], at(i, STEP1 - 2, 9))
                    act.copy(vaug[u][:, :, 0:HD], m[:, 0:D].rearrange("p (h w) -> p h w", w=HD)).then_inc(ready[u], 1)
                elif name == "b_scale":
                    act.wait_ge(z_ready[u], at(i, 2, 0))
                    act.activation(rz[u][:, :], rz[u][:, :], ACT.Exp, scale=-1.0).then_inc(ez_ready[u], 1)
                elif name == "b_qkT":
                    copy_out(qkT[u], 512, 10)
                elif name == "c_oT":
                    copy_out(oT[u], D, 12)
                elif name == "c_gate":
                    act.wait_ge(z_ready[u], at(i, 2, 1))
                    act.activation(tmp[u][:, D:2 * D], tmp[u][:, 0:D], ACT.Exp, scale=-1.0).then_inc(ez_ready[u], 1)
                elif name == "c_gT":
                    copy_out(oT[u], D, 14)
                elif name == "c_x1T":
                    copy_out(oT[u], D, 16)
                elif name == "d_T":
                    copy_out(srcT[u], 512, 0, STEP3, NI * (STEP1 - 2))
                elif name == "d_qkT":
                    copy_out(qkT[u], 512, 3, STEP3, NI * (STEP1 - 2))
                elif name == "e_oT":
                    copy_out(oT[u], D, 5, STEP3, NI * (STEP1 - 2))
                elif name == "e_T":
                    copy_out(srcT[u][:, 0:D], D, 7, STEP3, NI * (STEP1 - 2))
            return step

        def dve_steps(dve, own):
            def norm_stats(u, src, norm=row_norm):
                mv, veps, _, var_ready, _ = norm[u]
                own.mark(dve.bn_stats(stats[u][:, :], src))
                own.join_by(spare[u][:, :])
                own.mark(dve.bn_aggr(mv[:, :], stats[u][:, :]))
                own.join()
                dve.tensor_scalar(veps[:, :], mv[:, 1:2], EPS, None, ALU.add).then_inc(var_ready, 1)

            def normalize(u, dst, src, n, norm=row_norm):
                mv, _, rstd, _, rstd_ready = norm[u]
                dve.wait_ge(rstd_ready, n)
                return dve.tensor_scalar(dst, src, mv[:, 0:1], rstd[:, :], ALU.subtract, ALU.mult)

            def heads(x, w):
                return x.rearrange("p (h w) -> p h w", w=w)

            def sigmoid_of(dst, e, scale):
                own.mark(dve.tensor_scalar(e, e, 1.0, 1.0 / scale, ALU.add, ALU.mult))
                own.join()
                return dve.reciprocal(dst, e)

            def attention_out(u, dst):
                o = heads(M[u], VW)
                own.mark(dve.reciprocal(rsum[u][:, :], o[:, :, HD]))
                own.join()
                dve.tensor_tensor(heads(dst, HD), o[:, :, 0:HD],
                                  rsum[u][:, :].unsqueeze(2).broadcast_to([P, H, HD]), ALU.mult).then_inc(ready[u], 1)

            def core_step(name, core, g):
                u, a, i = core
                n = core_number(core)
                if name == "scores":
                    dve.wait_ge(scored, groups(n, g))
                    hs = slice(g * HG, (g + 1) * HG)
                    own.mark(dve.tensor_reduce(nbias[:, hs], SC[g % 2].rearrange("p (h k) -> p h k", h=HG), AX.X, ALU.max, negate=True))
                    own.join()
                    if a == 1:
                        dve.tensor_tensor(nbias[:, hs], nbias[:, hs], rowscale[u][:, hs], ALU.mult).then_inc(maxed, 1)
                    else:
                        dve.tensor_scalar(nbias[:, hs], nbias[:, hs], float(HD) ** -0.5, None, ALU.mult).then_inc(maxed, 1)

            def step(name, core, st):
                if core is not None:
                    return core_step(name, core, st)
                u, i = st
                m = M[u]

                def taken(k):
                    dve.wait_ge(full[u], at(i, STEP1 - 2, k))

                def taken3(k):
                    dve.wait_ge(full[u], at(i, STEP3 - 1, k, NI * (STEP1 - 2)))
                if name == "a_stat":
                    dve.wait_ge(x_loaded[u], at(i, 16, 15))
                    norm_stats(u, xcur[u])
                elif name == "a_norm":
                    normalize(u, xn[u], xcur[u], at(i, LN1, 0)).then_inc(ready[u], 1)
                elif name == "a_kv":
                    taken(1)
                    own.mark(dve.tensor_tensor(xcur[u], xcur[u], r_o[:, :], ALU.add))
                    own.mark(dve.tensor_tensor(qk[u][:, D:2 * D], m[:, 0:D], r_kv[:, 0:D], ALU.add))
                    dve.tensor_tensor(vaug[u][:, :, 0:HD], heads(m[:, D:2 * D], HD), heads(r_kv[:, D:2 * D], HD), ALU.add).then_inc(ready[u], 1)
                elif name == "a_q":
                    taken(2)
                    dve.tensor_tensor(qk[u][:, 0:D], m[:, 0:D], r_q[:, :], ALU.add).then_inc(ready[u], 1)
                elif name == "b_o":
                    taken(4)
                    attention_out(u, o_tok[u])
                elif name == "b_res":
                    taken(6)
                    own.join()
                    own.mark(dve.tensor_tensor(xcur[u], m[:, 0:D], xcur[u], ALU.add))
                    own.join()
                    norm_stats(u, xcur[u])
                elif name == "b_norm":
                    normalize(u, xn[u], xcur[u], at(i, LN1, 1)).then_inc(ready[u], 1)
                elif name == "b_scale":
                    dve.wait_ge(ready[u], at(i, STEP1, 10))
                    if not (isinstance(i, int) and i == 0):
                        dve.wait_ge(kept[u], at(i, 2, 1, -2))
                    own.mark(dve.tensor_tensor(tmp[u][:, 0:D], qk[u][:, 0:D], r_scale[:, :], ALU.mult))
                    own.join()
                    dve.tensor_reduce(rz[u][:, :], heads(tmp[u][:, 0:D], HD), AX.X, ALU.add).then_inc(z_ready[u], 1)
                elif name == "b_scale2":
                    dve.wait_ge(ez_ready[u], at(i, 2, 0))
                    own.mark(sigmoid_of(rowscale[u][:, :], rz[u][:, :], 2.0 * float(HD) ** -0.5))
                    own.join()
                elif name == "c_o":
                    taken(11)
                    attention_out(u, gate[u])
                elif name == "c_gate":
                    taken(13)
                    dve.tensor_tensor(tmp[u][:, 0:D], m[:, 0:D], r_gate[:, :], ALU.add).then_inc(z_ready[u], 1)
                elif name == "c_gate2":
                    dve.wait_ge(ez_ready[u], at(i, 2, 1))
                    own.mark(sigmoid_of(tmp[u][:, 0:D], tmp[u][:, D:2 * D], 1.0))
                    own.join()
                    dve.tensor_tensor(gate[u], gate[u], tmp[u][:, 0:D], ALU.mult).then_inc(ready[u], 1)
                elif name == "c_out":
                    taken(15)
                    own.mark(dve.tensor_tensor(tmp[u][:, D:2 * D], m[:, 0:D], xn[u], ALU.add))
                    own.join()
                    norm_stats(u, tmp[u][:, D:2 * D])
                elif name == "c_norm":
                    own.mark(normalize(u, tmp[u][:, 0:D], tmp[u][:, D:2 * D], at(i, LN1, 2)))
                    own.join()
                    own.mark(dve.tensor_tensor(tmp[u][:, 0:D], tmp[u][:, 0:D], r_n1[:, 0, :], ALU.mult))
                    own.join()
                    dve.tensor_tensor(tmp[u][:, 0:D], tmp[u][:, 0:D], r_n1[:, 1, :], ALU.add).then_inc(ready[u], 1)
                elif name == "c_logits":
                    taken(17)
                    own.mark(dve.tensor_tensor(logits[:, bass.ds(slot_bn(i, u), 1), :].rearrange("p a e -> p (a e)"),
                                               m[:, 0:E], r_route[:, :], ALU.add))
                elif name == "d_moe":
                    b = slot_bn(i, u)
                    row = lambda a: a[:, bass.ds(b, 1), :].rearrange("p a d -> p (a d)")
                    own.mark(dve.scalar_tensor_tensor(out=tmp[u][:, 0:D], in0=row(g_all), scalar=wsum[:, bass.ds(b, 1)],
                                                      in1=row(x1_all), op0=ALU.mult, op1=ALU.add))
                    own.join()
                    norm_stats(u, tmp[u][:, 0:D], block_norm)
                elif name == "d_n2":
                    normalize(u, tmp[u][:, 0:D], tmp[u][:, 0:D], i + 1, block_norm).then_inc(normed[u], 1)
                elif name == "d_stat":
                    dve.wait_ge(shifted[u], i + 1)
                    norm_stats(u, tmp[u][:, 0:D])
                elif name == "d_norm":
                    normalize(u, xn[u], tmp[u][:, 0:D], at(i, LN3, 0, NI * LN1)).then_inc(ready[u], 1)
                elif name == "d_kv":
                    taken3(1)
                    own.mark(dve.tensor_tensor(xcur[u], tmp[u][:, 0:D], r_o[:, :], ALU.add))
                    own.mark(dve.tensor_tensor(qk[u][:, D:2 * D], m[:, 0:D], r_kv[:, 0:D], ALU.add))
                    dve.tensor_tensor(vaug[u][:, :, 0:HD], heads(m[:, D:2 * D], HD), heads(r_kv[:, D:2 * D], HD), ALU.add).then_inc(ready[u], 1)
                elif name == "d_q":
                    taken3(2)
                    own.mark(dve.tensor_tensor(qk[u][:, 0:D], m[:, 0:D], r_q[:, :], ALU.add))
                    own.join()
                elif name == "d_rope":
                    both = qk[u].rearrange("p (a d) -> p a d", a=2)
                    hh = HD // 2
                    for a in range(2):
                        rot = heads(tmp[u][:, a * D:(a + 1) * D], HD)
                        x = heads(qk[u][:, a * D:(a + 1) * D], HD)
                        sn = heads(rope[:, 1, :], HD)
                        own.mark(dve.tensor_tensor(rot[:, :, 0:hh], x[:, :, hh:HD], sn[:, :, 0:hh], ALU.mult))
                        own.mark(dve.tensor_tensor(rot[:, :, hh:HD], x[:, :, 0:hh], sn[:, :, hh:HD], ALU.mult))
                    own.join()
                    own.mark(dve.tensor_tensor(both, both, rope[:, 0, :].unsqueeze(1).broadcast_to([P, 2, D]), ALU.mult))
                    own.join()
                    dve.tensor_tensor(qk[u], qk[u], tmp[u], ALU.add).then_inc(ready[u], 1)
                elif name == "e_o":
                    taken3(4)
                    attention_out(u, o_tok[u])
                elif name == "e_res":
                    taken3(6)
                    own.join()
                    own.mark(dve.tensor_tensor(xcur[u], m[:, 0:D], xcur[u], ALU.add))
                    own.join()
                    norm_stats(u, xcur[u])
                elif name == "e_norm":
                    normalize(u, xn[u], xcur[u], at(i, LN3, 1, NI * LN1)).then_inc(ready[u], 1)
                elif name == "e_ffn":
                    dve.wait_ge(ready[u], at(i, STEP3, 8, NI * STEP1))
                    own.mark(dve.tensor_tensor(xcur[u], xcur[u], r_mix[:, :], ALU.add))
                    own.join()
                    taken3(8)
                    wait(dve, y_stored[u], at(i, 16, -1))
                    dve.tensor_tensor(gate[u], m[:, 0:D], xcur[u], ALU.add).then_inc(y_done[u], 1)
            return step

        W0_ALL = 16 * 16
        with nc.Block() as block:

            @block.sync
            def _(sp):
                def load_rows(u, i):
                    if isinstance(i, int) and i == 0:
                        pass
                    else:
                        sp.wait_ge(kept[u], at(i, 2, 0, -2))
                    b = slot_bn(i, u)
                    sp.dma_start(xcur[u], t["x"][bass.ds(b, 1), :, :].rearrange("a p d -> p (a d)")).then_inc(x_loaded[u], 16)
                    sp.dma_start(c_in[u], t["ctx"][bass.ds(b, 1), :, :].rearrange("a p d -> p (a d)")).then_inc(c_loaded[u], 16)

                load_rows(0, 0)
                sp.dma_start(w_kv[:, :, :], t["w_kv"].rearrange("(c p) n -> p c n", p=P)).then_inc(weights0, 16)
                sp.dma_start(r_kv[:, :], bc_row("r_kv", 2 * D)).then_inc(weights0, 16)
                sp.dma_start(w_q[:, :, :], t["w_q"].rearrange("(c p) n -> p c n", p=P)).then_inc(weights0, 16)
                sp.dma_start(r_q[:, :], bc_row("r_q", D)).then_inc(weights0, 16)
                for u in range(1, SLOTS):
                    load_rows(u, 0)
                for dst, name in ((w_o, "w_o"), (w_qk2, "w_qk2"), (w_v2, "w_v2"), (w_gate, "w_gate"),
                                  (w_out, "w_out"), (w_route, "w_route")):
                    sp.dma_start(dst[:, :, :], t[name].rearrange("(c p) n -> p c n", p=P)).then_inc(weights0, 16)
                for dst, name, n in ((r_o, "r_o", D), (r_gate, "r_gate", D), (r_scale, "r_scale", D),
                                     (r_route, "r_route", E)):
                    sp.dma_start(dst[:, :], bc_row(name, n)).then_inc(weights0, 16)
                sp.dma_start(r_n1[:, :, :].rearrange("p a d -> p (a d)"), bc_row("r_n1", 2 * D)).then_inc(weights0, 16)
                sp.dma_start(r_n2[:, :, :].rearrange("p a d -> p (a d)"), bc_row("r_n2", 2 * D)).then_inc(weights0, 16)
                sp.dma_start(ids_i[:, :], t["ids"].rearrange("(a n) -> a n", a=1).broadcast_to([P, K_ADAPT])).then_inc(weights2, 16)
                sp.dma_start(wts[:, :], bc_row("wts", K_ADAPT)).then_inc(weights2, 16)
                sp.dma_start(rs_row[:, :], bc_row("res_scale", E)).then_inc(weights2, 16)
                sp.dma_start(rope[:, :, :], t["rope"]).then_inc(weights2, 16)
                sp.dma_start(gcol[:, :, :, :], t["ln_gb"]).then_inc(weights2, 16)
                for e in range(E):
                    sp.dma_start(w1[:, :, e * F:(e + 1) * F], t["w1"][e].rearrange("(c p) n -> p c n", p=P)).then_inc(weights2, 16)
                sp.wait_ge(zero_ready, 1)
                for n in range(TILES):
                    sp.dma_start(sorted_x[n * P:(n + 1) * P, :].rearrange("p (a n) -> p a n", a=2), top8[:, :, :].rearrange("p b e -> p (b e)")[:, 0:P].unsqueeze(1).broadcast_to([P, 2, P])).then_inc(zeroed, 16)
                with sp.Fori(1, NI) as i:
                    for u in range(SLOTS):
                        load_rows(u, i)
                for u in range(SLOTS):
                    sp.wait_ge(ready[u], at(NI - 1, STEP1, 17))
                sp.wait_ge(turned, 2 * SLOTS * NI * G)
                sp.dma_start(b1_all, bc_row("b1", E * F)).then_inc(rows2, 16)
                sp.dma_start(b2_all, bc_row("b2", E * D)).then_inc(rows2, 16)
                for u in range(2, SLOTS):
                    sp.wait_ge(full[u], NI * (STEP1 - 2))
                    sp.wait_ge(kept[u], 2 * NI)
                for e in range(E):
                    sp.dma_start(w2[:, :, e * D:(e + 1) * D], t["w2"][e].rearrange("(c p) n -> p c n", p=P)).then_inc(down_loaded, 16)
                for dst, name in ((w_kv, "w_kv3"), (w_q, "w_q3"), (w_o, "w_o3")):
                    sp.dma_start(dst[:, :, :], t[name].rearrange("(c p) n -> p c n", p=P)).then_inc(weights3, 16)
                for dst, name, n in ((r_kv, "r_kv3", 2 * D), (r_q, "r_q3", D), (r_o, "r_o3", D)):
                    sp.dma_start(dst[:, :], bc_row(name, n)).then_inc(weights3, 16)

            @block.gpsimd
            def _(pool):
                own = Chain(pool, pool_own)
                own.mark(pool.memset(ones[:, :], 1.0))
                own.mark(pool.memset(minus_half[:, :], -0.5))
                own.mark(pool.memset(mask_bf[:, :, :], 0.0))
                own.mark(pool.iota(iota_i[:, 0:32], pattern=[[1, 32]], base=0, channel_multiplier=0))
                own.join()
                own.mark(pool.affine_select(out=ident[:, :], in_=ones[:, :], compare_op=ALU.is_equal, fill=0.0,
                                            base=0, pattern=[[-1, P]], channel_multiplier=1))
                own.mark(pool.affine_select(out=ident_bf[:, :], in_=ones[:, :], compare_op=ALU.is_equal, fill=0.0,
                                            base=0, pattern=[[-1, P]], channel_multiplier=1))
                own.mark(pool.affine_select(out=before_me[:, :], in_=ones[:, :], compare_op=ALU.is_gt, fill=0.0,
                                            base=0, pattern=[[1, P]], channel_multiplier=-1))
                own.mark(pool.affine_select(out=mask_bf[:, :, :], in_=mask_bf[:, :, :], compare_op=ALU.is_ge, fill=MASKED,
                                            base=0, pattern=[[0, HG], [-1, P]], channel_multiplier=1))
                own.mark(pool.affine_select(out=headmask[:, :], in_=ones[:, 0:P // HD], compare_op=ALU.is_ge, fill=0.0,
                                            base=0, pattern=[[-HD, P // HD]], channel_multiplier=1))
                own.join()
                own.mark(pool.affine_select(out=headmask[:, :], in_=headmask[:, :], compare_op=ALU.is_ge, fill=0.0,
                                            base=HD - 1, pattern=[[HD, P // HD]], channel_multiplier=-1))
                own.mark(pool.tensor_copy(iota_e[:, :], iota_i[:, 0:E]))
                own.mark(pool.tensor_copy(iota_t[:, :], iota_i[:, 0:TILES]))
                own.mark(pool.tensor_scalar(iota_j[:, :], iota_i[:, 0:B], float(P), None, ALU.mult))
                own.join()
                for u in range(SLOTS):
                    own.mark(pool.memset(vaug[u], 0.0))
                own.join()
                for u in range(SLOTS):
                    pool.memset(vaug[u][:, :, HD:HD + 1], 1.0).then_inc(consts, 1)

                run_turns(pool, "pool", turn1, pool_steps(pool, own), own, 0)

                pool.wait_ge(route_c, 1)
                pool.wait_ge(zeroed, 16 * TILES)
                for u in range(SLOTS):
                    pool.wait_ge(kept[u], 2 * NI)
                for b in range(B):
                    pool.indirect_dma_start(out=sorted_x[:, :], out_offset=bass.IndirectOffsetOnAxis(ap=pos_u[:, b:b + 1], axis=0),
                                            in_=x1_all[:, b, :], in_offset=None).then_inc(scattered, 16)
                pool.wait_ge(scattered, 16 * B)

            @block.tensor
            def _(pe):
                pe.wait_ge(consts, SLOTS)
                run_turns(pe, "pe", turn1, pe_steps(pe))
                pe.wait_ge(route_a, 1)
                pe.matmul(bank[0][:, 0:P], before_me[:, :], onehot[:, :, :].rearrange("p b e -> p (b e)"), start=True, stop=True).then_inc(route_b, 1)
                pe.matmul(bank[1][:, 0:P], ones[:, :], onehot[:, :, :].rearrange("p b e -> p (b e)"), start=True, stop=True).then_inc(route_b, 1)

            @block.scalar
            def _(act):
                run_turns(act, "act", turn1, act_steps(act))
                act.wait_ge(z_ready[0], 2 * NI + 1)
                act.activation(small[:, 1, :], small[:, 0, :], ACT.Exp).then_inc(ez_ready[0], 1)

            @block.vector
            def _(dve):
                dve.memset(top8[:, :, :], 0.0).then_inc(zero_ready, 1)
                dve.wait_ge(weights0, W0_ALL)
                dve.wait_ge(consts, SLOTS)
                own = Chain(dve, dve_own)
                run_turns(dve, "dve", turn1, dve_steps(dve, own), own, PER_TURN1)

                dve.wait_ge(zeroed, 16 * TILES)
                own.join()
                own.mark(dve.tensor_scalar(ids_f[:, :], ids_i[:, :], 0.0, None, ALU.add))
                for b in range(B):
                    own.mark(dve.max(top8[:, b, :], logits[:, b, :]))
                own.join()
                for b in range(B):
                    own.mark(dve.max_index(idx8[:, b, :], top8[:, b, :], logits[:, b, :]))
                dve.tensor_tensor(small[:, 0, :], top8[:, :, 1], top8[:, :, 0], ALU.subtract).then_inc(z_ready[0], 1)
                own.join()
                own.mark(dve.tensor_tensor(chosen[:, :], idx8[:, :, 0], idx8[:, :, 1], ALU.max))
                own.join()
                dve.tensor_tensor(onehot[:, :, :], chosen[:, :].unsqueeze(2).broadcast_to([P, B, E]),
                                  iota_e[:, :].unsqueeze(1).broadcast_to([P, B, E]), ALU.is_equal).then_inc(route_a, 1)
                dve.wait_ge(ez_ready[0], 2 * NI + 1)
                own.mark(dve.tensor_scalar(small[:, 2, :], small[:, 1, :], 1.0, None, ALU.add))
                own.join()
                own.mark(dve.reciprocal(small[:, 3, :], small[:, 2, :]))
                own.join()
                own.mark(dve.tensor_tensor(small[:, 1, :], small[:, 1, :], small[:, 3, :], ALU.mult))
                own.join()
                own.mark(dve.tensor_tensor(wsum[:, :], small[:, 1, :], small[:, 3, :], ALU.add))
                dve.wait_ge(route_b, 2)
                own.mark(dve.tensor_copy(tot[:, :, :].rearrange("p b e -> p (b e)"), bank[1][:, 0:P]))
                own.mark(dve.memset(base[:, 0, :], 0.0))
                own.join()
                for b in range(1, B):
                    own.mark(dve.tensor_tensor(base[:, b, :], base[:, b - 1, :], tot[:, b - 1, :], ALU.add))
                    own.join()
                own.mark(dve.tensor_tensor(ecount[:, :], base[:, B - 1, :], tot[:, B - 1, :], ALU.add))
                own.join()
                own.mark(dve.tensor_tensor(ecmp[:, :, :], ecount[:, :].unsqueeze(2).broadcast_to([P, E, B]),
                                           iota_j[:, :].unsqueeze(1).broadcast_to([P, E, B]), ALU.is_gt))
                own.join()
                own.mark(dve.tensor_reduce(etiles[:, :], ecmp[:, :, :], AX.X, ALU.add))
                own.mark(dve.memset(estart[:, 0:1], 0.0))
                own.join()
                for e in range(1, E):
                    own.mark(dve.tensor_tensor(estart[:, e:e + 1], estart[:, e - 1:e], etiles[:, e - 1:e], ALU.add))
                    own.join()
                own.mark(dve.tensor_tensor(eend[:, :], estart[:, :], etiles[:, :], ALU.add))
                own.mark(dve.scalar_tensor_tensor(out=base[:, :, :], in0=estart[:, :].unsqueeze(1).broadcast_to([P, B, E]), scalar=float(P),
                                                  in1=base[:, :, :], op0=ALU.mult, op1=ALU.add))
                own.join()
                own.mark(dve.tensor_tensor(base[:, :, :], base[:, :, :],
                                           bank[0][:, 0:P].rearrange("p (b e) -> p b e", e=E), ALU.add))
                own.mark(dve.tensor_tensor(tcmp[:, :, :], iota_t[:, :].unsqueeze(2).broadcast_to([P, TILES, E]),
                                           eend[:, :].unsqueeze(1).broadcast_to([P, TILES, E]), ALU.is_ge))
                own.join()
                own.mark(dve.tensor_tensor(base[:, :, :], base[:, :, :], onehot[:, :, :], ALU.mult))
                own.mark(dve.tensor_reduce(texp[:, :], tcmp[:, :, :], AX.X, ALU.add))
                own.join()
                own.mark(dve.tensor_reduce(pos[:, :], base[:, :, :], AX.X, ALU.add))
                own.mark(dve.tensor_scalar(texp_i[:, :], texp[:, :], float(E - 1), None, ALU.min))
                own.join()
                dve.tensor_copy(pos_u[:, :], pos[:, :]).then_inc(route_c, 1)
                dve.wait_ge(weights2, 16)
                own.mark(dve.tensor_scalar(ids_n[:, :], ids_f[:, :], 0.0, float(ADAPTERS), ALU.is_lt, ALU.mult))
                own.join()
                own.mark(dve.tensor_tensor(ids_f[:, :], ids_f[:, :], ids_n[:, :], ALU.add))
                own.join()
                dve.tensor_scalar(ids_i[:, :], ids_f[:, :], 0.0, float(ADAPTERS - 1), ALU.max, ALU.min).then_inc(route_c, 1)


        TURNS2, REST2 = TILES // XSLOTS, TILES % XSLOTS

        def run_tiles(eng, turn):
            turn(0, XSLOTS)
            with eng.Fori(1, TURNS2) as i:
                turn(i, XSLOTS)
            turn(TURNS2, REST2)

        with nc.Block() as block:
            @block.sync
            def _(sp):
                def turn(i, n):
                    for s in range(n):
                        wait(sp, tile_out[s], i)
                        sp.dma_start(xe[s], sorted_x[bass.ds((i * XSLOTS + s) * P, P), :]).then_inc(tile_in[s], 16)
                run_tiles(sp, turn)

            @block.gpsimd
            def _(pool):
                def turn(i, n):
                    for s in range(n):
                        pool.wait_ge(tile_var[s], i + 1)
                        pool.tensor_tensor(rstd[s][:, :], veps[s][:, :], minus_half[:, :], ALU.pow).then_inc(tile_rstd[s], 1)
                    for s in range(n):
                        pool.wait_ge(tile_out[s], i + 1)
                        pool.dma_start(sorted_y[bass.ds((i * XSLOTS + s) * P, P), :], ye[s]).then_inc(tile_stored[s], 16)
                run_tiles(pool, turn)
                for s in range(XSLOTS):
                    pool.wait_ge(tile_stored[s], 16 * (TURNS2 + (s < REST2)))
                for b in range(B):
                    pool.indirect_dma_start(out=g_all[:, b, :], out_offset=None, in_=sorted_y[:, :],
                                            in_offset=bass.IndirectOffsetOnAxis(ap=pos_u[:, b:b + 1], axis=0)).then_inc(gathered, 16)
                pool.wait_ge(gathered, 16 * B)

            @block.tensor
            def _(pe):
                pe.wait_ge(weights2, 16 * (5 + E))

                def turn(i, n):
                    for s in range(n):
                        pe.wait_ge(tile_in[s], at(i, 16, 15))
                        wait(pe, tile_out[s], i)
                        for c in range(C):
                            last = pe.transpose(bank[s][:, c * P:(c + 1) * P], xe[s][:, c * P:(c + 1) * P], ident[:, :])
                        last.then_inc(tile_full[s], 1)
                    for s in range(n):
                        e = pe.value_load(texp_i[0:1, bass.ds(i * XSLOTS + s, 1)], min_val=0, max_val=E - 1)
                        pe.wait_ge(tile_ready[s], at(i, 3, 0))
                        for c in range(C):
                            last = pe.matmul(bank[s], xeT[s][:, c * P:(c + 1) * P], w1[:, c, bass.ds(e * F, F)],
                                             start=(c == 0), stop=(c == C - 1))
                        last.then_inc(tile_full[s], 1)
                    for s in range(n):
                        pe.wait_ge(tile_ready[s], at(i, 3, 1))
                        for c in range(FC):
                            last = pe.transpose(bank[s][:, c * P:(c + 1) * P], hid[s][:, c * P:(c + 1) * P], ident[:, :])
                        last.then_inc(tile_full[s], 1)
                    if isinstance(i, int) and i == 0:
                        pe.wait_ge(down_loaded, 16 * E)
                    for s in range(n):
                        e = pe.value_load(texp_i[0:1, bass.ds(i * XSLOTS + s, 1)], min_val=0, max_val=E - 1)
                        pe.wait_ge(tile_ready[s], at(i, 3, 2))
                        for c in range(FC):
                            last = pe.matmul(bank[s][:, 0:D], hT[s][:, c * P:(c + 1) * P], w2[:, c, bass.ds(e * D, D)],
                                             start=(c == 0), stop=(c == FC - 1))
                        last.then_inc(tile_full[s], 1)
                run_tiles(pe, turn)

            @block.scalar
            def _(act):
                def turn(i, n):
                    for s in range(n):
                        act.wait_ge(tile_full[s], at(i, 4, 0))
                        act.copy(xeT[s], bank[s][:, 0:D]).then_inc(tile_ready[s], 1)
                    for s in range(n):
                        act.wait_ge(tile_full[s], at(i, 4, 2))
                        act.wait_ge(tile_cols[s], i + 1)
                        for c in range(FC):
                            last = act.activation(hT[s][:, c * P:(c + 1) * P], bank[s][:, c * P:(c + 1) * P], ACT.Gelu,
                                                  bias=ecol[s][:, 1, c:c + 1], scale=ecol[s][:, 0, c:c + 1])
                        last.then_inc(tile_ready[s], 1)
                run_tiles(act, turn)

            @block.vector
            def _(dve):
                dve.wait_ge(weights2, 16 * (5 + E))
                dve.wait_ge(rows2, 32)
                own = Chain(dve, dve_own2)

                def turn(i, n):
                    for s in range(n):
                        e = dve.value_load(texp_i[0:1, bass.ds(i * XSLOTS + s, 1)], min_val=0, max_val=E - 1)
                        dve.wait_ge(tile_full[s], at(i, 4, 1))
                        own.mark(dve.tensor_tensor(hid[s], bank[s], b1_all[:, bass.ds(e * F, F)], ALU.add))
                        own.join()
                        own.mark(dve.bn_stats(stats[s][:, :], hid[s]))
                        own.join_by(spare[s][:, :])
                        own.mark(dve.bn_aggr(mv[s][:, :], stats[s][:, :]))
                        own.join()
                        dve.tensor_scalar(veps[s][:, :], mv[s][:, 1:2], EPS, None, ALU.add).then_inc(tile_var[s], 1)
                        own.mark(dve.tensor_copy(ers[s][:, :], rs_row[:, bass.ds(e, 1)]))
                        dve.tensor_copy(ecol[s][:, :, :], gcol[:, :, bass.ds(e, 1), :].rearrange("p a o c -> p a (o c)")).then_inc(tile_cols[s], 1)
                    for s in range(n):
                        dve.wait_ge(tile_rstd[s], i + 1)
                        dve.tensor_scalar(hid[s], hid[s], mv[s][:, 0:1], rstd[s][:, :], ALU.subtract, ALU.mult).then_inc(tile_ready[s], 1)
                    for s in range(n):
                        e = dve.value_load(texp_i[0:1, bass.ds(i * XSLOTS + s, 1)], min_val=0, max_val=E - 1)
                        dve.wait_ge(tile_full[s], at(i, 4, 3))
                        wait(dve, tile_stored[s], at(i, 16, -1))
                        own.mark(dve.tensor_tensor(ye[s], bank[s][:, 0:D], b2_all[:, bass.ds(e * D, D)], ALU.add))
                        own.join()
                        dve.scalar_tensor_tensor(out=ye[s], in0=ye[s], scalar=ers[s][:, 0:1], in1=xe[s],
                                                 op0=ALU.mult, op1=ALU.add).then_inc(tile_out[s], 1)
                turn(0, XSLOTS)
                with dve.Fori(1, TURNS2) as i:
                    own.start(i - 1, XSLOTS * 6)
                    turn(i, XSLOTS)
                    own.end(TURNS2 - 1)
                turn(TURNS2, REST2)

        with nc.Block() as block:
            @block.sync
            def _(sp):
                def load_context(u, i):
                    if not (isinstance(i, int) and i == 0):
                        sp.wait_ge(ready[u], at(i, STEP3, 1, NI * STEP1 - STEP3))
                    sp.dma_start(c_in[u], t["ctx"][bass.ds(slot_bn(i, u), 1), :, :].rearrange("a p d -> p (a d)")).then_inc(c_loaded[u], 16)

                for u in range(SLOTS):
                    load_context(u, 0)
                for k in range(K_ADAPT):
                    a = sp.value_load(ids_i[0:1, k:k + 1], min_val=0, max_val=ADAPTERS - 1)
                    sp.dma_start(w_adapt[:, k, :].rearrange("p (c n) -> p c n", c=C),
                                 t["w_adapt"][bass.ds(a, 1), :, :].rearrange("o (c p) n -> p (o c) n", p=P)).then_inc(adapters, 16)
                    sp.dma_start(b_adapt[:, k, :], t["b_adapt"][bass.ds(a, 1), :].broadcast_to([P, D])).then_inc(adapters, 16)
                with sp.Fori(1, NI) as i:
                    for u in range(SLOTS):
                        load_context(u, i)
                for u in range(SLOTS):
                    sp.wait_ge(y_stored[u], 16 * NI)

            @block.gpsimd
            def _(pool):
                own = Chain(pool, pool_own3)
                for u in range(SLOTS):
                    own.mark(pool.memset(vaug[u], 0.0))
                own.join()
                for u in range(SLOTS):
                    pool.memset(vaug[u][:, :, HD:HD + 1], 1.0).then_inc(consts, 1)
                own.join()
                run_turns(pool, "pool", turn3, pool_steps(pool, own), own, 2 * SLOTS)

            @block.tensor
            def _(pe):
                pe.wait_ge(weights3, 16 * 6)
                pe.wait_ge(mix_ready, 1)
                run_turns(pe, "pe", turn3, pe_steps(pe))

            @block.scalar
            def _(act):
                run_turns(act, "act", turn3, act_steps(act))

            @block.vector
            def _(dve):
                dve.wait_ge(weights3, 16 * 6)
                own = Chain(dve, dve_own3)
                dve.wait_ge(adapters, 2 * 16 * K_ADAPT)
                mix = w_mix[:, :, :].rearrange("p c n -> p (c n)")
                for k in range(K_ADAPT):
                    if k:
                        own.join()
                    if k == 0:
                        own.mark(dve.tensor_scalar(mix, w_adapt[:, 0, :], wts[:, 0:1], None, ALU.mult))
                        own.mark(dve.tensor_scalar(r_mix[:, :], b_adapt[:, 0, :], wts[:, 0:1], None, ALU.mult))
                        continue
                    ins = dve.scalar_tensor_tensor(out=mix, in0=w_adapt[:, k, :], scalar=wts[:, k:k + 1], in1=mix,
                                                   op0=ALU.mult, op1=ALU.add)
                    if k == K_ADAPT - 1:
                        ins.then_inc(mix_ready, 1)
                    else:
                        own.mark(ins)
                    own.mark(dve.scalar_tensor_tensor(out=r_mix[:, :], in0=b_adapt[:, k, :], scalar=wts[:, k:k + 1], in1=r_mix[:, :],
                                                      op0=ALU.mult, op1=ALU.add))
                own.join()
                run_turns(dve, "dve", turn3, dve_steps(dve, own), own, PER_TURN3)


def kernel(**inputs):
    import concourse.bacc as bacc
    from concourse.bass_utils import run_bass_kernel_spmd

    x = {k: np.asarray(v) for k, v in inputs.items()}
    half = HD // 2
    freq = (np.float32(1.0) / np.float32(10000.0) ** (np.arange(half, dtype=np.float32) / np.float32(half))).astype(np.float32)
    angle = np.arange(P, dtype=np.float32)[:, None] * freq[None, :]
    cos, sin = np.cos(angle), np.sin(angle)
    rope = np.stack([np.tile(np.concatenate([cos, cos], 1), (1, H)), np.tile(np.concatenate([-sin, sin], 1), (1, H))], 1)
    cat = np.concatenate
    arrays = {
        "x": x["x"], "ctx": x["ctx_1024"],
        "w_kv": cat([x["L0_xattn_Wk"].T, x["L0_xattn_Wv"].T], 1), "r_kv": cat([x["L0_xattn_bk"], x["L0_xattn_bv"]]),
        "w_q": x["L0_xattn_Wq"].T, "r_q": x["L0_xattn_bq"], "w_o": x["L0_xattn_Wo"].T, "r_o": x["L0_xattn_bo"],
        "w_qk2": cat([x["L0_ffn_q_w"], x["L0_ffn_k_w"]], 1), "w_v2": x["L0_ffn_v_w"], "w_gate": x["L0_ffn_gate_w"],
        "w_out": x["L0_ffn_out_w"], "w_route": x["L0_ffn_moe_gate_w"], "r_gate": x["L0_ffn_gate_b"],
        "r_scale": x["L0_ffn_scale_w"].reshape(-1), "r_route": x["L0_ffn_moe_gate_b"],
        "r_n1": cat([x["L0_ffn_n1_g"], x["L0_ffn_n1_b"]]), "r_n2": cat([x["L0_ffn_n2_g"], x["L0_ffn_n2_b"]]),
        "w1": x["L0_ffn_w1"], "w2": x["L0_ffn_w2"], "b1": x["L0_ffn_b1"].reshape(-1), "b2": x["L0_ffn_b2"].reshape(-1),
        "ln_gb": np.stack([x["L0_ffn_ln_g"], x["L0_ffn_ln_b"]]).reshape(2, E, FC, P).transpose(3, 0, 1, 2), "res_scale": x["L0_ffn_res_scale"],
        "w_kv3": cat([x["L1_xattn_Wk"].T, x["L1_xattn_Wv"].T], 1), "r_kv3": cat([x["L1_xattn_bk"], x["L1_xattn_bv"]]),
        "w_q3": x["L1_xattn_Wq"].T, "r_q3": x["L1_xattn_bq"], "w_o3": x["L1_xattn_Wo"].T, "r_o3": x["L1_xattn_bo"],
        "w_adapt": x["L1_ffn_W"].transpose(0, 2, 1), "b_adapt": x["L1_ffn_b"], "ids": x["L1_ffn_ids"],
        "wts": x["L1_ffn_weights"], "rope": rope.astype(np.float32),
    }
    arrays = {f"in_{k}": np.ascontiguousarray(v) for k, v in arrays.items()}
    nc = bacc.Bacc("TRN2", target_bir_lowering=False, num_devices=1)
    t = {k[3:]: nc.dram_tensor(k, v.shape, mybir.dt.from_np(v.dtype), kind="ExternalInput").ap() for k, v in arrays.items()}
    t["out"] = nc.dram_tensor("out", (B, P, D), F32, kind="ExternalOutput").ap()
    build(nc, t)
    r = run_bass_kernel_spmd(nc, [arrays], core_ids=[0])
    return r.results[0]["out"]
```

```python
from contextlib import ExitStack

import numpy as np

import concourse.bass as bass
from concourse import mybir

F32 = mybir.dt.float32
BF16 = mybir.dt.bfloat16
I32 = mybir.dt.int32
U32 = mybir.dt.uint32
ALU = mybir.AluOpType
ACT = mybir.ActivationFunctionType
AX = mybir.AxisListType

P = 128
B, D, H, HD = 16, 256, 16, 16
C = D // P
SLOTS = 4
NI = B // SLOTS
G, HG = 4, 4
E, F = 8, 512
FC = F // P
TILES = B * P // P + E - 1
XSLOTS = 4
ADAPTERS, K_ADAPT = 32, 8
VW = 32
EPS = 1e-5
MASKED = -1e30
STEP1, STEP3 = 19, 10
PER_TURN1, PER_TURN3 = 124, 100
LN1, LN3 = 2, 2


def at(i, per, k, base=0):
    return i * per + (base + k + 1)


def wait(eng, sem, value):
    if isinstance(value, int) and value <= 0:
        return
    eng.wait_ge(sem, value)


class Chain:

    def __init__(self, eng, sem):
        self.eng, self.sem, self.base, self.k, self.turn, self.per = eng, sem, 0, 0, 0, 0

    def start(self, turn, per):
        self.base, self.k, self.turn, self.per = self.base + self.k, 0, turn, per

    def end(self, turns):
        assert self.k == self.per, (self.k, self.per)
        self.base, self.k, self.turn, self.per = self.base + turns * self.per, 0, 0, 0

    def mark(self, ins):
        ins.then_inc(self.sem, 1)
        self.k += 1

    def join_by(self, spare):
        self.join()
        self.mark(self.eng.memset(spare, 0.0))

    def join(self):
        self.eng.wait_ge(self.sem, self.turn * self.per + (self.base + self.k))


SIDE_CA = ((["c_o", "c_oT", "c_gate", "c_gate2", "c_gT"], [],
             (0.37, 0.44, 0.59, 0.75, 0.91)),
            (["c_out", "c_norm", "c_x1T", "c_logits"], ["a_norm", "a_T", "a_kv"],
             (0.10, 0.35, 0.43, 0.59, 0.62, 0.65, 0.81)),
            ([], ["a_q"],
             (0.10,)))
SIDE_B = (([], ["b_o", "b_oT", "b_res"],
             (0.39, 0.67, 0.91)),
            ([], ["b_norm", "b_T", "b_qk", "b_v", "b_scale"],
             (0.10, 0.46, 0.82, 0.95, 0.98)),
            ([], ["b_qkT", "b_scale2"],
             (0.24, 0.51)))
SIDE_ED = ((["e_o", "e_oT", "e_res", "e_norm"], [],
             (0.31, 0.52, 0.73, 0.93)),
            (["e_T", "e_ffn"], ["d_stat", "d_norm", "d_T", "d_kv", "d_q"],
             (0.16, 0.30, 0.43, 0.57, 0.70, 0.83, 0.97)),
            ([], ["d_rope", "d_qkT"],
             (0.09, 0.31)))
SIDE_A0 = (["a_stat"], (0.44,))
SIDE_D0 = (["d_gather", "d_moe", "d_n2"], (0.09, 0.52, 0.64))
LAYOUT1 = (0.35, 0.61, 0.62, 0.65)
LAYOUT3 = (0.52, 0.57, 0.64, 0.67)
COST = {"scores": 1.07, "turn": 0.43, "mix": 0.32, "a_T": 0.43, "a_kv": 1.71, "a_q": 0.87, "b_o": 0.43,
        "b_oT": 0.21, "b_res": 0.86, "b_T": 0.21, "b_qk": 1.71, "b_v": 0.86, "b_qkT": 0.21, "c_o": 0.43, "c_oT": 0.21,
        "c_gate": 0.86, "c_gT": 0.21, "c_out": 0.86, "c_x1T": 0.21, "c_logits": 0.86, "d_T": 0.43, "d_kv": 1.71,
        "d_q": 0.86, "d_qkT": 0.43, "e_o": 0.43, "e_oT": 0.21, "e_res": 0.86, "e_T": 0.21, "e_ffn": 0.86}
AFTER = {("pool", "a_stat"): 0.7, ("pool", "b_res"): 0.8, ("pool", "c_out"): 0.38, ("act", "scores"): 0.72,
         ("act", "c_gate"): 0.56, ("act", "b_scale"): 0.7, ("pool", "d_gather"): 1.38,
         ("dve", "d_moe"): 1.88, ("pool", "d_moe"): 3.6, ("pool", "d_n2"): 1.6, ("pool", "d_stat"): 0.7,
         ("pool", "e_res"): 0.8, ("pool", "e_ffn"): 0.6}


def interval(core, before, following, sides, layout):
    steps = [("turn", core, 0), ("scores", core, 2), ("mix", before, 3), ("turn", core, 1), ("scores", core, 3),
             ("mix", core, 0), ("turn", core, 2), ("scores", following, 0), ("mix", core, 1), ("turn", core, 3),
             ("scores", following, 1), ("mix", core, 2)]
    placed = [((n + 0.5) / len(steps), s) for n, s in enumerate(steps) if s[1] is not None]
    for side in sides:
        placed += side
    if following is not None:
        placed += [(layout[g], ("expand", following, g)) for g in range(G)]
    return [s for _, s in sorted(placed, key=lambda p: p[0])]


def order_of(engine, steps):
    if engine == "pe":
        return steps
    now, keyed, free = 0.0, [], {}
    for s in steps:
        start, cost = now, COST.get(s[0], 0.0)
        if s[1] is None:
            chain = (s[2][0], s[0] in SIDE_A0[0] + SIDE_D0[0])
            start = max(now, free.get(chain, 0.0), free.get((s[2][0], True), 0.0) if s[0] in ("d_stat", "a_norm") else 0.0)
            free[chain] = start + cost + 0.1 + max([t for (_, n), t in AFTER.items() if n == s[0]] + [0.0])
        if cost:
            now = start + cost
        keyed.append((start + cost + 0.05 + AFTER.get((engine, s[0]), 0.0), s))
    return [s for _, s in sorted(keyed, key=lambda k: k[0])]


def turn_steps(i, first, last, attns, between, extra, layout):
    per = len(attns) * SLOTS

    def core_of(q):
        if (q < 0 and first) or (q >= per and last):
            return None
        turn = i + q // per
        return q % SLOTS, attns[q % per // SLOTS], turn

    def part(q, k):
        if q < 0 or (last and q >= per + SLOTS):
            return []
        slot, turn = q % SLOTS, i + q // per
        old, new, positions = between[q % per // SLOTS][k]
        steps = [(n, None, (slot, turn - 1)) for n in old] + [(n, None, (slot, turn)) for n in new]
        return [(p, s) for p, s in zip(positions, steps) if not (first and q < SLOTS and s[0] in old)
                and not (last and q >= per and s[0] in new)]
    out = []
    for q in range(-3 if first else 0, per + 3 if last else per):
        sides = [part(q + 3 - k, k) for k in range(3)]
        if (q + 3) % per < SLOTS and not (last and q + 3 >= per):
            slot, turn = (q + 3) % SLOTS, i + (q + 3) // per
            sides.append([(p, (n, None, (slot, turn))) for n, p in zip(*extra)])
        out += interval(core_of(q), core_of(q - 1) if (q > 0 or not first) else None,
                        core_of(q + 1) if q >= -1 else None, sides, layout)
    return out


def turn1(i, first, last):
    return turn_steps(i, first, last, (0, 1), (SIDE_CA, SIDE_B), SIDE_A0, LAYOUT1)


def turn3(i, first, last):
    return turn_steps(i, first, last, (2,), (SIDE_ED,), SIDE_D0, LAYOUT3)


def run_turns(eng, name, turn, step, chain=None, per=0):
    for body, turns in ((0, 1), (1, NI - 2), (2, 1)):
        if body == 1:
            with eng.Fori(1, NI - 1) as i:
                if chain:
                    chain.start(i - 1, per)
                for s in order_of(name, turn(i, False, False)):
                    step(*s)
                if chain:
                    chain.end(turns)
        else:
            i = 0 if body == 0 else NI - 1
            for s in order_of(name, turn(i, body == 0, body == 2)):
                step(*s)


def build(nc, t):
    ctx = ExitStack()
    with ctx:
        def sb(name, shape, dt=F32):
            return ctx.enter_context(nc.sbuf_tensor(name, shape, dt))

        def sem(name):
            return ctx.enter_context(nc.semaphore(name))

        ps = ctx.enter_context(nc.psum_tensor("ps", [P, 8, 512], F32))
        bank = [ps[:, n, :] for n in range(8)]
        SC = [bank[0], bank[1]]
        PT = [bank[2], bank[3]]
        M = bank[4:8]

        w_kv = sb("w_kv", [P, C, 2 * D])
        w_q = sb("w_q", [P, C, D])
        w_o = sb("w_o", [P, C, D])
        w_qk2 = sb("w_qk2", [P, C, 2 * D])
        w_v2 = sb("w_v2", [P, C, D])
        w_gate = sb("w_gate", [P, C, D])
        w_out = sb("w_out", [P, C, D])
        w_route = sb("w_route", [P, C, E])
        w1 = sb("w1", [P, C, E * F])
        w2 = sb("w2", [P, FC, E * D])
        w_mix = w_gate
        r_kv = sb("r_kv", [P, 2 * D])
        r_q = sb("r_q", [P, D])
        col_k = sb("col_k", [P, C])
        col_q = sb("col_q", [P, C])
        r_o = sb("r_o", [P, D])
        r_gate = sb("r_gate", [P, D])
        r_scale = sb("r_scale", [P, D])
        r_n1 = sb("r_n1", [P, 2, D])
        r_n2 = sb("r_n2", [P, 2, D])
        r_route = sb("r_route", [P, E])
        rope = sb("rope", [P, 2, D])
        r_mix = r_gate
        ident = sb("ident", [P, P])
        ident_bf = sb("ident_bf", [P, P], BF16)
        ones = sb("ones", [P, P])
        before_me = sb("before_me", [P, P])
        mask_bf = sb("mask_bf", [P, HG, P], BF16)
        headmask = sb("headmask", [P, P // HD])
        minus_half = sb("minus_half", [P, 1])
        x_all = sb("x_all", [P, B, D])
        x1_all = sb("x1_all", [P, B, D])
        logits = sb("logits", [P, B, E])
        wsum = sb("wsum", [P, B])
        kexp = sb("kexp", [P, 2, H, P])
        prob = sb("prob", [P, G, HG * P])
        pts = sb("pts", [P, 2, HG * P])
        b1_all = kexp[:, :, :, :].rearrange("p s h k -> p (s h k)")
        b2_all = prob[:, :, :].rearrange("p g k -> p (g k)")
        HALF = K_ADAPT // 2
        w_adapt = [w_qk2[:, 0, :], w_qk2[:, 1, :], w_v2[:, :, :].rearrange("p c n -> p (c n)"),
                   w_out[:, :, :].rearrange("p c n -> p (c n)")]
        ARENA = 3584
        w2_all = w2[:, :, :].rearrange("p c n -> p (c n)")
        arena = [sb("arena0", [P, ARENA])[:, :], sb("arena1", [P, ARENA])[:, :],
                 w2_all[:, 0:ARENA], w2_all[:, ARENA:2 * ARENA]]

        def carve(a, sizes):
            out, off = [], 0
            for n in sizes:
                out.append(a[:, off:off + n])
                off += n
            assert off <= ARENA
            return out
        (xcur, c_in, xn, srcT, qk, vaug, qkT, gate, tmp) = map(list, zip(*[
            carve(arena[u], [D, D, D, 2 * D, 2 * D, H * VW, 2 * D, D, 2 * D]) for u in range(SLOTS)]))
        o_tok, ots = xn, qk
        oT = [s[:, D:2 * D] for s in srcT]
        vaug = [v.rearrange("p (h w) -> p h w", w=VW) for v in vaug]
        stats = [sb(f"stats{u}", [P, 6]) for u in range(XSLOTS)]
        mv = [sb(f"mv{u}", [P, 2]) for u in range(XSLOTS)]
        veps = [sb(f"veps{u}", [P, 1]) for u in range(XSLOTS)]
        rstd = [sb(f"rstd{u}", [P, 1]) for u in range(XSLOTS)]
        spare = [sb(f"spare{u}", [P, 1]) for u in range(XSLOTS)]
        rsum = [sb(f"rsum{u}", [P, H]) for u in range(SLOTS)]
        rowscale = [sb(f"rowscale{u}", [P, H]) for u in range(SLOTS)]
        rz = [sb(f"rz{u}", [P, H]) for u in range(SLOTS)]
        nbias = sb("nbias", [P, H])
        (xe, xeT, hid, hT, ye) = map(list, zip(*[
            carve(arena[u // 2][:, (u % 2) * (ARENA // 2):(u % 2 + 1) * (ARENA // 2)], [D, D, F, F, D])
            for u in range(XSLOTS)]))
        x_res = [sb(f"x_res{u}", [P, D]) for u in range(XSLOTS)]
        top8 = sb("top8", [P, B, 8])
        idx8 = sb("idx8", [P, B, 8], U32)
        chosen = sb("chosen", [P, B])
        onehot = sb("onehot", [P, B, E])
        tot = sb("tot", [P, B, E])
        base = sb("base", [P, B, E])
        base2 = sb("base2", [P, B, E])
        iota_e = sb("iota_e", [P, E])
        iota_j = sb("iota_j", [P, B])
        iota_t = sb("iota_t", [P, TILES])
        iota_i = sb("iota_i", [P, 32], I32)
        ecount = sb("ecount", [P, E])
        etiles = sb("etiles", [P, E])
        estart = sb("estart", [P, E])
        eend = sb("eend", [P, E])
        ecmp = sb("ecmp", [P, E, B])
        tcmp = sb("tcmp", [P, TILES, E])
        texp = sb("texp", [P, TILES])
        texp_i = sb("texp_i", [P, TILES], I32)
        pos = sb("pos", [P, B])
        pos_u = sb("pos_u", [P, B], U32)
        small = sb("small", [P, 4, B])
        gcol = sb("gcol", [P, 2, E, FC])
        ecol = [sb(f"ecol{u}", [P, 2, FC]) for u in range(XSLOTS)]
        rs_row = sb("rs_row", [P, E])
        minus_mean = [sb(f"minus_mean{u}", [P, 1]) for u in range(XSLOTS)]
        nmr = [sb(f"nmr{u}", [P, 1]) for u in range(XSLOTS)]
        ers = [sb(f"ers{u}", [P, 1]) for u in range(XSLOTS)]
        moe_in = [sb(f"moe_in{u}", [P, D]) for u in range(SLOTS)]
        spare_p = sb("spare_p", [P, 1])
        moe_at = [sb(f"moe_at{u}", [P, 1], U32) for u in range(SLOTS)]
        wts_col = sb("wts_col", [K_ADAPT, 1])
        wts_k = sb("wts_k", [K_ADAPT, P])
        b_adapt = sb("b_adapt", [K_ADAPT, D])
        ids_i = sb("ids_i", [P, K_ADAPT], I32)
        ids_f = sb("ids_f", [P, K_ADAPT])
        ids_n = sb("ids_n", [P, K_ADAPT])
        wts = sb("wts", [P, K_ADAPT])

        sorted_x = nc.dram_tensor("sorted_x", [TILES * P, D], F32)
        sorted_y = nc.dram_tensor("sorted_y", [TILES * P, D], F32)

        x_loaded = [sem(f"x_loaded{u}") for u in range(SLOTS)]
        c_loaded = [sem(f"c_loaded{u}") for u in range(SLOTS)]
        weights_a = sem("weights_a")
        weights0 = sem("weights0")
        weights2 = sem("weights2")
        down_loaded = sem("down_loaded")
        rows2 = sem("rows2")
        weights3 = sem("weights3")
        adapters = sem("adapters")
        adapter_rows = sem("adapter_rows")
        half_mixed = sem("half_mixed")
        row_mixed = sem("row_mixed")
        consts = sem("consts")
        pool_own = sem("pool_own")
        dve_own = sem("dve_own")
        act_own = sem("act_own")
        ready = [sem(f"ready{u}") for u in range(SLOTS)]
        full = [sem(f"full{u}") for u in range(SLOTS)]
        var_ready = [sem(f"var_ready{u}") for u in range(SLOTS)]
        rstd_ready = [sem(f"rstd_ready{u}") for u in range(SLOTS)]
        kexp_ready = sem("kexp_ready")
        z_ready = [sem(f"z_ready{u}") for u in range(SLOTS)]
        ez_ready = [sem(f"ez_ready{u}") for u in range(SLOTS)]
        kept = [sem(f"kept{u}") for u in range(SLOTS)]
        scored = sem("scored")
        maxed = sem("maxed")
        exped = sem("exped")
        turned = sem("turned")
        copied = sem("copied")
        mixed = sem("mixed")
        y_done = [sem(f"y_done{u}") for u in range(SLOTS)]
        y_stored = [sem(f"y_stored{u}") for u in range(SLOTS)]
        zeroed = sem("zeroed")
        zero_ready = sem("zero_ready")
        route_a = sem("route_a")
        route_b = sem("route_b")
        route_c = sem("route_c")
        scattered = sem("scattered")
        gathered = [sem(f"gathered{u}") for u in range(SLOTS)]
        tile_in, tile_kept, tile_turned, tile_xT, tile_full, tile_ready, tile_var, tile_rstd, tile_cols, tile_out, tile_stored = (
            [sem(f"{name}{s}") for s in range(XSLOTS)]
            for name in ("tile_in", "tile_kept", "tile_turned", "tile_xT", "tile_full", "tile_ready", "tile_var", "tile_rstd", "tile_cols", "tile_out", "tile_stored"))
        dve_own2 = sem("dve_own2")
        dve_own3 = sem("dve_own3")
        pool_own2 = sem("pool_own2")
        pool_own3 = sem("pool_own3")
        mix_ready = sem("mix_ready")

        normed = [sem(f"normed{u}") for u in range(SLOTS)]
        shifted = [sem(f"shifted{u}") for u in range(SLOTS)]
        row_norm = [(mv[u], veps[u], rstd[u], var_ready[u], rstd_ready[u]) for u in range(SLOTS)]
        source_norm = [(sb(f"mv_b{u}", [P, 2]), sb(f"veps_b{u}", [P, 1]), sb(f"rstd_b{u}", [P, 1]),
                       sem(f"var_ready_b{u}"), sem(f"rstd_ready_b{u}")) for u in range(SLOTS)]

        WA_ALL, W0_ALL = 6 * 16, 11 * 16

        def slot_bn(i, u):
            return i * SLOTS + u

        def bc_row(name, n):
            return t[name].rearrange("(a n) -> a n", a=1).broadcast_to([P, n])

        def pool_steps(pool, own):
            def rstd_step(u, n, norm=row_norm):
                mv, veps, rstd, var_ready, rstd_ready = norm[u]
                pool.wait_ge(var_ready, n)
                pool.tensor_tensor(rstd[:, :], veps[:, :], minus_half[:, :], ALU.pow).then_inc(rstd_ready, 1)

            def expand(core, g):
                u, _, _ = core
                n = core_number(core)
                if g == 0:
                    pool.wait_ge(ready[u], product(core))
                    if not (isinstance(n, int) and n < 2):
                        pool.wait_ge(scored, groups(n, G - 1) - 2 * G)
                c, h0 = g // 2, (g % 2) * HG
                keys = qkT[u][:, D + c * P:D + (c + 1) * P]
                pool.tensor_tensor(kexp[:, u % 2, g * HG:(g + 1) * HG, :], keys.unsqueeze(1).broadcast_to([P, HG, P]),
                                   headmask[:, h0:h0 + HG].unsqueeze(2).broadcast_to([P, HG, P]),
                                   ALU.mult).then_inc(kexp_ready, 1)

            def keep(u, dst, src, b, value):
                pool.wait_ge(ready[u], value)
                pool.tensor_copy(dst[:, bass.ds(b, 1), :].rearrange("p a d -> p (a d)"), src).then_inc(kept[u], 1)

            def gather_rows(u, i):
                own.mark(pool.tensor_copy(moe_at[u][:, :], pos_u[:, bass.ds(slot_bn(i, u), 1)]))
                own.join()
                own.mark(pool.tensor_tensor(spare_p[:, :], minus_half[:, :], minus_half[:, :], ALU.mult))
                pool.indirect_dma_start(out=moe_in[u][:, :], out_offset=None, in_=sorted_y[:, :],
                                        in_offset=bass.IndirectOffsetOnAxis(ap=moe_at[u][:, 0:1], axis=0)).then_inc(gathered[u], 16)

            def step(name, core, st):
                if name == "expand":
                    return expand(core, st)
                if core is not None:
                    return
                u, i = st
                if name == "a_stat":
                    rstd_step(u, i + 1, source_norm)
                elif name == "b_res":
                    rstd_step(u, at(i, LN1, 0))
                elif name == "b_T":
                    keep(u, x_all, xcur[u], slot_bn(i, u), at(i, STEP1, 7))
                elif name == "c_out":
                    rstd_step(u, at(i, LN1, 1))
                elif name == "c_x1T":
                    keep(u, x1_all, tmp[u][:, 0:D], slot_bn(i, u), at(i, STEP1, 17))
                elif name == "d_gather":
                    gather_rows(u, i)
                elif name == "d_moe":
                    rstd_step(u, i + (NI + 1), source_norm)
                elif name == "d_n2":
                    x = tmp[u][:, 0:D]
                    pool.wait_ge(normed[u], i + 1)
                    own.mark(pool.tensor_tensor(x, x, r_n2[:, 0, :], ALU.mult))
                    own.join()
                    own.mark(pool.tensor_tensor(x, x, r_n2[:, 1, :], ALU.add))
                    own.join()
                    pool.tensor_tensor(x, x, x_all[:, bass.ds(slot_bn(i, u), 1), :].rearrange("p a d -> p (a d)"),
                                       ALU.add).then_inc(shifted[u], 1)
                elif name == "d_stat":
                    rstd_step(u, at(i, LN3, 0, NI * LN1))
                elif name == "e_res":
                    rstd_step(u, at(i, LN3, 1, NI * LN1))
                elif name == "e_ffn":
                    pool.wait_ge(y_done[u], i + 1)
                    pool.dma_start(t["out"][bass.ds(slot_bn(i, u), 1), :, :].rearrange("a p d -> p (a d)"),
                                   gate[u]).then_inc(y_stored[u], 16)
            return step

        def core_number(core):
            u, a, i = core
            if a == 2:
                return i * SLOTS + (u + 2 * SLOTS * NI)
            return i * (2 * SLOTS) + (a * SLOTS + u)

        def groups(n, g):
            return n * G + (g + 1)

        def product(core):
            u, a, i = core
            return at(i, STEP3, 4, NI * STEP1) if a == 2 else at(i, STEP1, 11 if a else 3)

        def pe_steps(pe):
            def transposes(dst, srcs):
                for n, s in enumerate(srcs):
                    last = pe.transpose(dst[:, n * P:(n + 1) * P], s, ident[:, :])
                return last

            def halves(x):
                return [x[:, c * P:(c + 1) * P] for c in range(x.shape[1] // P)]

            def project(dst, xT, w):
                for c in range(C):
                    last = pe.matmul(dst, xT[:, c * P:(c + 1) * P], w[:, c, :], start=(c == 0), stop=(c == C - 1))
                return last

            def project_T(dst, xT, w):
                for n in range(C):
                    for c in range(C):
                        last = pe.matmul(dst[:, n * P:(n + 1) * P], w[:, c, n * P:(n + 1) * P], xT[:, c * P:(c + 1) * P],
                                         start=(c == 0), stop=(c == C - 1))
                return last

            def core_step(name, core, g):
                u, a, i = core
                n = core_number(core)
                if name == "scores":
                    if g == 0:
                        pe.wait_ge(ready[u], product(core))
                    pe.wait_ge(kexp_ready, groups(n, g))
                    wait(pe, exped, groups(n, g) - 2)
                    if a != 1:
                        pe.matmul(SC[g % 2], ident_bf[:, :], mask_bf[:, :, :].rearrange("p h k -> p (h k)"),
                                  start=True, stop=False)
                    c = g // 2
                    pe.matmul(SC[g % 2], qkT[u][:, c * P:(c + 1) * P],
                              kexp[:, u % 2, g * HG:(g + 1) * HG, :].rearrange("p h k -> p (h k)"),
                              start=(a == 1), stop=True).then_inc(scored, 1)
                elif name == "turn":
                    pe.wait_ge(exped, groups(n, g))
                    wait(pe, copied, groups(n, g) - 2)
                    transposes(PT[g % 2], [prob[:, g, j * P:(j + 1) * P] for j in range(HG)]).then_inc(turned, 1)
                elif name == "mix":
                    pe.wait_ge(copied, groups(n, g))
                    for j in range(HG):
                        last = pe.matmul(M[u][VW * j:VW * (j + 1), g * P:(g + 1) * P], vaug[u][:, g * HG + j, :],
                                         pts[:, g % 2, j * P:(j + 1) * P], start=True, stop=True)
                    last.then_inc(mixed, 1)

            def step(name, core, st):
                if core is not None:
                    return core_step(name, core, st)
                u, i = st
                m = M[u]

                def start(k):
                    pe.wait_ge(ready[u], at(i, STEP1, k))

                def start3(k):
                    pe.wait_ge(ready[u], at(i, STEP3, k, NI * STEP1))
                if name == "a_T":
                    start(0)
                    pe.wait_ge(c_loaded[u], at(i, 16, 15))
                    transposes(m, halves(c_in[u]) + halves(xn[u])).then_inc(full[u], 1)
                elif name == "a_kv":
                    start(1)
                    if isinstance(i, int) and i == 0 and u == 0:
                        pe.wait_ge(weights_a, WA_ALL)
                    project(m[:, 0:D], srcT[u][:, 0:D], w_kv[:, :, D:2 * D])
                    project_T(m[:, D:2 * D], srcT[u][:, 0:D], w_kv[:, :, 0:D]).then_inc(full[u], 1)
                elif name == "a_q":
                    start(2)
                    project_T(m[:, 0:D], srcT[u][:, D:2 * D], w_q).then_inc(full[u], 1)
                elif name == "b_o":
                    start(4)
                    transposes(m, halves(ots[u])).then_inc(full[u], 1)
                elif name == "b_oT":
                    start(5)
                    transposes(m, halves(o_tok[u])).then_inc(full[u], 1)
                elif name == "b_res":
                    start(6)
                    if isinstance(i, int) and i == 0 and u == 0:
                        pe.wait_ge(weights0, W0_ALL)
                    project(m[:, 0:D], oT[u], w_o).then_inc(full[u], 1)
                elif name == "b_T":
                    start(7)
                    transposes(m, halves(xn[u])).then_inc(full[u], 1)
                elif name == "b_qk":
                    start(8)
                    project(m[:, 0:D], srcT[u][:, 0:D], w_qk2[:, :, 0:D])
                    project_T(m[:, D:2 * D], srcT[u][:, 0:D], w_qk2[:, :, D:2 * D]).then_inc(full[u], 1)
                elif name == "b_v":
                    start(9)
                    project(m[:, 0:D], srcT[u][:, 0:D], w_v2).then_inc(full[u], 1)
                elif name == "b_qkT":
                    start(10)
                    transposes(m, halves(qk[u][:, 0:D])).then_inc(full[u], 1)
                elif name == "c_o":
                    start(12)
                    transposes(m, halves(ots[u])).then_inc(full[u], 1)
                elif name == "c_oT":
                    start(13)
                    transposes(m, halves(gate[u])).then_inc(full[u], 1)
                elif name == "c_gate":
                    start(14)
                    project(m[:, 0:D], oT[u], w_gate).then_inc(full[u], 1)
                elif name == "c_gT":
                    start(15)
                    transposes(m, halves(gate[u])).then_inc(full[u], 1)
                elif name == "c_out":
                    start(16)
                    project(m[:, 0:D], oT[u], w_out).then_inc(full[u], 1)
                elif name == "c_x1T":
                    start(17)
                    transposes(m, halves(tmp[u][:, 0:D])).then_inc(full[u], 1)
                elif name == "c_logits":
                    start(18)
                    project(m[:, 0:E], oT[u], w_route).then_inc(full[u], 1)
                elif name == "d_T":
                    start3(0)
                    pe.wait_ge(c_loaded[u], at(i, 16, 15, 16 * NI))
                    transposes(m, halves(c_in[u]) + halves(xn[u])).then_inc(full[u], 1)
                elif name == "d_kv":
                    start3(1)
                    project(m, srcT[u][:, 0:D], w_kv).then_inc(full[u], 1)
                elif name == "d_q":
                    start3(2)
                    project(m[:, 0:D], srcT[u][:, D:2 * D], w_q).then_inc(full[u], 1)
                elif name == "d_qkT":
                    start3(3)
                    transposes(m, halves(qk[u])).then_inc(full[u], 1)
                elif name == "e_o":
                    start3(5)
                    transposes(m, halves(ots[u])).then_inc(full[u], 1)
                elif name == "e_oT":
                    start3(6)
                    transposes(m, halves(o_tok[u])).then_inc(full[u], 1)
                elif name == "e_res":
                    start3(7)
                    project(m[:, 0:D], oT[u], w_o).then_inc(full[u], 1)
                elif name == "e_T":
                    start3(8)
                    transposes(m, halves(xn[u])).then_inc(full[u], 1)
                elif name == "e_ffn":
                    start3(9)
                    project(m[:, 0:D], srcT[u][:, 0:D], w_mix).then_inc(full[u], 1)
            return step

        def act_steps(act):
            def core_step(name, core, g):
                u, a, i = core
                n = core_number(core)
                if name == "scores":
                    act.wait_ge(maxed, groups(n, g))
                    wait(act, turned, groups(n, g) - G)
                    for j in range(HG):
                        h = g * HG + j
                        last = act.activation(prob[:, g, j * P:(j + 1) * P], SC[g % 2][:, j * P:(j + 1) * P], ACT.Exp,
                                              bias=nbias[:, h:h + 1],
                                              scale=rowscale[u][:, h:h + 1] if a == 1 else float(HD) ** -0.5)
                    last.then_inc(exped, 1)
                elif name == "turn":
                    act.wait_ge(turned, groups(n, g))
                    wait(act, mixed, groups(n, g) - 2)
                    act.copy(pts[:, g % 2, :], PT[g % 2]).then_inc(copied, 1)
                elif name == "mix" and g == G - 1:
                    act.wait_ge(mixed, groups(n, g))
                    act.copy(ots[u], M[u]).then_inc(ready[u], 1)

            def step(name, core, st):
                if core is not None:
                    return core_step(name, core, st)
                u, i = st
                m = M[u]

                def copy_out(dst, n, k, per=STEP1, base=0):
                    act.wait_ge(full[u], at(i, per - 2 if per == STEP1 else per - 1, k, base))
                    act.copy(dst, m[:, 0:n]).then_inc(ready[u], 1)
                if name == "a_T":
                    copy_out(srcT[u], 512, 0)
                elif name == "b_oT":
                    copy_out(oT[u], D, 4)
                elif name == "b_T":
                    copy_out(srcT[u][:, 0:D], D, 6)
                elif name == "b_qk":
                    act.wait_ge(full[u], at(i, STEP1 - 2, 7))
                    act.copy(qkT[u][:, D:2 * D], m[:, D:2 * D])
                    act.copy(qk[u][:, 0:D], m[:, 0:D]).then_inc(ready[u], 1)
                elif name == "b_v":
                    act.wait_ge(full[u], at(i, STEP1 - 2, 8))
                    act.copy(vaug[u][:, :, 0:HD], m[:, 0:D].rearrange("p (h w) -> p h w", w=HD)).then_inc(ready[u], 1)
                elif name == "b_scale":
                    act.wait_ge(z_ready[u], at(i, 2, 0))
                    act.activation(rz[u][:, :], rz[u][:, :], ACT.Exp, scale=-1.0).then_inc(ez_ready[u], 1)
                elif name == "b_qkT":
                    copy_out(qkT[u][:, 0:D], D, 9)
                elif name == "c_oT":
                    copy_out(oT[u], D, 11)
                elif name == "c_gate":
                    act.wait_ge(z_ready[u], at(i, 2, 1))
                    act.activation(tmp[u][:, D:2 * D], tmp[u][:, 0:D], ACT.Exp, scale=-1.0).then_inc(ez_ready[u], 1)
                elif name == "c_gT":
                    copy_out(oT[u], D, 13)
                elif name == "c_x1T":
                    copy_out(oT[u], D, 15)
                elif name == "d_T":
                    copy_out(srcT[u], 512, 0, STEP3, NI * (STEP1 - 2))
                elif name == "d_qkT":
                    copy_out(qkT[u], 512, 3, STEP3, NI * (STEP1 - 2))
                elif name == "e_oT":
                    copy_out(oT[u], D, 5, STEP3, NI * (STEP1 - 2))
                elif name == "e_T":
                    copy_out(srcT[u][:, 0:D], D, 7, STEP3, NI * (STEP1 - 2))
            return step

        def dve_steps(dve, own):
            def norm_stats(u, src, norm=row_norm):
                mv, veps, _, var_ready, _ = norm[u]
                own.mark(dve.bn_stats(stats[u][:, :], src))
                own.join_by(spare[u][:, :])
                own.mark(dve.bn_aggr(mv[:, :], stats[u][:, :]))
                own.join()
                dve.tensor_scalar(veps[:, :], mv[:, 1:2], EPS, None, ALU.add).then_inc(var_ready, 1)

            def normalize(u, dst, src, n, norm=row_norm):
                mv, _, rstd, _, rstd_ready = norm[u]
                dve.wait_ge(rstd_ready, n)
                return dve.tensor_scalar(dst, src, mv[:, 0:1], rstd[:, :], ALU.subtract, ALU.mult)

            def heads(x, w):
                return x.rearrange("p (h w) -> p h w", w=w)

            def columns(dst, src, col):
                return dve.tensor_tensor(dst.rearrange("p (c k) -> p c k", c=C), src.rearrange("p (c k) -> p c k", c=C),
                                         col[:, :].unsqueeze(2).broadcast_to([P, C, P]), ALU.add)

            def sigmoid_of(dst, e, scale):
                own.mark(dve.tensor_scalar(e, e, 1.0, 1.0 / scale, ALU.add, ALU.mult))
                own.join()
                return dve.reciprocal(dst, e)

            def attention_out(u, dst):
                o = heads(M[u], VW)
                own.mark(dve.reciprocal(rsum[u][:, :], o[:, :, HD]))
                own.join()
                dve.tensor_tensor(heads(dst, HD), o[:, :, 0:HD],
                                  rsum[u][:, :].unsqueeze(2).broadcast_to([P, H, HD]), ALU.mult).then_inc(ready[u], 1)

            def core_step(name, core, g):
                u, a, i = core
                n = core_number(core)
                if name == "scores":
                    dve.wait_ge(scored, groups(n, g))
                    hs = slice(g * HG, (g + 1) * HG)
                    own.mark(dve.tensor_reduce(nbias[:, hs], SC[g % 2].rearrange("p (h k) -> p h k", h=HG), AX.X, ALU.max, negate=True))
                    own.join()
                    if a == 1:
                        dve.tensor_tensor(nbias[:, hs], nbias[:, hs], rowscale[u][:, hs], ALU.mult).then_inc(maxed, 1)
                    else:
                        dve.tensor_scalar(nbias[:, hs], nbias[:, hs], float(HD) ** -0.5, None, ALU.mult).then_inc(maxed, 1)

            def step(name, core, st):
                if core is not None:
                    return core_step(name, core, st)
                u, i = st
                m = M[u]

                def taken(k):
                    dve.wait_ge(full[u], at(i, STEP1 - 2, k))

                def taken3(k):
                    dve.wait_ge(full[u], at(i, STEP3 - 1, k, NI * (STEP1 - 2)))
                if name == "a_stat":
                    dve.wait_ge(x_loaded[u], at(i, 16, 15))
                    norm_stats(u, xcur[u], source_norm)
                elif name == "a_norm":
                    normalize(u, xn[u], xcur[u], i + 1, source_norm).then_inc(ready[u], 1)
                elif name == "a_kv":
                    taken(1)
                    if isinstance(i, int) and i == 0 and u == 0:
                        dve.wait_ge(weights_a, WA_ALL)
                    own.mark(dve.tensor_tensor(xcur[u], xcur[u], r_o[:, :], ALU.add))
                    own.mark(dve.tensor_tensor(vaug[u][:, :, 0:HD], heads(m[:, 0:D], HD), heads(r_kv[:, D:2 * D], HD), ALU.add))
                    columns(qkT[u][:, D:2 * D], m[:, D:2 * D], col_k).then_inc(ready[u], 1)
                elif name == "a_q":
                    taken(2)
                    columns(qkT[u][:, 0:D], m[:, 0:D], col_q).then_inc(ready[u], 1)
                elif name == "b_o":
                    taken(3)
                    attention_out(u, o_tok[u])
                elif name == "b_res":
                    taken(5)
                    own.join()
                    own.mark(dve.tensor_tensor(xcur[u], m[:, 0:D], xcur[u], ALU.add))
                    own.join()
                    norm_stats(u, xcur[u])
                elif name == "b_norm":
                    normalize(u, xn[u], xcur[u], at(i, LN1, 0)).then_inc(ready[u], 1)
                elif name == "b_scale":
                    if isinstance(i, int) and i == 0 and u == 0:
                        dve.wait_ge(weights0, W0_ALL)
                    dve.wait_ge(ready[u], at(i, STEP1, 9))
                    if not (isinstance(i, int) and i == 0):
                        dve.wait_ge(kept[u], at(i, 2, 1, -2))
                    own.mark(dve.tensor_tensor(tmp[u][:, 0:D], qk[u][:, 0:D], r_scale[:, :], ALU.mult))
                    own.join()
                    dve.tensor_reduce(rz[u][:, :], heads(tmp[u][:, 0:D], HD), AX.X, ALU.add).then_inc(z_ready[u], 1)
                elif name == "b_scale2":
                    dve.wait_ge(ez_ready[u], at(i, 2, 0))
                    own.mark(sigmoid_of(rowscale[u][:, :], rz[u][:, :], 2.0 * float(HD) ** -0.5))
                    own.join()
                elif name == "c_o":
                    taken(10)
                    attention_out(u, gate[u])
                elif name == "c_gate":
                    taken(12)
                    dve.tensor_tensor(tmp[u][:, 0:D], m[:, 0:D], r_gate[:, :], ALU.add).then_inc(z_ready[u], 1)
                elif name == "c_gate2":
                    dve.wait_ge(ez_ready[u], at(i, 2, 1))
                    own.mark(sigmoid_of(tmp[u][:, 0:D], tmp[u][:, D:2 * D], 1.0))
                    own.join()
                    dve.tensor_tensor(gate[u], gate[u], tmp[u][:, 0:D], ALU.mult).then_inc(ready[u], 1)
                elif name == "c_out":
                    taken(14)
                    own.mark(dve.tensor_tensor(tmp[u][:, D:2 * D], m[:, 0:D], xn[u], ALU.add))
                    own.join()
                    norm_stats(u, tmp[u][:, D:2 * D])
                elif name == "c_norm":
                    own.mark(normalize(u, tmp[u][:, 0:D], tmp[u][:, D:2 * D], at(i, LN1, 1)))
                    own.join()
                    own.mark(dve.tensor_tensor(tmp[u][:, 0:D], tmp[u][:, 0:D], r_n1[:, 0, :], ALU.mult))
                    own.join()
                    dve.tensor_tensor(tmp[u][:, 0:D], tmp[u][:, 0:D], r_n1[:, 1, :], ALU.add).then_inc(ready[u], 1)
                elif name == "c_logits":
                    taken(16)
                    own.mark(dve.tensor_tensor(logits[:, bass.ds(slot_bn(i, u), 1), :].rearrange("p a e -> p (a e)"),
                                               m[:, 0:E], r_route[:, :], ALU.add))
                elif name == "d_moe":
                    b = slot_bn(i, u)
                    row = lambda a: a[:, bass.ds(b, 1), :].rearrange("p a d -> p (a d)")
                    dve.wait_ge(gathered[u], at(i, 16, 15))
                    own.mark(dve.scalar_tensor_tensor(out=tmp[u][:, 0:D], in0=moe_in[u][:, :], scalar=wsum[:, bass.ds(b, 1)],
                                                      in1=row(x1_all), op0=ALU.mult, op1=ALU.add))
                    own.join()
                    norm_stats(u, tmp[u][:, 0:D], source_norm)
                elif name == "d_n2":
                    normalize(u, tmp[u][:, 0:D], tmp[u][:, 0:D], i + (NI + 1), source_norm).then_inc(normed[u], 1)
                elif name == "d_stat":
                    dve.wait_ge(shifted[u], i + 1)
                    norm_stats(u, tmp[u][:, 0:D])
                elif name == "d_norm":
                    normalize(u, xn[u], tmp[u][:, 0:D], at(i, LN3, 0, NI * LN1)).then_inc(ready[u], 1)
                elif name == "d_kv":
                    taken3(1)
                    own.mark(dve.tensor_tensor(xcur[u], tmp[u][:, 0:D], r_o[:, :], ALU.add))
                    own.mark(dve.tensor_tensor(qk[u][:, D:2 * D], m[:, 0:D], r_kv[:, 0:D], ALU.add))
                    dve.tensor_tensor(vaug[u][:, :, 0:HD], heads(m[:, D:2 * D], HD), heads(r_kv[:, D:2 * D], HD), ALU.add).then_inc(ready[u], 1)
                elif name == "d_q":
                    taken3(2)
                    own.mark(dve.tensor_tensor(qk[u][:, 0:D], m[:, 0:D], r_q[:, :], ALU.add))
                    own.join()
                elif name == "d_rope":
                    both = qk[u].rearrange("p (a d) -> p a d", a=2)
                    hh = HD // 2
                    for a in range(2):
                        rot = heads(tmp[u][:, a * D:(a + 1) * D], HD)
                        x = heads(qk[u][:, a * D:(a + 1) * D], HD)
                        sn = heads(rope[:, 1, :], HD)
                        own.mark(dve.tensor_tensor(rot[:, :, 0:hh], x[:, :, hh:HD], sn[:, :, 0:hh], ALU.mult))
                        own.mark(dve.tensor_tensor(rot[:, :, hh:HD], x[:, :, 0:hh], sn[:, :, hh:HD], ALU.mult))
                    own.join()
                    own.mark(dve.tensor_tensor(both, both, rope[:, 0, :].unsqueeze(1).broadcast_to([P, 2, D]), ALU.mult))
                    own.join()
                    dve.tensor_tensor(qk[u], qk[u], tmp[u], ALU.add).then_inc(ready[u], 1)
                elif name == "e_o":
                    taken3(4)
                    attention_out(u, o_tok[u])
                elif name == "e_res":
                    taken3(6)
                    own.join()
                    own.mark(dve.tensor_tensor(xcur[u], m[:, 0:D], xcur[u], ALU.add))
                    own.join()
                    norm_stats(u, xcur[u])
                elif name == "e_norm":
                    normalize(u, xn[u], xcur[u], at(i, LN3, 1, NI * LN1)).then_inc(ready[u], 1)
                elif name == "e_ffn":
                    dve.wait_ge(ready[u], at(i, STEP3, 8, NI * STEP1))
                    own.mark(dve.tensor_tensor(xcur[u], xcur[u], r_mix[:, :], ALU.add))
                    own.join()
                    taken3(8)
                    wait(dve, y_stored[u], at(i, 16, -1))
                    dve.tensor_tensor(gate[u], m[:, 0:D], xcur[u], ALU.add).then_inc(y_done[u], 1)
            return step

        with nc.Block() as block:

            @block.sync
            def _(sp):
                def load_rows(u, i):
                    if isinstance(i, int) and i == 0:
                        pass
                    else:
                        sp.wait_ge(kept[u], at(i, 2, 0, -2))
                    b = slot_bn(i, u)
                    sp.dma_start(xcur[u], t["x"][bass.ds(b, 1), :, :].rearrange("a p d -> p (a d)")).then_inc(x_loaded[u], 16)
                    sp.dma_start(c_in[u], t["ctx"][bass.ds(b, 1), :, :].rearrange("a p d -> p (a d)")).then_inc(c_loaded[u], 16)

                load_rows(0, 0)
                sp.dma_start(w_kv[:, :, :], t["w_kv"].rearrange("(c p) n -> p c n", p=P)).then_inc(weights_a, 16)
                sp.dma_start(r_kv[:, D:2 * D], bc_row("r_v", D)).then_inc(weights_a, 16)
                sp.dma_start(col_k[:, :], t["col_k"]).then_inc(weights_a, 16)
                sp.dma_start(r_o[:, :], bc_row("r_o", D)).then_inc(weights_a, 16)
                sp.dma_start(w_q[:, :, :], t["w_q"].rearrange("(c p) n -> p c n", p=P)).then_inc(weights_a, 16)
                sp.dma_start(col_q[:, :], t["col_q"]).then_inc(weights_a, 16)
                for u in range(1, SLOTS):
                    load_rows(u, 0)
                for dst, name in ((w_o, "w_o"), (w_qk2, "w_qk2"), (w_v2, "w_v2"), (w_gate, "w_gate"),
                                  (w_out, "w_out"), (w_route, "w_route")):
                    sp.dma_start(dst[:, :, :], t[name].rearrange("(c p) n -> p c n", p=P)).then_inc(weights0, 16)
                for dst, name, n in ((r_gate, "r_gate", D), (r_scale, "r_scale", D),
                                     (r_route, "r_route", E)):
                    sp.dma_start(dst[:, :], bc_row(name, n)).then_inc(weights0, 16)
                sp.dma_start(r_n1[:, :, :].rearrange("p a d -> p (a d)"), bc_row("r_n1", 2 * D)).then_inc(weights0, 16)
                sp.dma_start(r_n2[:, :, :].rearrange("p a d -> p (a d)"), bc_row("r_n2", 2 * D)).then_inc(weights0, 16)
                sp.dma_start(ids_i[:, :], t["ids"].rearrange("(a n) -> a n", a=1).broadcast_to([P, K_ADAPT])).then_inc(weights2, 16)
                sp.dma_start(wts[:, :], bc_row("wts", K_ADAPT)).then_inc(weights2, 16)
                sp.dma_start(wts_col[:, :], t["wts"].rearrange("(k a) -> k a", a=1)).then_inc(weights2, 16)
                sp.dma_start(rs_row[:, :], bc_row("res_scale", E)).then_inc(weights2, 16)
                sp.dma_start(rope[:, :, :], t["rope"]).then_inc(weights2, 16)
                sp.dma_start(gcol[:, :, :, :], t["ln_gb"]).then_inc(weights2, 16)
                for e in range(E):
                    sp.dma_start(w1[:, :, e * F:(e + 1) * F], t["w1"][e].rearrange("(c p) n -> p c n", p=P)).then_inc(weights2, 16)
                sp.wait_ge(zero_ready, 1)
                for n in range(TILES):
                    sp.dma_start(sorted_x[n * P:(n + 1) * P, :].rearrange("p (a n) -> p a n", a=2), top8[:, :, :].rearrange("p b e -> p (b e)")[:, 0:P].unsqueeze(1).broadcast_to([P, 2, P])).then_inc(zeroed, 16)
                with sp.Fori(1, NI) as i:
                    for u in range(SLOTS):
                        load_rows(u, i)
                for u in range(SLOTS):
                    sp.wait_ge(ready[u], at(NI - 1, STEP1, 16))
                sp.wait_ge(turned, 2 * SLOTS * NI * G)
                sp.dma_start(b1_all, bc_row("b1", E * F)).then_inc(rows2, 16)
                sp.dma_start(b2_all, bc_row("b2", E * D)).then_inc(rows2, 16)
                for u in range(2, SLOTS):
                    sp.wait_ge(full[u], NI * (STEP1 - 2))
                    sp.wait_ge(kept[u], 2 * NI)
                for e in range(E):
                    sp.dma_start(w2[:, :, e * D:(e + 1) * D], t["w2"][e].rearrange("(c p) n -> p c n", p=P)).then_inc(down_loaded, 16)
                for dst, name in ((w_kv, "w_kv3"), (w_q, "w_q3"), (w_o, "w_o3")):
                    sp.dma_start(dst[:, :, :], t[name].rearrange("(c p) n -> p c n", p=P)).then_inc(weights3, 16)
                for dst, name, n in ((r_kv, "r_kv3", 2 * D), (r_q, "r_q3", D), (r_o, "r_o3", D)):
                    sp.dma_start(dst[:, :], bc_row(name, n)).then_inc(weights3, 16)

            @block.gpsimd
            def _(pool):
                own = Chain(pool, pool_own)
                own.mark(pool.memset(ones[:, :], 1.0))
                own.mark(pool.memset(minus_half[:, :], -0.5))
                own.mark(pool.memset(mask_bf[:, :, :], 0.0))
                own.mark(pool.iota(iota_i[:, 0:32], pattern=[[1, 32]], base=0, channel_multiplier=0))
                own.join()
                own.mark(pool.affine_select(out=ident[:, :], in_=ones[:, :], compare_op=ALU.is_equal, fill=0.0,
                                            base=0, pattern=[[-1, P]], channel_multiplier=1))
                own.mark(pool.affine_select(out=ident_bf[:, :], in_=ones[:, :], compare_op=ALU.is_equal, fill=0.0,
                                            base=0, pattern=[[-1, P]], channel_multiplier=1))
                own.mark(pool.affine_select(out=before_me[:, :], in_=ones[:, :], compare_op=ALU.is_gt, fill=0.0,
                                            base=0, pattern=[[1, P]], channel_multiplier=-1))
                own.mark(pool.affine_select(out=mask_bf[:, :, :], in_=mask_bf[:, :, :], compare_op=ALU.is_ge, fill=MASKED,
                                            base=0, pattern=[[0, HG], [-1, P]], channel_multiplier=1))
                own.mark(pool.affine_select(out=headmask[:, :], in_=ones[:, 0:P // HD], compare_op=ALU.is_ge, fill=0.0,
                                            base=0, pattern=[[-HD, P // HD]], channel_multiplier=1))
                own.join()
                own.mark(pool.affine_select(out=headmask[:, :], in_=headmask[:, :], compare_op=ALU.is_ge, fill=0.0,
                                            base=HD - 1, pattern=[[HD, P // HD]], channel_multiplier=-1))
                own.mark(pool.tensor_copy(iota_e[:, :], iota_i[:, 0:E]))
                own.mark(pool.tensor_copy(iota_t[:, :], iota_i[:, 0:TILES]))
                own.mark(pool.tensor_scalar(iota_j[:, :], iota_i[:, 0:B], float(P), None, ALU.mult))
                own.join()
                for u in range(SLOTS):
                    own.mark(pool.memset(vaug[u], 0.0))
                own.join()
                for u in range(SLOTS):
                    pool.memset(vaug[u][:, :, HD:HD + 1], 1.0).then_inc(consts, 1)

                run_turns(pool, "pool", turn1, pool_steps(pool, own), own, 0)

                pool.wait_ge(route_c, 1)
                pool.wait_ge(zeroed, 16 * TILES)
                for u in range(SLOTS):
                    pool.wait_ge(kept[u], 2 * NI)
                for b in range(B):
                    pool.indirect_dma_start(out=sorted_x[:, :], out_offset=bass.IndirectOffsetOnAxis(ap=pos_u[:, b:b + 1], axis=0),
                                            in_=x1_all[:, b, :], in_offset=None).then_inc(scattered, 16)
                pool.wait_ge(scattered, 16 * B)

            @block.tensor
            def _(pe):
                pe.wait_ge(consts, SLOTS)
                run_turns(pe, "pe", turn1, pe_steps(pe))
                pe.wait_ge(route_a, 1)
                pe.matmul(bank[0][:, 0:P], before_me[:, :], onehot[:, :, :].rearrange("p b e -> p (b e)"), start=True, stop=True).then_inc(route_b, 1)
                pe.matmul(bank[1][:, 0:P], ones[:, :], onehot[:, :, :].rearrange("p b e -> p (b e)"), start=True, stop=True).then_inc(route_b, 1)

            @block.scalar
            def _(act):
                run_turns(act, "act", turn1, act_steps(act))
                act.wait_ge(z_ready[0], 2 * NI + 1)
                act.activation(small[:, 1, :], small[:, 0, :], ACT.Exp).then_inc(ez_ready[0], 1)

            @block.vector
            def _(dve):
                dve.memset(top8[:, :, :], 0.0).then_inc(zero_ready, 1)
                dve.wait_ge(consts, SLOTS)
                own = Chain(dve, dve_own)
                run_turns(dve, "dve", turn1, dve_steps(dve, own), own, PER_TURN1)

                dve.wait_ge(zeroed, 16 * TILES)
                own.join()
                own.mark(dve.tensor_scalar(ids_f[:, :], ids_i[:, :], 0.0, None, ALU.add))
                for b in range(B):
                    own.mark(dve.max(top8[:, b, :], logits[:, b, :]))
                own.join()
                for b in range(B):
                    own.mark(dve.max_index(idx8[:, b, :], top8[:, b, :], logits[:, b, :]))
                dve.tensor_tensor(small[:, 0, :], top8[:, :, 1], top8[:, :, 0], ALU.subtract).then_inc(z_ready[0], 1)
                own.join()
                own.mark(dve.tensor_tensor(chosen[:, :], idx8[:, :, 0], idx8[:, :, 1], ALU.max))
                own.join()
                dve.tensor_tensor(onehot[:, :, :], chosen[:, :].unsqueeze(2).broadcast_to([P, B, E]),
                                  iota_e[:, :].unsqueeze(1).broadcast_to([P, B, E]), ALU.is_equal).then_inc(route_a, 1)
                dve.wait_ge(ez_ready[0], 2 * NI + 1)
                own.mark(dve.tensor_scalar(small[:, 2, :], small[:, 1, :], 1.0, None, ALU.add))
                own.join()
                own.mark(dve.reciprocal(small[:, 3, :], small[:, 2, :]))
                own.join()
                own.mark(dve.tensor_tensor(small[:, 1, :], small[:, 1, :], small[:, 3, :], ALU.mult))
                own.join()
                own.mark(dve.tensor_tensor(wsum[:, :], small[:, 1, :], small[:, 3, :], ALU.add))
                dve.wait_ge(route_b, 2)
                own.mark(dve.tensor_copy(tot[:, :, :].rearrange("p b e -> p (b e)"), bank[1][:, 0:P]))
                own.mark(dve.memset(base[:, 0, :], 0.0))
                own.join()
                own.mark(dve.tensor_copy(base[:, 1:B, :], tot[:, 0:B - 1, :]))
                own.join()
                src, dst = base, base2
                step = 1
                while step < B:
                    own.mark(dve.tensor_copy(dst[:, 0:step, :], src[:, 0:step, :]))
                    own.mark(dve.tensor_tensor(dst[:, step:B, :], src[:, step:B, :], src[:, 0:B - step, :], ALU.add))
                    own.join()
                    src, dst, step = dst, src, 2 * step
                assert src is base
                own.mark(dve.tensor_tensor(ecount[:, :], base[:, B - 1, :], tot[:, B - 1, :], ALU.add))
                own.join()
                own.mark(dve.tensor_tensor(ecmp[:, :, :], ecount[:, :].unsqueeze(2).broadcast_to([P, E, B]),
                                           iota_j[:, :].unsqueeze(1).broadcast_to([P, E, B]), ALU.is_gt))
                own.join()
                own.mark(dve.tensor_reduce(etiles[:, :], ecmp[:, :, :], AX.X, ALU.add))
                own.mark(dve.memset(estart[:, 0:1], 0.0))
                own.join()
                for e in range(1, E):
                    own.mark(dve.tensor_tensor(estart[:, e:e + 1], estart[:, e - 1:e], etiles[:, e - 1:e], ALU.add))
                    own.join()
                own.mark(dve.tensor_tensor(eend[:, :], estart[:, :], etiles[:, :], ALU.add))
                own.mark(dve.scalar_tensor_tensor(out=base[:, :, :], in0=estart[:, :].unsqueeze(1).broadcast_to([P, B, E]), scalar=float(P),
                                                  in1=base[:, :, :], op0=ALU.mult, op1=ALU.add))
                own.join()
                own.mark(dve.tensor_tensor(base[:, :, :], base[:, :, :],
                                           bank[0][:, 0:P].rearrange("p (b e) -> p b e", e=E), ALU.add))
                own.mark(dve.tensor_tensor(tcmp[:, :, :], iota_t[:, :].unsqueeze(2).broadcast_to([P, TILES, E]),
                                           eend[:, :].unsqueeze(1).broadcast_to([P, TILES, E]), ALU.is_ge))
                own.join()
                own.mark(dve.tensor_tensor(base[:, :, :], base[:, :, :], onehot[:, :, :], ALU.mult))
                own.mark(dve.tensor_reduce(texp[:, :], tcmp[:, :, :], AX.X, ALU.add))
                own.join()
                own.mark(dve.tensor_reduce(pos[:, :], base[:, :, :], AX.X, ALU.add))
                own.mark(dve.tensor_scalar(texp_i[:, :], texp[:, :], float(E - 1), None, ALU.min))
                own.join()
                dve.tensor_copy(pos_u[:, :], pos[:, :]).then_inc(route_c, 1)
                dve.wait_ge(weights2, 16)
                own.mark(dve.tensor_scalar(ids_n[:, :], ids_f[:, :], 0.0, float(ADAPTERS), ALU.is_lt, ALU.mult))
                own.join()
                own.mark(dve.tensor_tensor(ids_f[:, :], ids_f[:, :], ids_n[:, :], ALU.add))
                own.join()
                dve.tensor_scalar(ids_i[:, :], ids_f[:, :], 0.0, float(ADAPTERS - 1), ALU.max, ALU.min).then_inc(route_c, 1)


        TURNS2, REST2 = TILES // XSLOTS, TILES % XSLOTS

        def run_tiles(eng, turn, own=None, per=0):
            turn(0, XSLOTS, XSLOTS)
            with eng.Fori(1, TURNS2 - 1) as i:
                if own:
                    own.start(i - 1, per)
                turn(i, XSLOTS, XSLOTS)
                if own:
                    own.end(TURNS2 - 2)
            turn(TURNS2 - 1, XSLOTS, REST2)
            turn(TURNS2, REST2, 0)

        with nc.Block() as block:
            @block.sync
            def _(sp):
                def turn(i, n, _):
                    for s in range(n):
                        wait(sp, tile_turned[s], i)
                        wait(sp, tile_kept[s], i)
                        sp.dma_start(xe[s], sorted_x[bass.ds((i * XSLOTS + s) * P, P), :]).then_inc(tile_in[s], 16)

                def load_adapter(k):
                    a = sp.value_load(ids_i[0:1, k:k + 1], min_val=0, max_val=ADAPTERS - 1)
                    sp.dma_start(w_adapt[k % HALF].rearrange("p (c n) -> p c n", c=C),
                                 t["w_adapt"][bass.ds(a, 1), :, :].rearrange("o (c p) n -> p (o c) n", p=P)).then_inc(adapters, 16)
                    sp.dma_start(b_adapt[k:k + 1, :], t["b_adapt"][bass.ds(a, 1), :]).then_inc(adapter_rows, 16)
                turn(0, XSLOTS, XSLOTS)
                for k in range(HALF):
                    load_adapter(k)
                with sp.Fori(1, TURNS2 - 1) as i:
                    turn(i, XSLOTS, XSLOTS)
                sp.wait_ge(half_mixed, 1)
                for k in range(HALF, K_ADAPT):
                    load_adapter(k)
                turn(TURNS2 - 1, XSLOTS, REST2)
                turn(TURNS2, REST2, 0)

            @block.gpsimd
            def _(pool):
                def turn(i, n, _):
                    for s in range(n):
                        e = pool.value_load(texp_i[0:1, bass.ds(i * XSLOTS + s, 1)], min_val=0, max_val=E - 1)
                        own.mark(pool.tensor_copy(ers[s][:, :], rs_row[:, bass.ds(e, 1)]))
                        pool.tensor_copy(ecol[s][:, :, :], gcol[:, :, bass.ds(e, 1), :].rearrange("p a o c -> p a (o c)")).then_inc(tile_cols[s], 1)
                    for s in range(n):
                        pool.wait_ge(tile_var[s], at(i, 2, 1))
                        own.mark(pool.tensor_tensor(rstd[s][:, :], veps[s][:, :], minus_half[:, :], ALU.pow))
                        own.join()
                        pool.tensor_tensor(nmr[s][:, :], minus_mean[s][:, :], rstd[s][:, :], ALU.mult).then_inc(tile_rstd[s], 1)
                    for s in range(n):
                        pool.wait_ge(tile_out[s], i + 1)
                        pool.dma_start(sorted_y[bass.ds((i * XSLOTS + s) * P, P), :], ye[s]).then_inc(tile_stored[s], 16)
                own = Chain(pool, pool_own2)
                pool.wait_ge(weights2, 16 * (6 + E))
                run_tiles(pool, turn, own, XSLOTS * 2)
                for s in range(XSLOTS):
                    pool.wait_ge(tile_stored[s], 16 * (TURNS2 + (s < REST2)))
            @block.tensor
            def _(pe):
                pe.wait_ge(weights2, 16 * (6 + E))

                def rows(i, s):
                    pe.wait_ge(tile_in[s], at(i, 16, 15))
                    for c in range(C):
                        last = pe.transpose(bank[XSLOTS + s][:, c * P:(c + 1) * P], xe[s][:, c * P:(c + 1) * P], ident[:, :])
                    last.then_inc(tile_turned[s], 1)

                def hidden(i, s):
                    e = pe.value_load(texp_i[0:1, bass.ds(i * XSLOTS + s, 1)], min_val=0, max_val=E - 1)
                    pe.wait_ge(tile_xT[s], i + 1)
                    wait(pe, tile_out[s], i)
                    for c in range(C):
                        last = pe.matmul(bank[s], xeT[s][:, c * P:(c + 1) * P], w1[:, c, bass.ds(e * F, F)],
                                         start=(c == 0), stop=(c == C - 1))
                    last.then_inc(tile_full[s], 1)

                def hidden_T(i, s):
                    pe.wait_ge(tile_ready[s], at(i, 2, 0))
                    for c in range(FC):
                        last = pe.transpose(bank[s][:, c * P:(c + 1) * P], hid[s][:, c * P:(c + 1) * P], ident[:, :])
                    last.then_inc(tile_full[s], 1)

                def output(i, s):
                    if isinstance(i, int) and i == 0 and s == 0:
                        pe.wait_ge(down_loaded, 16 * E)
                    e = pe.value_load(texp_i[0:1, bass.ds(i * XSLOTS + s, 1)], min_val=0, max_val=E - 1)
                    pe.wait_ge(tile_ready[s], at(i, 2, 1))
                    for c in range(FC):
                        last = pe.matmul(bank[s][:, 0:D], hT[s][:, c * P:(c + 1) * P], w2[:, c, bass.ds(e * D, D)],
                                         start=(c == 0), stop=(c == FC - 1))
                    last.then_inc(tile_full[s], 1)

                def turn(i, n, following):
                    for step, s in ((hidden, 0), (hidden, 1), (hidden, 2), (rows, 0), (hidden, 3), (hidden_T, 0),
                                    (rows, 1), (hidden_T, 1), (rows, 2), (output, 0), (hidden_T, 2), (rows, 3),
                                    (output, 1), (hidden_T, 3), (output, 2), (output, 3)):
                        if step is rows:
                            if s < following:
                                rows(i + 1, s)
                        elif s < n:
                            step(i, s)
                for s in range(XSLOTS):
                    rows(0, s)
                run_tiles(pe, turn)
                pe.wait_ge(half_mixed, 1)
                pe.wait_ge(adapter_rows, 16 * K_ADAPT)
                pe.matmul(bank[7][:, 0:D], wts_k[:, :], b_adapt[:, :], start=True, stop=True).then_inc(row_mixed, 1)

            @block.scalar
            def _(act):
                def rows(i, s):
                    act.wait_ge(tile_turned[s], i + 1)
                    act.copy(xeT[s], bank[XSLOTS + s][:, 0:D]).then_inc(tile_xT[s], 1)

                def norm(i, s):
                    act.wait_ge(tile_rstd[s], i + 1)
                    act.activation(hid[s], hid[s], ACT.Identity, bias=nmr[s][:, 0:1], scale=rstd[s][:, 0:1]).then_inc(tile_ready[s], 1)

                def gelu(i, s):
                    act.wait_ge(tile_full[s], at(i, 3, 1))
                    act.wait_ge(tile_cols[s], i + 1)
                    for c in range(FC):
                        last = act.activation(hT[s][:, c * P:(c + 1) * P], bank[s][:, c * P:(c + 1) * P], ACT.Gelu,
                                              bias=ecol[s][:, 1, c:c + 1], scale=ecol[s][:, 0, c:c + 1])
                    last.then_inc(tile_ready[s], 1)

                def keep(i, s):
                    act.wait_ge(tile_in[s], at(i, 16, 15))
                    wait(act, tile_out[s], i)
                    act.copy(x_res[s][:, :], xe[s]).then_inc(tile_kept[s], 1)

                def turn(i, n, following):
                    for step, s in ((keep, 0), (keep, 1), (keep, 2), (keep, 3), (norm, 0), (norm, 1), (gelu, 0), (rows, 0),
                                    (norm, 2), (gelu, 1), (rows, 1), (rows, 2), (norm, 3), (gelu, 2), (rows, 3), (gelu, 3)):
                        if step is rows:
                            if s < following:
                                rows(i + 1, s)
                        elif s < n:
                            step(i, s)
                for s in range(XSLOTS):
                    rows(0, s)
                run_tiles(act, turn)

            @block.vector
            def _(dve):
                dve.wait_ge(weights2, 16 * (6 + E))
                dve.wait_ge(rows2, 32)
                own = Chain(dve, dve_own2)

                def hidden(i, s):
                    e = dve.value_load(texp_i[0:1, bass.ds(i * XSLOTS + s, 1)], min_val=0, max_val=E - 1)
                    dve.wait_ge(tile_full[s], at(i, 3, 0))
                    own.mark(dve.tensor_tensor(hid[s], bank[s], b1_all[:, bass.ds(e * F, F)], ALU.add))
                    own.join()
                    own.mark(dve.bn_stats(stats[s][:, :], hid[s]))
                    own.join_by(spare[s][:, :])
                    own.mark(dve.bn_aggr(mv[s][:, :], stats[s][:, :]))
                    own.join()
                    dve.tensor_scalar(veps[s][:, :], mv[s][:, 1:2], EPS, None, ALU.add).then_inc(tile_var[s], 1)
                    dve.tensor_scalar(minus_mean[s][:, :], mv[s][:, 0:1], -1.0, None, ALU.mult).then_inc(tile_var[s], 1)

                def output(i, s):
                    e = dve.value_load(texp_i[0:1, bass.ds(i * XSLOTS + s, 1)], min_val=0, max_val=E - 1)
                    dve.wait_ge(tile_full[s], at(i, 3, 2))
                    wait(dve, tile_stored[s], at(i, 16, -1))
                    own.mark(dve.tensor_tensor(ye[s], bank[s][:, 0:D], b2_all[:, bass.ds(e * D, D)], ALU.add))
                    own.join()
                    dve.wait_ge(tile_kept[s], i + 1)
                    dve.wait_ge(tile_cols[s], i + 1)
                    dve.scalar_tensor_tensor(out=ye[s], in0=ye[s], scalar=ers[s][:, 0:1], in1=x_res[s][:, :],
                                             op0=ALU.mult, op1=ALU.add).then_inc(tile_out[s], 1)

                def turn(i, n, _):
                    for step in (hidden, output):
                        for s in range(n):
                            step(i, s)

                def mix_half(first):
                    dve.wait_ge(adapters, 16 * (HALF if first else K_ADAPT))
                    mix = w_mix[:, :, :].rearrange("p c n -> p (c n)")
                    for n in range(HALF):
                        k = n + (0 if first else HALF)
                        if k == 0:
                            ins = dve.tensor_scalar(mix, w_adapt[n], wts[:, k:k + 1], None, ALU.mult)
                        else:
                            own.join()
                            ins = dve.scalar_tensor_tensor(out=mix, in0=w_adapt[n], scalar=wts[:, k:k + 1], in1=mix,
                                                           op0=ALU.mult, op1=ALU.add)
                        own.mark(ins)
                    own.join()
                    if first:
                        own.mark(dve.tensor_scalar(wts_k[:, :], ones[0:K_ADAPT, :], wts_col[:, 0:1], None, ALU.mult))
                        own.join()
                        dve.memset(spare[0][:, :], 0.0).then_inc(half_mixed, 1)
                turn(0, XSLOTS, XSLOTS)
                mix_half(True)
                with dve.Fori(1, TURNS2 - 1) as i:
                    own.start(i - 1, XSLOTS * 5)
                    turn(i, XSLOTS, XSLOTS)
                    own.end(TURNS2 - 2)
                turn(TURNS2 - 1, XSLOTS, REST2)
                mix_half(False)
                turn(TURNS2, REST2, 0)
                dve.wait_ge(row_mixed, 1)
                own.mark(dve.tensor_copy(r_mix[:, :], bank[7][:, 0:D]))
                own.join()
                dve.memset(spare[0][:, :], 0.0).then_inc(mix_ready, 1)

        with nc.Block() as block:
            @block.sync
            def _(sp):
                def load_context(u, i):
                    if not (isinstance(i, int) and i == 0):
                        sp.wait_ge(ready[u], at(i, STEP3, 1, NI * STEP1 - STEP3))
                    sp.dma_start(c_in[u], t["ctx"][bass.ds(slot_bn(i, u), 1), :, :].rearrange("a p d -> p (a d)")).then_inc(c_loaded[u], 16)

                for u in range(SLOTS):
                    load_context(u, 0)
                with sp.Fori(1, NI) as i:
                    for u in range(SLOTS):
                        load_context(u, i)
                for u in range(SLOTS):
                    sp.wait_ge(y_stored[u], 16 * NI)

            @block.gpsimd
            def _(pool):
                own = Chain(pool, pool_own3)
                for u in range(SLOTS):
                    own.mark(pool.memset(vaug[u], 0.0))
                own.join()
                for u in range(SLOTS):
                    pool.memset(vaug[u][:, :, HD:HD + 1], 1.0).then_inc(consts, 1)
                run_turns(pool, "pool", turn3, pool_steps(pool, own), own, 4 * SLOTS)

            @block.tensor
            def _(pe):
                pe.wait_ge(weights3, 16 * 6)
                pe.wait_ge(mix_ready, 1)
                run_turns(pe, "pe", turn3, pe_steps(pe))

            @block.scalar
            def _(act):
                run_turns(act, "act", turn3, act_steps(act))

            @block.vector
            def _(dve):
                dve.wait_ge(weights3, 16 * 6)
                own = Chain(dve, dve_own3)
                run_turns(dve, "dve", turn3, dve_steps(dve, own), own, PER_TURN3)


def kernel(**inputs):
    import concourse.bacc as bacc
    from concourse.bass_utils import run_bass_kernel_spmd

    x = {k: np.asarray(v) for k, v in inputs.items()}
    half = HD // 2
    freq = (np.float32(1.0) / np.float32(10000.0) ** (np.arange(half, dtype=np.float32) / np.float32(half))).astype(np.float32)
    angle = np.arange(P, dtype=np.float32)[:, None] * freq[None, :]
    cos, sin = np.cos(angle), np.sin(angle)
    rope = np.stack([np.tile(np.concatenate([cos, cos], 1), (1, H)), np.tile(np.concatenate([-sin, sin], 1), (1, H))], 1)
    cat = np.concatenate
    arrays = {
        "x": x["x"], "ctx": x["ctx_1024"],
        "w_kv": cat([x["L0_xattn_Wk"].T, x["L0_xattn_Wv"].T], 1), "r_v": x["L0_xattn_bv"], "col_k": x["L0_xattn_bk"].reshape(C, P).T,
        "w_q": x["L0_xattn_Wq"].T, "col_q": x["L0_xattn_bq"].reshape(C, P).T, "w_o": x["L0_xattn_Wo"].T, "r_o": x["L0_xattn_bo"],
        "w_qk2": cat([x["L0_ffn_q_w"], x["L0_ffn_k_w"]], 1), "w_v2": x["L0_ffn_v_w"], "w_gate": x["L0_ffn_gate_w"],
        "w_out": x["L0_ffn_out_w"], "w_route": x["L0_ffn_moe_gate_w"], "r_gate": x["L0_ffn_gate_b"],
        "r_scale": x["L0_ffn_scale_w"].reshape(-1), "r_route": x["L0_ffn_moe_gate_b"],
        "r_n1": cat([x["L0_ffn_n1_g"], x["L0_ffn_n1_b"]]), "r_n2": cat([x["L0_ffn_n2_g"], x["L0_ffn_n2_b"]]),
        "w1": x["L0_ffn_w1"], "w2": x["L0_ffn_w2"], "b1": x["L0_ffn_b1"].reshape(-1), "b2": x["L0_ffn_b2"].reshape(-1),
        "ln_gb": np.stack([x["L0_ffn_ln_g"], x["L0_ffn_ln_b"]]).reshape(2, E, FC, P).transpose(3, 0, 1, 2), "res_scale": x["L0_ffn_res_scale"],
        "w_kv3": cat([x["L1_xattn_Wk"].T, x["L1_xattn_Wv"].T], 1), "r_kv3": cat([x["L1_xattn_bk"], x["L1_xattn_bv"]]),
        "w_q3": x["L1_xattn_Wq"].T, "r_q3": x["L1_xattn_bq"], "w_o3": x["L1_xattn_Wo"].T, "r_o3": x["L1_xattn_bo"],
        "w_adapt": x["L1_ffn_W"].transpose(0, 2, 1), "b_adapt": x["L1_ffn_b"], "ids": x["L1_ffn_ids"],
        "wts": x["L1_ffn_weights"], "rope": rope.astype(np.float32),
    }
    arrays = {f"in_{k}": np.ascontiguousarray(v) for k, v in arrays.items()}
    nc = bacc.Bacc("TRN2", target_bir_lowering=False, num_devices=1)
    t = {k[3:]: nc.dram_tensor(k, v.shape, mybir.dt.from_np(v.dtype), kind="ExternalInput").ap() for k, v in arrays.items()}
    t["out"] = nc.dram_tensor("out", (B, P, D), F32, kind="ExternalOutput").ap()
    build(nc, t)
    r = run_bass_kernel_spmd(nc, [arrays], core_ids=[0])
    return r.results[0]["out"]
```
